# Optimizing a Trainium2 kernel written in Bass

```python
import numpy as np
import jax
import jax.numpy as jnp

def _softmax(x, axis=-1):
    return jax.nn.softmax(x, axis=axis)

def _gelu(x):
    return jax.nn.gelu(x, approximate=True)

def _silu(x):
    return jax.nn.silu(x)

def _sigmoid(x):
    return jax.nn.sigmoid(x)

def _layernorm(x, axis=-1, eps=1e-05):
    m = jnp.mean(x, axis=axis, keepdims=True)
    v = jnp.var(x, axis=axis, keepdims=True)
    return (x - m) / jnp.sqrt(v + eps)

def _scatter_add(tgt, idx, src, axis=0):
    return tgt.at[idx].add(src)

def _segment_sum(src, seg, n):
    return jax.ops.segment_sum(src, seg, n)
kernel_name = 'mk_adj_ffn_d1_adj_r2_171550'

def setup_inputs(seed: int=0):
    np.random.seed(seed)
    _w = jnp.asarray

    def _rec_inputs():
        import jax
        import jax.numpy as jnp
        _gk = jax.random.key(seed)
        x = -0.0002928 + 1 * jax.random.normal(jax.random.fold_in(_gk, 1), (2048, 256), jnp.float32)
        _w = (1.0 + jnp.arange(2048, dtype=jnp.float32)) ** (-0.5)
        _w = _w / _w.mean()
        _pij = jnp.clip(0.0078125 * _w[:, None] * _w[None, :], 0.0, 1.0)
        _a = jax.random.uniform(jax.random.fold_in(_gk, 2), (2048, 2048)) < _pij
        _a = jnp.logical_or(_a, jnp.eye(2048, dtype=bool))
        _af = _a.astype(jnp.float32)
        _af = _af * jax.random.uniform(jax.random.fold_in(_gk, 3), (2048, 2048), jnp.float32, 0.05, 1)
        adj = _af
        return (x, adj)
    x, adj = _rec_inputs()

    def _L0_gnn_setup():
        import jax, jax.numpy as jnp
        import numpy as np
        EPS = 1e-08
        key = jax.random.key(seed)
        k1, k2, k3, k4 = jax.random.split(key, 4)
        N, IN, OUT = (4096, 256, 256)
        x = jax.random.normal(k1, (N, IN), dtype=jnp.float32)
        adj = jax.random.uniform(k2, (N, N), dtype=jnp.float32)
        W = jax.random.normal(k3, (OUT, IN), dtype=jnp.float32) * (1.0 / np.sqrt(IN))
        b = jax.random.normal(k4, (OUT,), dtype=jnp.float32) * 0.01
        return {'x': x, 'adj': adj, 'W': W, 'b': b}
    _L0_gnn_all = _L0_gnn_setup()
    _L0_gnn_in = {k: v for k, v in _L0_gnn_all.items() if k in ('W', 'b')}
    del _L0_gnn_all

    def _L0_ffn_setup():
        import jax, jax.numpy as jnp
        import numpy as np
        D_MODEL = 256
        DFF = 1024
        TOP_K = 2
        EXPERTS_PER_LEVEL = (4, 8)

        def _moe_level(x, Wr, W1, b1, W2, b2, k):
            probs = jax.nn.softmax(jnp.einsum('bsd,de->bse', x, Wr), axis=-1)
            _, top_idx = jax.lax.top_k(probs, k)
            dispatch = jax.nn.one_hot(top_idx, probs.shape[-1], dtype=x.dtype).sum(axis=-2)
            xm = x[:, :, None, :] * dispatch[..., None]
            h = jax.nn.relu(jnp.einsum('bsed,edf->bsef', xm, W1) + b1)
            y = jnp.einsum('bsef,efd->bsed', h, W2) + b2
            return jnp.sum(y * probs[..., None], axis=2)
        key = jax.random.key(seed)
        ks = jax.random.split(key, 12)

        def w(k, fan_in, shape):
            return jax.random.normal(k, shape, jnp.float32) * (1.0 / np.sqrt(fan_in))

        def b(k, shape):
            return jax.random.normal(k, shape, jnp.float32) * 0.01
        E0, E1 = EXPERTS_PER_LEVEL
        return {'x': jax.random.normal(ks[0], (4, 1024, D_MODEL), jnp.float32), 'Wr0': w(ks[1], D_MODEL, (D_MODEL, E0)), 'W1_0': w(ks[2], D_MODEL, (E0, D_MODEL, DFF)), 'b1_0': b(ks[3], (E0, DFF)), 'W2_0': w(ks[4], DFF, (E0, DFF, D_MODEL)), 'b2_0': b(ks[5], (E0, D_MODEL)), 'Wr1': w(ks[6], D_MODEL, (D_MODEL, E1)), 'W1_1': w(ks[7], D_MODEL, (E1, D_MODEL, DFF)), 'b1_1': b(ks[8], (E1, DFF)), 'W2_1': w(ks[9], DFF, (E1, DFF, D_MODEL)), 'b2_1': b(ks[10], (E1, D_MODEL))}
    _L0_ffn_all = _L0_ffn_setup()
    _L0_ffn_in = {k: v for k, v in _L0_ffn_all.items() if k in ('Wr0', 'W1_0', 'b1_0', 'W2_0', 'b2_0', 'Wr1', 'W1_1', 'b1_1', 'W2_1', 'b2_1')}
    del _L0_ffn_all
    return {'x': x, 'adj': adj, 'L0_gnn_W': _L0_gnn_in['W'], 'L0_gnn_b': _L0_gnn_in['b'], 'L0_ffn_Wr0': _L0_ffn_in['Wr0'], 'L0_ffn_W1_0': _L0_ffn_in['W1_0'], 'L0_ffn_b1_0': _L0_ffn_in['b1_0'], 'L0_ffn_W2_0': _L0_ffn_in['W2_0'], 'L0_ffn_b2_0': _L0_ffn_in['b2_0'], 'L0_ffn_Wr1': _L0_ffn_in['Wr1'], 'L0_ffn_W1_1': _L0_ffn_in['W1_1'], 'L0_ffn_b1_1': _L0_ffn_in['b1_1'], 'L0_ffn_W2_1': _L0_ffn_in['W2_1'], 'L0_ffn_b2_1': _L0_ffn_in['b2_1']}

def reference(x, adj, L0_gnn_W, L0_gnn_b, L0_ffn_Wr0, L0_ffn_W1_0, L0_ffn_b1_0, L0_ffn_W2_0, L0_ffn_b2_0, L0_ffn_Wr1, L0_ffn_W1_1, L0_ffn_b1_1, L0_ffn_W2_1, L0_ffn_b2_1):
    import jax
    import jax.numpy as jnp

    def _L0_gnn_ref(x, adj, W, b):
        import jax, jax.numpy as jnp
        import numpy as np
        EPS = 1e-08
        deg = adj.sum(axis=1)
        dis = (deg + EPS) ** (-0.5)
        a_norm = dis[:, None] * adj * dis[None, :]
        h = a_norm @ x
        return h @ W.T + b

    def _L0_ffn_ref(x, Wr0, W1_0, b1_0, W2_0, b2_0, Wr1, W1_1, b1_1, W2_1, b2_1):
        import jax, jax.numpy as jnp
        import numpy as np
        D_MODEL = 256
        DFF = 1024
        TOP_K = 2
        EXPERTS_PER_LEVEL = (4, 8)

        def _moe_level(x, Wr, W1, b1, W2, b2, k):
            probs = jax.nn.softmax(jnp.einsum('bsd,de->bse', x, Wr), axis=-1)
            _, top_idx = jax.lax.top_k(probs, k)
            dispatch = jax.nn.one_hot(top_idx, probs.shape[-1], dtype=x.dtype).sum(axis=-2)
            xm = x[:, :, None, :] * dispatch[..., None]
            h = jax.nn.relu(jnp.einsum('bsed,edf->bsef', xm, W1) + b1)
            y = jnp.einsum('bsef,efd->bsed', h, W2) + b2
            return jnp.sum(y * probs[..., None], axis=2)
        h0 = _moe_level(x, Wr0, W1_0, b1_0, W2_0, b2_0, TOP_K)
        out = _moe_level(h0, Wr1, W1_1, b1_1, W2_1, b2_1, TOP_K)
        return out
    x = x + _L0_gnn_ref(_layernorm(x, axis=-1), adj, L0_gnn_W, L0_gnn_b)
    x = x + _L0_ffn_ref(_layernorm(x, axis=-1)[None], L0_ffn_Wr0, L0_ffn_W1_0, L0_ffn_b1_0, L0_ffn_W2_0, L0_ffn_b2_0, L0_ffn_Wr1, L0_ffn_W1_1, L0_ffn_b1_1, L0_ffn_W2_1, L0_ffn_b2_1)[0]
    return x

_drawn_inputs = setup_inputs


def setup_inputs(seed=0):
    import zlib

    import numpy as np

    out = dict(_drawn_inputs(seed))
    spreads = {}
    factors = {'L0_gnn_b': 5.436,
     'L0_ffn_b1_0': 26.192,
     'L0_ffn_b2_0': 6.938,
     'L0_ffn_b1_1': 24.6,
     'L0_ffn_b2_1': 8.0}
    for name, (base, spread) in spreads.items():
        noise = np.random.default_rng([zlib.crc32(name.encode()), seed]).standard_normal(out[name].shape)
        drawn = base * np.exp(spread * noise) if base else spread * noise
        out[name] = jnp.asarray(drawn.astype(out[name].dtype))
    for name, factor in factors.items():
        out[name] = (out[name] * factor).astype(out[name].dtype)
    return out
```

```python
from contextlib import ExitStack

import concourse.bass as bass
from concourse import mybir

F32, F16, I32 = mybir.dt.float32, mybir.dt.float16, mybir.dt.int32
ALU = mybir.AluOpType
ACT = mybir.ActivationFunctionType
AX = mybir.AxisListType
RED = bass.bass_isa.ReduceOp

P = 128
EXPONENT = 0x7F800000


def bass_gnn_moe(nc, x, adj, gnn_W, gnn_b, Wr0, W1_0, b1_0, W2_0, b2_0, Wr1, W1_1, b1_1, W2_1, b2_1, out):
    T, D = x.shape
    NB = T // P
    GB = 4
    NG = NB // GB
    KD = D // P
    F = W1_0.shape[2]
    FC = F // P
    EXPERTS = (W1_0.shape[0], W1_1.shape[0])
    EM = max(EXPERTS)
    ARENA = T + P
    TILES = [2 * NB + e for e in EXPERTS]
    JUNK = [e * ARENA for e in EXPERTS]
    RW = 2 * D + 2
    IDC = 2 * D
    PADROW = 2 * T
    YROWS = 2 * T + (EM + 2) * P
    CW = 32
    WSLOT = 2 * (KD * F + FC * D)
    UNIT = KD * F
    NSLOT = 9
    ATB = 2 * NB * P
    FIRSTSLOT = (NSLOT - EXPERTS[0], 0)
    EARLY = EM - 3
    EPS_LN, EPS_DEG = 1e-5, 1e-8
    Wr, W1, b1, W2, b2 = (Wr0, Wr1), (W1_0, W1_1), (b1_0, b1_1), (W2_0, W2_1), (b2_0, b2_1)
    W1v = [w.rearrange("e (k p) f -> e p k f", p=P) for w in W1]
    W2v = [w.rearrange("e (c p) d -> e p c d", p=P) for w in W2]

    ctx = ExitStack()
    with ctx:
        def sb(name, shape, dt=F32):
            return ctx.enter_context(nc.sbuf_tensor(name, shape, dt))

        def ps(name, shape, dt=F32):
            return ctx.enter_context(nc.psum_tensor(name, shape, dt))

        def sem(name):
            return ctx.enter_context(nc.semaphore(name))

        def dram(name, shape, dt):
            return nc.dram_tensor(name, shape, dt).ap()

        arena = [dram(f"arena{l}", (EXPERTS[l] * ARENA + 2 * P, RW), F16) for l in range(2)]
        NCONST = 16
        ys = [dram(f"ys{l}", (YROWS, D), F32) for l in range(2)]
        x1_dram = dram("x1_dram", (T, D), F32)

        R = sb("R", [P, NSLOT * WSLOT], F16)
        stage = sb("stage", [P, 2, UNIT])
        U = sb("U", [P, NB * 2 * D], F16)
        v = U[:, :].rearrange("p (j h d) -> p j h d", j=NB, h=2)
        hid = U[:, 0:2 * F].bitcast(F32).rearrange("p (c t) -> p c t", c=FC)
        hid_hi = U[:, 2 * F:4 * F].rearrange("p (s c t) -> p s c t", s=2, c=FC)
        hid_lo = U[:, 4 * F:6 * F].rearrange("p (s c t) -> p s c t", s=2, c=FC)
        yab = U[:, 0:GB * 4 * D].bitcast(F32).rearrange("p (b r d) -> p b r d", b=GB, r=2)
        u_all = R[:, (NSLOT - 1) * WSLOT:NSLOT * WSLOT].bitcast(F32).rearrange("p (j d) -> p j d", j=NB)
        rows = sb("rows", [P, GB, 2, RW], F16)
        xr = sb("xr", [P, GB, D])
        wg_nat = xr[:, 0:KD, :]
        wgT = xr[:, KD:2 * KD, :]
        xT = sb("xT", [P, 2, 2 * KD, P], F16)
        xrT = xT[:, :, :, :].rearrange("p s a t -> p (s a t)").bitcast(F32).rearrange("p (k t) -> p k t", k=KD * 2)
        xin = sb("xin", [P, 2, D])
        xtile = sb("xtile", [P, 2, RW], F16)
        xn = sb("xn", [P, 2, D])
        xb = sb("xb", [P, 2, D])
        bB = sb("bB", [P, D])
        zeros = sb("zeros", [P, 2 * D], F16)
        ident = sb("ident", [P, P])
        ident16 = sb("ident16", [P, P], F16)
        before = sb("before", [P, P], F16)
        ones16 = sb("ones16", [P, P], F16)
        onesrow = sb("onesrow", [1, P])
        brow = sb("brow", [1, D])
        diff = xb[:, 0, 0:P]
        tileno = sb("tileno", [1, max(TILES)])
        junkrow = sb("junkrow", [1, 2, max(TILES)])
        ids = sb("ids", [P, NB, 2], I32)
        padids = sb("padids", [P, EM + 2], I32)
        base_e = sb("base_e", [P, EM])
        rank_e = sb("rank_e", [P, EM])
        half = sb("half", [P, 4])
        wr = [sb(f"wr{l}", [P, KD, EXPERTS[l]]) for l in range(2)]
        b1n = [sb(f"b1n{l}", [EXPERTS[l] * FC, P]) for l in range(2)]
        b1T = [sb(f"b1T{l}", [P, EXPERTS[l], FC]) for l in range(2)]
        prm = [sb(f"prm{l}", [P, EXPERTS[l], FC + 2]) for l in range(2)]
        wstat = sb("wstat", [P, 2])
        wnorm = sb("wnorm", [P, 2])
        wtot = sb("wtot", [P, 2])
        wpow = sb("wpow", [P, 2, 12])
        winv = sb("winv", [P, 2, 12])
        wscl = sb("wscl", [P, 2, 12])
        lv = [sb(f"lv{l}", [P, 16]) for l in range(2)]
        lve = [sb(f"lve{l}", [P, 4, EXPERTS[l]]) for l in range(2)]
        CB = sb("CB", [P, D])
        coef = sb("coef", [P, NB, CW])
        cgrp = sb("cgrp", [P, GB, CW])
        cT = sb("cT", [P, P])
        p12 = sb("p12", [P, NB, 2])
        stat = sb("stat", [P, 2, 6])
        mv = sb("mv", [P, 2, 2])
        rstd = sb("rstd", [P, 2])
        deg = sb("deg", [P, NB])
        dis = sb("dis", [P, NB])
        pdeg = sb("pdeg", [P, NB])
        rdeg = sb("rdeg", [P, 2])
        vscale = sb("vscale", [P, NB])
        gscale = sb("gscale", [P, NB])
        gst = sb("gst", [P, 12])
        degE = sb("degE", [P, NB])
        vare = sb("vare", [P, 2])
        rt = sb("rt", [P, 12, GB, EM])
        rs = sb("rs", [P, 8, GB])
        disp = sb("disp", [P, GB, EM], F16)
        tot = sb("tot", [P, EM], F16)
        cpick = sb("cpick", [P, EM])
        slot = sb("slot", [P, GB, 2], I32)
        cnt = sb("cnt", [1, 8, EM])
        cnti = sb("cnti", [1, 2, EM], I32)
        steps = U[0:1, 0:4 * EM * max(TILES)].bitcast(F32).rearrange("p (i e t) -> p i e t", i=2, e=EM)
        tabf = sb("tabf", [1, 2, max(TILES)])
        tab = sb("tab", [1, 3, max(TILES)], I32)
        tprm = sb("tprm", [P, 2, FC + 2])
        tgam = sb("tgam", [P, max(TILES)])
        tids = sb("tids", [P, max(TILES)], I32)
        yid = sb("yid", [P, 2], I32)
        ymax = sb("ymax", [P, 2])
        yrun = sb("yrun", [P, 2])

        Z = ps("Z", [P, 2, FC, P])
        Zq = Z[:, :, :, :].rearrange("p s (q c) t -> p (s q) (c t)", q=2)
        p_log = Zq[:, 0, 0:GB * EM].rearrange("p (b e) -> p b e", b=GB)
        p_pos = Zq[:, 1, 0:GB * EM].rearrange("p (b e) -> p b e", b=GB)
        p_cnt = Zq[:, 2, 0:EM]
        p_cT = Zq[:, 3, 0:P]
        Y2 = ps("Y", [P, 2, 4 * P])
        Y = Y2[:, :, 0:D]
        PT = ps("PT", [P, 2 * KD, 2, P], F16)
        PM = PT[:, :, :, :].rearrange("p a b t -> p (a b t)").bitcast(F32)
        PX = ps("PX", [P, 2 * KD, P])

        consts_made = sem("consts_made")
        masks_made = sem("masks_made")
        gnnw_loaded = sem("gnnw_loaded")
        gnnw_squared = sem("gnnw_squared")
        gnnw_transposed = sem("gnnw_transposed")
        gnnw_copied = sem("gnnw_copied")
        bias_spread = sem("bias_spread")
        bias_copied = sem("bias_copied")
        small_loaded = sem("small_loaded")
        b1_transposed = sem("b1_transposed")
        b1_copied = sem("b1_copied")
        var_made = sem("var_made")
        rstd_made = sem("rstd_made")
        xn_made = sem("xn_made")
        xn_transposed = sem("xn_transposed")
        xn_copied = sem("xn_copied")
        u_summed = sem("u_summed")
        u_copied = sem("u_copied")
        deg_made = sem("deg_made")
        deg_rounded = sem("deg_rounded")
        dis_made = sem("dis_made")
        adj_scaled = sem("adj_scaled")
        adj_transposed = sem("adj_transposed")
        adj_hi = sem("adj_hi")
        adj_lo = sem("adj_lo")
        v_bounds = sem("v_bounds")
        v_bounds_max = sem("v_bounds_max")
        v_bound_root = sem("v_bound_root")
        v_scales = sem("v_scales")
        v_hi = sem("v_hi")
        v_lo = sem("v_lo")
        graph_summed = sem("graph_summed")
        bias_added = sem("bias_added")
        x1_made = sem("x1_made")
        xr_made = sem("xr_made")
        xr_transposed = sem("xr_transposed")
        xr_copied = sem("xr_copied")
        logits_made = sem("logits_made")
        logits_shifted = sem("logits_shifted")
        exps_made = sem("exps_made")
        picks_made = sem("picks_made")
        places_counted = sem("places_counted")
        slots_made = sem("slots_made")
        rows_hi = sem("rows_hi")
        rows_lo = sem("rows_lo")
        rows_id = sem("rows_id")
        totals_made = sem("totals_made")
        counts_made = sem("counts_made")
        table_made = sem("table_made")
        pads_stored = sem("pads_stored")
        junk_stored = sem("junk_stored")
        w_loaded = sem("w_loaded")
        w_squared = sem("w_squared")
        w_summed = sem("w_summed")
        w_normed = sem("w_normed")
        w_scaled = sem("w_scaled")
        w_hi = sem("w_hi")
        w_lo = sem("w_lo")
        level_stats = sem("level_stats")
        level_maxima = sem("level_maxima")
        level_scales = sem("level_scales")
        tile_transposed = sem("tile_transposed")
        tile_copied = sem("tile_copied")
        tile_params = sem("tile_params")
        z_made = sem("z_made")
        hid_made = sem("hid_made")
        hid_hi_made = sem("hid_hi_made")
        hid_lo_made = sem("hid_lo_made")
        y_made = sem("y_made")
        y_scaled = sem("y_scaled")
        y_ids = sem("y_ids")
        cb_cleared = sem("cb_cleared")
        cb_loaded = sem("cb_loaded")
        coef_grouped = sem("coef_grouped")
        coef_transposed = sem("coef_transposed")
        coef_copied = sem("coef_copied")
        corr_made = sem("corr_made")
        out_made = sem("out_made")
        x_loaded = [sem(f"x_loaded{h}") for h in range(2)]
        adj_loaded = [sem(f"adj_loaded{h}") for h in range(2)]
        x1_stored = [sem(f"x1_stored{h}") for h in range(2)]
        tile_loaded = [sem(f"tile_loaded{h}") for h in range(2)]
        y_sent = [sem(f"y_sent{h}") for h in range(2)]
        out_stored = [sem(f"out_stored{h}") for h in range(2)]
        rows_sent = [sem(f"rows_sent{h}") for h in range(GB)]
        yab_loaded = [sem(f"yab_loaded{h}") for h in range(GB)]


        def some(n):
            return not isinstance(n, int) or n > 0

        def ring(n, h):
            return (n - h) * 8 + 16

        def at(start, n):
            return bass.ds(start, n) if not isinstance(start, int) else slice(start, start + n)

        def w_load(sp, n, l, e, s):
            if some(2 * n):
                sp.wait_ge(w_lo, 2 * n)
            if some(2 * n):
                sp.wait_ge(w_hi, 2 * n)
            sp.nop(nofuse=True)
            sp.dma_start(stage[:, 0, :].rearrange("p (k f) -> p k f", k=KD), W1v[l][at(e, 1)].rearrange("e p k f -> (e p) k f")).then_inc(w_loaded, 16)
            sp.dma_start(stage[:, 1, :].rearrange("p (c d) -> p c d", c=FC), W2v[l][at(e, 1)].rearrange("e p c d -> (e p) c d")).then_inc(w_loaded, 16)

        def w_square(act, n, l, e, s, place_free=0):
            act.wait_ge(w_loaded, 32 * n + 32)
            act.wait_ge(v_lo, NB)
            if some(GB * n if l == 0 else NB):
                act.wait_ge(graph_summed, GB * n if l == 0 else NB)
            if l == 1:
                if some(place_free):
                    act.wait_ge(y_made, place_free)
            for m in range(2):
                act.activation(R[:, at(s * WSLOT + m * 2 * UNIT, UNIT)], stage[:, m, :], ACT.Square,
                               accum_out=wstat[:, m:m + 1]).then_inc(w_squared, 1)

        def w_norm(pool, n, l, e, s):
            pool.wait_ge(w_squared, 2 * n + 2)
            for m in range(2):
                pool.nop(nofuse=True)
                pool.partition_all_reduce(wtot[:, m:m + 1], wstat[:, m:m + 1], P, RED.add).then_inc(w_summed, 1)
            for m in range(2):
                pool.wait_ge(w_summed, 2 * n + 1 + m)
                pool.tensor_tensor(wnorm[:, m:m + 1], wtot[:, m:m + 1], half[:, 1:2], ALU.pow).then_inc(w_normed, 1)

        def w_scale(dve, n, l, e, s):
            dve.wait_ge(w_normed, 2 * n + 2)
            dve.tensor_scalar(wpow[:, :, at(n, 1)], wnorm[:, :].unsqueeze(2), 1e-15, None, ALU.max)
            dve.drain()
            dve.tensor_scalar(wpow[:, :, at(n, 1)].bitcast(I32), wpow[:, :, at(n, 1)].bitcast(I32), EXPONENT, None, ALU.bitwise_and)
            dve.drain()
            dve.reciprocal(winv[:, :, at(n, 1)], wpow[:, :, at(n, 1)])
            dve.drain()
            dve.tensor_scalar(wscl[:, :, at(n, 1)], winv[:, :, at(n, 1)], 8192.0, None, ALU.mult).then_inc(w_scaled, 1)

        def w_parts(s):
            b = s * WSLOT
            w1 = [R[:, at(b + h * UNIT, UNIT)] for h in range(2)]
            w2 = R[:, at(b + 2 * UNIT, 2 * UNIT)].rearrange("p (c h d) -> p h c d", h=2, d=D)
            return [(w1[0], w1[1], stage[:, 0, :]),
                    (w2[:, 0], w2[:, 1], stage[:, 1, :].rearrange("p (c d) -> p c d", c=FC))]

        def w_high(act, n, l, e, s):
            act.wait_ge(w_scaled, n + 1)
            act.wait_ge(w_squared, 2 * n + 2)
            for m, (hi, lo, src) in enumerate(w_parts(s)):
                act.activation(hi, src, ACT.Copy, scale=wscl[:, m, at(n, 1)]).then_inc(w_hi, 1)

        def w_low(dve, n, l, e, s):
            for m, (hi, lo, src) in enumerate(w_parts(s)):
                dve.wait_ge(w_hi, 2 * n + 1 + m)
                dve.nop(nofuse=True)
                dve.scalar_tensor_tensor(lo, src, wscl[:, m, at(n, 1)], hi, ALU.mult, ALU.subtract).then_inc(w_lo, 1)

        def level_scales_dve(dve, l):
            E, n0 = EXPERTS[l], 0 if l == 0 else EXPERTS[0]
            dve.wait_ge(b1_copied, l + 1)
            dve.tensor_reduce(lv[l][:, 0:1], b1T[l][:, :, :].rearrange("p e c -> p (e c)"), AX.X, ALU.max, apply_absolute_value=True)
            if l == 0:
                dve.memset(lv[l][:, 1:3], 0.0).then_inc(level_stats, 1)
            else:
                dve.tensor_reduce(lv[l][:, 1:2], CB[:, :], AX.X, ALU.max, apply_absolute_value=True)
                dve.tensor_copy(lv[l][:, 2:3], yrun[:, 0:1]).then_inc(level_stats, 1)
            dve.drain()
            dve.memset(lv[l][:, 15:16], 0.0).then_inc(level_stats, 1)
            dve.wait_ge(level_maxima, 3 * l + 3)
            X, M1, PW = lv[l], lve[l], wpow
            if l == 0:
                dve.memset(X[:, 6:7], 1.0)
                dve.drain()
            else:
                dve.tensor_tensor(X[:, 6:7], X[:, 4:5], X[:, 5:6], ALU.add)
                dve.drain()
                dve.tensor_scalar(X[:, 6:7], X[:, 6:7], 1e-15, None, ALU.max)
                dve.drain()
            dve.tensor_scalar(X[:, 7:8].bitcast(I32), X[:, 6:7].bitcast(I32), EXPONENT, None, ALU.bitwise_and)
            dve.drain()
            dve.reciprocal(X[:, 8:9], X[:, 7:8])
            dve.drain()
            dve.tensor_scalar(X[:, 9:10], X[:, 8:9], 1024.0 if l == 0 else 8192.0, None, ALU.mult).then_inc(level_scales, 1)
            dve.tensor_scalar(X[:, 10:11], X[:, 7:8], 1 / 1024.0 if l == 0 else 1 / 8192.0, None, ALU.mult)
            dve.tensor_scalar(X[:, 11:12], X[:, 6:7], 32.0, None, ALU.mult)
            dve.drain()

        def level_params_dve(dve, l):
            E, n0 = EXPERTS[l], 0 if l == 0 else EXPERTS[0]
            X, M1 = lv[l], lve[l]
            order = [(e, (NG - 1 - e) if l == 0 else EXPERTS[0] + e) for e in range(E)]
            for e, n in order:
                dve.scalar_tensor_tensor(M1[:, 0, e:e + 1], wpow[:, 0, n:n + 1], X[:, 11:12], X[:, 3:4], ALU.mult, ALU.add)
            dve.drain()
            dve.tensor_scalar(M1[:, 1, :].bitcast(I32), M1[:, 0, :].bitcast(I32), EXPONENT, None, ALU.bitwise_and)
            dve.drain()
            dve.reciprocal(M1[:, 2, :], M1[:, 1, :])
            dve.drain()
            for e, n in order:
                dve.scalar_tensor_tensor(M1[:, 3, e:e + 1], wpow[:, 0, n:n + 1], 2.0, M1[:, 2, e:e + 1], ALU.mult, ALU.mult)
                dve.scalar_tensor_tensor(prm[l][:, e, 1:2], wpow[:, 1, n:n + 1], 2.0 ** -27, M1[:, 1, e:e + 1], ALU.mult, ALU.mult)
                dve.tensor_scalar(prm[l][:, e, 2:], b1T[l][:, e, :], M1[:, 2, e:e + 1], 16384.0, ALU.mult, ALU.mult)
            dve.drain()
            dve.tensor_scalar(prm[l][:, :, 0], M1[:, 3, :], X[:, 10:11], None, ALU.mult).then_inc(level_scales, 1)

        def level_scales_pool(pool, l):
            pool.wait_ge(level_stats, 2 * l + 2)
            for i in range(3):
                pool.partition_all_reduce(lv[l][:, 3 + i:4 + i], lv[l][:, i:i + 1], P, RED.max).then_inc(level_maxima, 1)


        def blk_of(l, g, b):
            return NB - GB - GB * g + b if l == 0 else GB * g - NB + b

        def route_t_pe(pe, q, b):
            pe.wait_ge(xr_made, q + 1)
            if some(q):
                pe.wait_ge(xr_copied, q)
            pe.wait_ge(xn_copied, NB)
            for k in range(KD):
                ins = pe.transpose(PX[:, k, :], xr[:, b, k * P:(k + 1) * P], ident[:, :])
            ins.then_inc(xr_transposed, 1)

        def route_copy_act(act, q, b):
            act.wait_ge(xr_transposed, q + 1)
            if some(q - 1):
                act.wait_ge(logits_made, q - 1)
            act.wait_ge(u_summed, NB)
            act.activation(xrT[:, 2 * (b % 2):2 * (b % 2) + 2, :], PX[:, 0:KD, :], ACT.Copy).then_inc(xr_copied, 1)

        def route_logits_pe(pe, l, g, q, b):
            pe.wait_ge(xr_copied, q + 1)
            if some(g):
                pe.wait_ge(logits_shifted, g)
            for k in range(KD):
                ins = pe.matmul(p_log[:, b, 0:EXPERTS[l]], xrT[:, 2 * (b % 2) + k, :], wr[l][:, k, :],
                                start=(k == 0), stop=(k == KD - 1))
            ins.then_inc(logits_made, 1)

        def route_pos_pe(pe, l, g):
            E = EXPERTS[l]
            pe.wait_ge(picks_made, g + 1)
            if some(g + l):
                pe.wait_ge(totals_made, g + l)
            if some(2 * g):
                pe.wait_ge(slots_made, 2 * g)
            for b in range(GB):
                pe.matmul(p_pos[:, b, 0:E], ones16[:, :], tot[:, 0:E], start=True, stop=False)
                for b2 in range(b):
                    pe.matmul(p_pos[:, b, 0:E], ones16[:, :], disp[:, b2, 0:E], start=False, stop=False)
                ins = pe.matmul(p_pos[:, b, 0:E], before[:, :], disp[:, b, 0:E], start=False, stop=True)
            ins.then_inc(places_counted, 1)

        def route_exp_act(act, l, g):
            act.wait_ge(logits_shifted, g + 1)
            act.activation(rt[:, 1, :, 0:EXPERTS[l]], rt[:, 0, :, 0:EXPERTS[l]], ACT.Exp).then_inc(exps_made, 1)

        def route_picks_dve(dve, l, g, blk):
            E = EXPERTS[l]
            r = [rt[:, i, :, 0:E] for i in range(12)]
            s = [rs[:, i, :] for i in range(8)]

            def wide(x):
                return x.unsqueeze(2).broadcast_to([P, GB, E])

            rank = rank_e[:, 0:E].unsqueeze(1).broadcast_to([P, GB, E])
            dve.wait_ge(logits_made, GB * g + GB)
            dve.tensor_reduce(s[0], p_log[:, :, 0:E], AX.X, ALU.max)
            dve.drain()
            dve.tensor_tensor(r[0], p_log[:, :, 0:E], wide(s[0]), ALU.subtract).then_inc(logits_shifted, 1)
            dve.wait_ge(exps_made, g + 1)
            dve.tensor_reduce(s[1], r[1], AX.X, ALU.add)
            dve.drain()
            dve.reciprocal(s[2], s[1])
            dve.drain()
            dve.tensor_tensor(r[2], r[1], wide(s[2]), ALU.mult)
            dve.drain()
            left, masks = r[2], []
            for i, (eq, best, pick) in enumerate(((3, 4, 5), (6, 7, 8))):
                dve.tensor_reduce(s[3 + i], left, AX.X, ALU.max)
                dve.drain()
                dve.tensor_tensor(r[eq], left, wide(s[3 + i]), ALU.is_equal)
                dve.drain()
                dve.tensor_tensor(r[best], r[eq], rank, ALU.mult)
                dve.drain()
                dve.tensor_reduce(s[5 + i], r[best], AX.X, ALU.max)
                dve.drain()
                dve.tensor_tensor(r[pick], r[best], wide(s[5 + i]), ALU.is_equal)
                dve.drain()
                masks.append(r[pick])
                if i == 0:
                    dve.scalar_tensor_tensor(r[9], r[pick], -2.0, r[2], ALU.mult, ALU.add)
                    dve.drain()
                    left = r[9]
            if some(g):
                dve.wait_ge(places_counted, g)
            dve.tensor_tensor(disp[:, :, 0:E], masks[0], masks[1], ALU.add).then_inc(picks_made, 1)
            dve.tensor_tensor(r[10], masks[0], masks[1], ALU.add)
            for i in range(2):
                dve.tensor_copy(p12[:, at(blk, GB), i], s[3 + i])
            dve.tensor_copy(coef[:, at(blk, GB), E:2 * E], r[2])
            dve.drain()
            dve.tensor_tensor(r[11], r[10], r[2], ALU.mult)
            dve.drain()
            dve.tensor_tensor(coef[:, at(blk, GB), 0:E], r[2], r[11], ALU.subtract)

        def route_slots_dve(dve, l, g):
            E = EXPERTS[l]
            base = base_e[:, 0:E].unsqueeze(1).broadcast_to([P, GB, E])
            dve.wait_ge(places_counted, g + 1)
            dve.tensor_tensor(rt[:, 0, :, 0:E], p_pos[:, :, 0:E], base, ALU.add)
            dve.tensor_reduce(cpick[:, 0:E], disp[:, :, 0:E].rearrange("p b e -> p e b"), AX.X, ALU.add)
            dve.drain()
            dve.tensor_tensor(rt[:, 3, :, 0:E], rt[:, 0, :, 0:E], rt[:, 5, :, 0:E], ALU.mult)
            dve.tensor_tensor(rt[:, 4, :, 0:E], rt[:, 0, :, 0:E], rt[:, 8, :, 0:E], ALU.mult)
            dve.tensor_tensor(tot[:, 0:E], tot[:, 0:E], cpick[:, 0:E], ALU.add).then_inc(totals_made, 1)
            dve.drain()
            for b in range(GB):
                if some(2 * 16 * g):
                    dve.wait_ge(rows_sent[b], 2 * 16 * g)
            with nc.allow_low_precision(reason="row numbers, whole and below 2^24"):
                for i in range(2):
                    dve.tensor_reduce(slot[:, :, i], rt[:, 3 + i, :, 0:E], AX.X, ALU.add).then_inc(slots_made, 1)

        def pack_act(act, l, q, b):
            act.wait_ge(xr_made, q + 1)
            if some((q - b) * 8):
                act.wait_ge(rows_sent[b], (q - b) * 8)
            act.wait_ge(level_scales, 2 * l + 1)
            act.activation(rows[:, b, :, 0:D], xr[:, b, :].unsqueeze(1).broadcast_to([P, 2, D]), ACT.Copy,
                           scale=lv[l][:, 9:10]).then_inc(rows_hi, 1)

        def pack_dve(dve, l, q, b, blk):
            dve.wait_ge(rows_hi, q + 1)
            dve.scalar_tensor_tensor(rows[:, b, :, D:2 * D], xr[:, b, :].unsqueeze(1).broadcast_to([P, 2, D]),
                                     lv[l][:, 9:10], rows[:, b, :, 0:D], ALU.mult, ALU.subtract).then_inc(rows_lo, 1)
            dve.tensor_copy(rows[:, b, :, IDC:IDC + 2].bitcast(I32).rearrange("p r a -> p (r a)"),
                            ids[:, at(blk, 1), :].rearrange("p a r -> p (a r)")).then_inc(rows_id, 1)

        def scatter_pool(pool, l, g, q, b):
            pool.wait_ge(slots_made, 2 * g + 2)
            pool.wait_ge(rows_lo, q + 1)
            pool.wait_ge(rows_id, q + 1)
            for i in range(2):
                pool.nop(nofuse=True)
                pool.indirect_dma_start(arena[l], bass.IndirectOffsetOnAxis(ap=slot[:, b, i:i + 1], axis=0),
                                        rows[:, b, i, :], None).then_inc(rows_sent[b], 16)

        def table_dve(dve, l):
            E, NT = EXPERTS[l], TILES[l]
            c = [cnt[:, i, 0:E] for i in range(8)]
            tn = tileno[:, 0:NT]
            dve.wait_ge(counts_made, l + 1)
            dve.tensor_copy(c[0], p_cnt[0:1, 0:E])
            dve.memset(c[4], 1.0)
            dve.drain()
            dve.tensor_copy(cnti[:, 0, 0:E], c[0])
            dve.tensor_tensor(cnti[:, 1, 0:E], c[0], base_e[0:1, 0:E], ALU.add)
            dve.drain()
            dve.tensor_scalar(cnti[:, 0, 0:E], cnti[:, 0, 0:E], 7, None, ALU.logical_shift_right)
            dve.drain()
            dve.tensor_copy(c[1], cnti[:, 0, 0:E])
            dve.drain()
            dve.tensor_scalar(c[1], c[1], 1.0, None, ALU.add)
            dve.drain()
            dve.tensor_tensor_scan(c[2], c[4], c[1], 0.0, ALU.mult, ALU.add)
            dve.tensor_scalar(c[3], c[1], -float(P), float(ARENA), ALU.mult, ALU.add)
            dve.drain()
            dve.memset(c[3][:, E - 1:E], float(1 << 17))
            dve.memset(steps[:, 1, E - 1:E, 0:NT], 0.0)
            dve.drain()
            for e in range(E):
                dve.tensor_scalar(steps[:, 0, e, 0:NT], tn, c[2][:, e:e + 1], c[3][:, e:e + 1], ALU.is_ge, ALU.mult)
                if e < E - 1:
                    dve.tensor_scalar(steps[:, 1, e, 0:NT], tn, c[2][:, e:e + 1], None, ALU.is_ge)
            dve.drain()
            for i in range(2):
                dve.tensor_reduce(tabf[:, i, 0:NT], steps[:, i, 0:E, 0:NT].rearrange("p e t -> p t e"), AX.X, ALU.add)
            dve.drain()
            dve.scalar_tensor_tensor(tabf[:, 0, 0:NT], tn, float(P), tabf[:, 0, 0:NT], ALU.mult, ALU.add)
            dve.drain()
            dve.tensor_tensor(tab[:, 0, 0:NT], tabf[:, 0, 0:NT], junkrow[:, l, 0:NT], ALU.min)
            dve.tensor_scalar(tab[:, 1, 0:NT], tabf[:, 1, 0:NT], float(WSLOT), float(FIRSTSLOT[l] * WSLOT), ALU.mult, ALU.add)
            dve.tensor_copy(tab[:, 2, 0:NT], tabf[:, 1, 0:NT])
            dve.drain()
            dve.memset(cnt[:, 5, 0:1], 0.0).then_inc(table_made, 1)

        def pads_sp(sp, l):
            sp.wait_ge(table_made, l + 1)
            sp.wait_ge(consts_made, NCONST)
            for e in range(EXPERTS[l]):
                row = sp.value_load(cnti[0:1, 1, e:e + 1], min_val=e * ARENA, max_val=e * ARENA + T)
                sp.dma_start(arena[l][at(row, P), 0:2 * D], zeros[:, :]).then_inc(pads_stored, 16)
                sp.dma_start(arena[l][at(row, P), IDC:IDC + 2], padids[:, e:e + 1].bitcast(F16)).then_inc(pads_stored, 16)

        T0 = (0, TILES[0])

        def tile_load(sp, l, t, h):
            n = T0[l] + t
            if isinstance(t, int) and t == 0:
                for b in range(GB):
                    sp.wait_ge(rows_sent[b], 2 * 16 * NG * (l + 1))
                sp.wait_ge(pads_stored, 32 * sum(EXPERTS[:l + 1]))
                sp.wait_ge(junk_stored, 128)
            src = sp.value_load(tab[0:1, 0, at(t, 1)], min_val=0, max_val=JUNK[l] + P)
            if some(n - 1):
                sp.wait_ge(tile_transposed, n - 1)
            if some(3 * (n - 1)):
                sp.nop(nofuse=True)
                sp.wait_ge(tile_params, 3 * (n - 1))
            sp.dma_start(xtile[:, h, :], arena[l][at(src, P), :]).then_inc(tile_loaded[h], 16)


        def turn_gnn(g):
            return g, 0, EXPERTS[0] - 1 - g, NSLOT - 1 - g

        def turn_early(j):
            return EXPERTS[0] + j, 1, j, j

        def turn_late(g):
            return EXPERTS[0] + EARLY + g, 1, EARLY + g, EARLY + g

        def in_groups(eng, body, peeled, count):
            for g in range(peeled):
                body(g, True, g > 0, True)
            with eng.Fori(peeled, count) as g:
                body(g, True, True, True)
            for g in range(count, NG):
                body(g, True, True, False)
            body(NG, False, True, False)

        def in_tiles(eng, l, step):
            NT = TILES[l]
            first = 4 if l == 0 else 2
            for t in range(first):
                step(t, t % 2, None)
            mid = first + 4 * EARLY if l == 0 else first
            if l == 0:
                with eng.Fori(0, EARLY) as j:
                    for o in range(4):
                        step(j * 4 + (first + o), o % 2, (j, o))
            with eng.Fori(mid // 2, NT // 2 - 1) as i:
                for o in range(2):
                    step(i * 2 + o, o, None)
            for t in range(NT - 2, NT):
                step(t, t % 2, None)

        block = ctx.enter_context(nc.Block())

        @block.sync
        def _(sp):
            sp.dma_start(wg_nat, gnn_W.rearrange("(k p) d -> p k d", p=P)).then_inc(gnnw_loaded, 16)
            sp.dma_start(brow[:, :], gnn_b.rearrange("(a d) -> a d", a=1)).then_inc(gnnw_loaded, 16)

            def front(r, h):
                if some(r - 1):
                    sp.wait_ge(xn_made, r - 1)
                sp.dma_start(xin[:, h, :], x[at(r * P, P), :]).then_inc(x_loaded[h], 16)
                if some(4 * (r - 1)):
                    sp.wait_ge(adj_transposed, 4 * (r - 1))
                sp.dma_start(stage[:, h, :], adj[at(r * P, P), :]).then_inc(adj_loaded[h], 16)

            for r in range(2):
                front(r, r)
            for l in range(2):
                sp.dma_start(wr[l][:, :, :], Wr[l].rearrange("(k p) e -> p k e", p=P)).then_inc(small_loaded, 16)
                sp.dma_start(b1n[l][:, :], b1[l].rearrange("e (c p) -> (e c) p", p=P)).then_inc(small_loaded, 16)
            sp.wait_ge(consts_made, NCONST)
            for l in range(2):
                for o in range(2):
                    junk = arena[l][JUNK[l] + o * P:JUNK[l] + (o + 1) * P, :]
                    sp.dma_start(junk[:, 0:2 * D], zeros[:, :]).then_inc(junk_stored, 16)
                    sp.dma_start(junk[:, IDC:IDC + 2], padids[:, EM + o:EM + o + 1].bitcast(F16)).then_inc(junk_stored, 16)
            with sp.Fori(1, NB // 2) as i:
                for o in range(2):
                    front(i * 2 + o, o)

            def group_gnn(g, new, old, prep):
                if not new:
                    return
                if prep:
                    if isinstance(g, int):
                        sp.wait_ge(adj_transposed, 4 * NB)
                    w_load(sp, *turn_gnn(g))
                for b in range(GB):
                    q = g * GB + b
                    sp.wait_ge(xn_made, NB)
                    if some(q - 1):
                        sp.wait_ge(bias_added, q - 1)
                    sp.nop(nofuse=True)
                    sp.dma_start(xin[:, b % 2, :], x[at((NB - GB - GB * g + b) * P, P), :]).then_inc(x_loaded[b % 2], 16)
                    if b:
                        store_x1(g * GB + b - 1, g, b - 1)
                store_x1(g * GB + GB - 1, g, GB - 1)

            def store_x1(q, g, b):
                sp.wait_ge(x1_made, q + 1)
                sp.dma_start(x1_dram[at((NB - GB - GB * g + b) * P, P), :], xn[:, b % 2, :]).then_inc(x1_stored[b % 2], 16)

            in_groups(sp, group_gnn, 2, NG)

            def tiles(l):
                pads_sp(sp, l)
                tile_load(sp, l, 0, 0)

                def step(t, h, turn):
                    if not (isinstance(t, int) and t == TILES[l] - 1):
                        tile_load(sp, l, t + 1, 1 - h)
                    if turn and turn[1] == 0:
                        w_load(sp, *turn_early(turn[0]))

                in_tiles(sp, l, step)

            def load_corrections(l):
                E = EXPERTS[l]
                for h in range(2):
                    sp.wait_ge(y_sent[h], 8 * (T0[l] + TILES[l]))
                sp.wait_ge(cb_cleared, l + 1)
                for b in range(GB):
                    sp.dma_start(CB[CW * b:CW * b + E, :],
                                 ys[l][PADROW:PADROW + E * P, :].rearrange("(e p) d -> e p d", p=P)[:, 0, :]).then_inc(cb_loaded, 16)
                    sp.dma_start(CB[CW * b + E:CW * b + 2 * E, :], b2[l]).then_inc(cb_loaded, 16)

            tiles(0)
            load_corrections(0)

            def group_mid(g, new, old, prep):
                if not new:
                    return
                if prep:
                    w_load(sp, *turn_late(g))
                for b in range(GB):
                    sp.wait_ge(xr_made, NB + GB * g + b - GB + 1)
                    sp.dma_start(yab[:, b, :, :], ys[0][0:2 * T, :].rearrange("(t r) d -> t r d", r=2)[at((g * GB + b) * P, P), :, :]).then_inc(yab_loaded[b], 16)

            in_groups(sp, group_mid, 1, NG - 1)
            tiles(1)
            load_corrections(1)

            def last(g, first):
                for b in range(GB):
                    c = g * GB + b
                    if not (first and b < 2):
                        sp.wait_ge(out_made, c - 1)
                    if not first:
                        sp.nop(nofuse=True)
                        sp.wait_ge(out_made, c - GB + 1)
                    sp.dma_start(xin[:, b % 2, :], x1_dram[at(c * P, P), :]).then_inc(x_loaded[b % 2], 16)
                    sp.dma_start(yab[:, b, :, :], ys[1][0:2 * T, :].rearrange("(t r) d -> t r d", r=2)[at(c * P, P), :, :]).then_inc(yab_loaded[b], 16)
                    if not (first and b == 0):
                        store(c - 1, (b - 1) % 2)

            def store(c, h):
                sp.wait_ge(out_made, c + 1)
                sp.dma_start(out[at(c * P, P), :], xn[:, h, :]).then_inc(out_stored[h], 16)

            for h in range(2):
                sp.wait_ge(x1_stored[h], 8 * NB)
            last(0, True)
            with sp.Fori(1, NG) as g:
                last(g, False)
            store(NB - 1, 1)
            for h in range(2):
                sp.wait_ge(out_stored[h], 8 * NB)

        @block.gpsimd
        def _(pool):
            pool.iota(diff, [[1, P]], base=0, channel_multiplier=-1, allow_small_or_imprecise_dtypes=True).then_inc(consts_made, 1)
            pool.memset(onesrow[:, :], 1.0).then_inc(consts_made, 1)
            pool.memset(half[:, 0:1], -0.5).then_inc(consts_made, 1)
            pool.memset(half[:, 1:2], 0.5).then_inc(consts_made, 1)
            pool.memset(zeros[:, :], 0.0).then_inc(consts_made, 1)
            pool.memset(ones16[:, :], 1.0).then_inc(consts_made, 1)
            pool.iota(tileno[:, :], [[1, max(TILES)]], base=0, channel_multiplier=0, allow_small_or_imprecise_dtypes=True).then_inc(consts_made, 1)
            for l in range(2):
                pool.iota(junkrow[:, l, :].rearrange("a (i o) -> a i o", o=2), [[0, max(TILES) // 2], [P, 2]], base=JUNK[l],
                          channel_multiplier=0, allow_small_or_imprecise_dtypes=True).then_inc(consts_made, 1)
            pool.iota(ids[:, :, :], [[2 * P, NB], [1, 2]], base=0, channel_multiplier=2).then_inc(consts_made, 1)
            pool.iota(padids[:, :], [[P, EM + 2]], base=PADROW, channel_multiplier=1).then_inc(consts_made, 1)
            pool.iota(base_e[:, :], [[ARENA, EM]], base=0, channel_multiplier=0, allow_small_or_imprecise_dtypes=True).then_inc(consts_made, 1)
            pool.iota(rank_e[:, :], [[-1, EM]], base=EM, channel_multiplier=0, allow_small_or_imprecise_dtypes=True).then_inc(consts_made, 1)
            pool.memset(coef[:, :, :], 0.0).then_inc(consts_made, 1)
            pool.memset(tot[:, :], 0.0).then_inc(consts_made, 1)
            pool.memset(yrun[:, :], 0.0).then_inc(consts_made, 1)

            def front(r, h):
                pool.wait_ge(var_made, r + 1)
                pool.tensor_tensor(rstd[:, h:h + 1], vare[:, h:h + 1], half[:, 0:1], ALU.pow).then_inc(rstd_made, 1)
                pool.wait_ge(deg_rounded, r + 1)
                pool.tensor_tensor(dis[:, at(r, 1)], degE[:, at(r, 1)], half[:, 0:1], ALU.pow).then_inc(dis_made, 1)
                pool.tensor_scalar(stage[:, h, :], stage[:, h, :], rdeg[:, h:h + 1], 4096.0, ALU.mult, ALU.mult).then_inc(adj_scaled, 1)

            for r in range(2):
                front(r, r)
            with pool.Fori(1, NB // 2) as i:
                for o in range(2):
                    front(i * 2 + o, o)
            pool.wait_ge(v_bounds, 2)
            for i in range(2):
                pool.partition_all_reduce(gst[:, 2 + i:3 + i], gst[:, i:i + 1], P, RED.max).then_inc(v_bounds_max, 1)
            pool.wait_ge(v_bounds_max, 2)
            pool.tensor_tensor(gst[:, 4:5], gst[:, 2:3], half[:, 1:2], ALU.pow).then_inc(v_bound_root, 1)

            level_scales_pool(pool, 0)

            def group_gnn(g, new, old, prep):
                for b in range(GB):
                    q = g * GB + b
                    if new:
                        pool.wait_ge(x_loaded[b % 2], ring(NB + q, b % 2))
                        pool.wait_ge(bias_copied, 1)
                        if some(q - 1):
                            pool.wait_ge(x1_made, q - 1)
                        pool.tensor_tensor(xb[:, b % 2, :], xin[:, b % 2, :], bB[:, :], ALU.add).then_inc(bias_added, 1)
                    if old and b == GB - 1:
                        for b2 in range(2):
                            scatter_pool(pool, 0, g - 1, q - b - GB + b2, b2)
                    if new:
                        pool.wait_ge(var_made, NB + q + 1)
                        pool.tensor_tensor(rstd[:, b % 2:b % 2 + 1], vare[:, b % 2:b % 2 + 1], half[:, 0:1], ALU.pow).then_inc(rstd_made, 1)
                    if prep and b == 1:
                        w_norm(pool, *turn_gnn(g))
                if old:
                    for b2 in range(2, GB):
                        scatter_pool(pool, 0, g - 1, g * GB - GB + b2, b2)

            in_groups(pool, group_gnn, 2, NG)

            def keep(l, t, h):
                n = T0[l] + t
                e = pool.value_load(tab[0:1, 2, at(t, 1)], min_val=0, max_val=EXPERTS[l] - 1)
                pool.wait_ge(tile_loaded[h], ring(n, h))
                if some(FC * (n - 1)):
                    pool.wait_ge(hid_made, FC * (n - 1))
                pool.tensor_copy(tprm[:, h, :], prm[l][:, at(e, 1), :].rearrange("p a c -> p (a c)")).then_inc(tile_params, 1)
                pool.tensor_copy(tgam[:, at(t, 1)], prm[l][:, at(e, 1), 1:2].rearrange("p a c -> p (a c)")).then_inc(tile_params, 1)
                pool.tensor_copy(tids[:, at(t, 1)], xtile[:, h, IDC:IDC + 2].bitcast(I32)).then_inc(tile_params, 1)

            def scatter_results(l, t, h):
                n = T0[l] + t
                if some((n - h) * 8):
                    pool.wait_ge(y_sent[h], (n - h) * 8)
                pool.wait_ge(tile_params, 3 * n + 3)
                pool.nop(nofuse=True)
                pool.tensor_copy(yid[:, h:h + 1], tids[:, at(t, 1)]).then_inc(y_ids, 1)
                pool.wait_ge(y_ids, n + 1)
                pool.wait_ge(y_scaled, n + 1)
                pool.nop(nofuse=True)
                pool.indirect_dma_start(ys[l], bass.IndirectOffsetOnAxis(ap=yid[:, h:h + 1], axis=0), xn[:, h, :], None).then_inc(y_sent[h], 16)

            def tiles(l):
                pool.wait_ge(table_made, l + 1)
                pool.wait_ge(level_scales, 2 * l + 2)
                if l == 1:
                    for h in range(2):
                        pool.wait_ge(y_sent[h], 8 * TILES[0])
                keep(l, 0, 0)

                def step(t, h, turn):
                    if not (isinstance(t, int) and t == TILES[l] - 1):
                        keep(l, t + 1, 1 - h)
                    if turn and turn[1] == 2:
                        w_norm(pool, *turn_early(turn[0]))
                    if not (isinstance(t, int) and t == 0):
                        scatter_results(l, t - 1, 1 - h)

                in_tiles(pool, l, step)
                scatter_results(l, TILES[l] - 1, (TILES[l] - 1) % 2)

            tiles(0)
            level_scales_pool(pool, 1)

            def group_mid(g, new, old, prep):
                if prep:
                    w_norm(pool, *turn_late(g))
                if old:
                    for b in range(GB):
                        scatter_pool(pool, 1, NG + g - 1, NB + g * GB - GB + b, b)

            in_groups(pool, group_mid, 1, NG - 1)
            tiles(1)

        @block.scalar
        def _(act):
            act.wait_ge(gnnw_loaded, 32)
            for k in range(KD):
                act.activation(U[:, 2 * D * k:2 * D * (k + 1)].bitcast(F32), wg_nat[:, k, :], ACT.Square,
                               accum_out=gst[:, 10 + k:11 + k]).then_inc(gnnw_squared, 1)
            act.wait_ge(bias_spread, 1)
            act.activation(bB[:, :], PM[:, 0:D], ACT.Copy).then_inc(bias_copied, 1)
            act.wait_ge(gnnw_transposed, 1)
            for k in range(KD):
                act.activation(wgT[:, k, :], Zq[:, k, 0:D], ACT.Copy).then_inc(gnnw_copied, 1)

            def front(r, h):
                act.wait_ge(adj_loaded[h], ring(r, h))
                act.activation(stage[:, h, :], stage[:, h, :], ACT.Copy, accum_out=deg[:, at(r, 1)]).then_inc(deg_made, 1)
                act.wait_ge(xn_transposed, r + 1)
                if some(r - 1):
                    act.wait_ge(u_summed, r - 1)
                act.activation(xrT[:, 2 * h:2 * h + 2, :], PX[:, 0:KD, :], ACT.Copy).then_inc(xn_copied, 1)
                act.wait_ge(u_summed, r + 1)
                act.activation(u_all[:, at(r, 1), :].rearrange("p a d -> p (a d)"), Y[:, h, :], ACT.Copy).then_inc(u_copied, 1)

            def back(r, h):
                for q in range(4):
                    act.wait_ge(adj_transposed, r * 4 + q + 1)
                    act.activation(R[:, at(r * ATB + q * 4 * P, 4 * P)], Zq[:, q, :], ACT.Copy).then_inc(adj_hi, 1)

            front(0, 0)
            for r in range(2):
                front(r + 1, 1 - r)
                back(r, r)
            with act.Fori(1, NB // 2 - 1) as i:
                for o in range(2):
                    front(i * 2 + (o + 1), 1 - o)
                    back(i * 2 + o, o)
            front(NB - 1, 1)
            back(NB - 2, 0)
            back(NB - 1, 1)
            for l in range(2):
                act.wait_ge(b1_transposed, 2)
                act.activation(b1T[l][:, :, :].rearrange("p e c -> p (e c)"), PM[:, 256 + 64 * l:256 + 64 * l + EXPERTS[l] * FC], ACT.Copy).then_inc(b1_copied, 1)
            act.wait_ge(v_scales, 1)
            with act.Fori(0, NB) as j:
                act.activation(v[:, at(j, 1), 0, :].rearrange("p a d -> p (a d)"), u_all[:, at(j, 1), :].rearrange("p a d -> p (a d)"),
                               ACT.Copy, scale=vscale[:, at(j, 1)]).then_inc(v_hi, 1)

            def group(l):
                def body(g, new, old, prep):
                    G = g + NG * l
                    turn = (turn_gnn if l == 0 else turn_late)
                    if new and l == 1:
                        act.wait_ge(coef_transposed, g + 1)
                        if some(GB * g):
                            act.wait_ge(corr_made, GB * g)
                        act.activation(cT[:, :], p_cT, ACT.Copy).then_inc(coef_copied, 1)
                    for b in range(GB):
                        q = G * GB + b
                        if old:
                            pack_act(act, l, q - GB, b)
                            if b == 0:
                                route_copy_act(act, q - 1, GB - 1)
                            elif b == 1:
                                route_exp_act(act, l, G - 1)
                        if new and b:
                            route_copy_act(act, q - 1, b - 1)
                        if prep and b == 0:
                            w_square(act, *turn(g), place_free=TILES[0])
                        if prep and b == 2:
                            w_high(act, *turn(g))
                return body

            in_groups(act, group(0), 2, NG)

            def tile_copy(l, t, h):
                n = T0[l] + t
                act.wait_ge(tile_transposed, n + 1)
                if some(2 * (n - 1)):
                    act.wait_ge(z_made, 2 * (n - 1))
                act.activation(xT[:, h, :, :], PT[:, :, 0, :], ACT.Copy).then_inc(tile_copied, 1)

            def tiles(l):
                if l == 0:
                    act.wait_ge(logits_made, NB)
                    act.wait_ge(graph_summed, NB)
                else:
                    act.wait_ge(logits_made, 2 * NB)
                tile_copy(l, 0, 0)

                def step(t, h, turn):
                    n = T0[l] + t
                    if not (isinstance(t, int) and t == TILES[l] - 1):
                        tile_copy(l, t + 1, 1 - h)
                    act.wait_ge(tile_params, 3 * n + 3)
                    if some(2 * n):
                        act.wait_ge(hid_lo_made, 2 * n)
                    for c in range(FC):
                        if c % 4 == 0:
                            act.wait_ge(z_made, n * 2 + c // 4 + 1)
                        act.activation(hid[:, c, :], Z[:, h, c, :], ACT.Relu, bias=tprm[:, h, 2 + c:3 + c],
                                       scale=tprm[:, h, 0:1]).then_inc(hid_made, 1)
                    if some(n - 1):
                        act.wait_ge(y_made, n - 1)
                    for m in range(2):
                        act.wait_ge(hid_made, n * FC + 4 * m + 4)
                        act.activation(hid_hi[:, h, 4 * m:4 * m + 4, :], hid[:, 4 * m:4 * m + 4, :], ACT.Copy).then_inc(hid_hi_made, 1)
                    if turn and turn[1] == 1:
                        w_square(act, *turn_early(turn[0]))
                    if turn and turn[1] == 3:
                        w_high(act, *turn_early(turn[0]))

                in_tiles(act, l, step)

            tiles(0)
            in_groups(act, group(1), 1, NG - 1)
            tiles(1)

            def last(g):
                act.wait_ge(coef_transposed, g + NG + 1)
                act.wait_ge(corr_made, g * GB + NB)
                act.activation(cT[:, :], p_cT, ACT.Copy).then_inc(coef_copied, 1)
            with act.Fori(0, NG) as g:
                last(g)

        @block.vector
        def _(dve):
            dve.wait_ge(consts_made, NCONST)
            dve.tensor_scalar(ident[:, :], diff, 0.0, None, ALU.is_equal)
            dve.tensor_scalar(ident16[:, :], diff, 0.0, None, ALU.is_equal)
            dve.tensor_scalar(before[:, :], diff, 0.0, None, ALU.is_gt).then_inc(masks_made, 1)
            dve.drain()
            dve.memset(cpick[:, 0:1], 0.0).then_inc(masks_made, 1)

            def front(r, h):
                dve.wait_ge(x_loaded[h], ring(r, h))
                dve.bn_stats(stat[:, h, :], xin[:, h, :])
                dve.drain()
                dve.bn_aggr(mv[:, h, :], stat[:, h, :])
                dve.drain()
                dve.tensor_scalar(vare[:, h:h + 1], mv[:, h, 1:2], EPS_LN, None, ALU.add).then_inc(var_made, 1)
                dve.wait_ge(deg_made, r + 1)
                dve.tensor_scalar(degE[:, at(r, 1)], deg[:, at(r, 1)], EPS_DEG, None, ALU.add)
                dve.drain()
                dve.tensor_scalar(pdeg[:, at(r, 1)].bitcast(I32), degE[:, at(r, 1)].bitcast(I32), EXPONENT, None, ALU.bitwise_and)
                dve.drain()
                dve.reciprocal(rdeg[:, h:h + 1], pdeg[:, at(r, 1)]).then_inc(deg_rounded, 1)
                dve.wait_ge(rstd_made, r + 1)
                if some(r - 1):
                    dve.wait_ge(xn_transposed, r - 1)
                dve.tensor_scalar(xn[:, h, :], xin[:, h, :], mv[:, h, 0:1], rstd[:, h:h + 1], ALU.subtract, ALU.mult).then_inc(xn_made, 1)

            def back(r, h):
                for q in range(4):
                    dve.wait_ge(adj_hi, r * 4 + q + 1)
                    dve.tensor_tensor(R[:, at(r * ATB + (NB * P + q * 4 * P), 4 * P)], Zq[:, q, :],
                                      R[:, at(r * ATB + q * 4 * P, 4 * P)], ALU.subtract).then_inc(adj_lo, 1)

            front(0, 0)
            for r in range(2):
                front(r + 1, 1 - r)
                back(r, r)
            with dve.Fori(1, NB // 2 - 1) as i:
                for o in range(2):
                    front(i * 2 + (o + 1), 1 - o)
                    back(i * 2 + o, o)
            front(NB - 1, 1)
            back(NB - 2, 0)
            back(NB - 1, 1)

            dve.wait_ge(gnnw_squared, 2)
            dve.wait_ge(dis_made, NB)
            dve.tensor_tensor(gst[:, 0:1], gst[:, 10:11], gst[:, 11:12], ALU.max).then_inc(v_bounds, 1)
            dve.tensor_reduce(gst[:, 1:2], dis[:, :], AX.X, ALU.max).then_inc(v_bounds, 1)
            dve.wait_ge(v_bound_root, 1)
            dve.tensor_scalar(gst[:, 5:6], gst[:, 4:5], 16.0, gst[:, 3:4], ALU.mult, ALU.mult)
            dve.drain()
            dve.tensor_scalar(gst[:, 5:6], gst[:, 5:6], 1e-15, None, ALU.max)
            dve.drain()
            dve.tensor_scalar(gst[:, 6:7].bitcast(I32), gst[:, 5:6].bitcast(I32), EXPONENT, None, ALU.bitwise_and)
            dve.drain()
            dve.reciprocal(gst[:, 7:8], gst[:, 6:7])
            dve.drain()
            dve.tensor_scalar(gscale[:, :], dis[:, :], gst[:, 6:7], 2.0 ** -26, ALU.mult, ALU.mult)
            dve.drain()
            dve.tensor_tensor(gscale[:, :], gscale[:, :], pdeg[:, :], ALU.mult)
            dve.tensor_scalar(vscale[:, :], dis[:, :], gst[:, 7:8], 16384.0, ALU.mult, ALU.mult).then_inc(v_scales, 1)
            dve.drain()
            with dve.Fori(0, NB) as j:
                dve.wait_ge(v_hi, j + 1)
                dve.scalar_tensor_tensor(v[:, at(j, 1), 1, :].rearrange("p a d -> p (a d)"),
                                         u_all[:, at(j, 1), :].rearrange("p a d -> p (a d)"), vscale[:, at(j, 1)],
                                         v[:, at(j, 1), 0, :].rearrange("p a d -> p (a d)"), ALU.mult, ALU.subtract).then_inc(v_lo, 1)
            level_scales_dve(dve, 0)

            def group_gnn(g, new, old, prep):
                for b in range(GB):
                    q, h = g * GB + b, b % 2
                    if old:
                        pack_dve(dve, 0, q - GB, b, (NB - GB + GB + b) - GB * g)
                    if new:
                        dve.wait_ge(graph_summed, q + 1)
                        dve.wait_ge(bias_added, q + 1)
                        if some((q - h) * 8):
                            dve.wait_ge(x1_stored[h], (q - h) * 8)
                        dve.wait_ge(xn_transposed, NB)
                        dve.nop(nofuse=True)
                        dve.scalar_tensor_tensor(xn[:, h, :], Y[:, h, :], gscale[:, at(NB - GB + b - GB * g, 1)], xb[:, h, :],
                                                 ALU.mult, ALU.add).then_inc(x1_made, 1)
                        dve.wait_ge(x1_made, q + 1)
                        dve.bn_stats(stat[:, h, :], xn[:, h, :])
                        dve.drain()
                        dve.bn_aggr(mv[:, h, :], stat[:, h, :])
                        dve.drain()
                        dve.tensor_scalar(vare[:, h:h + 1], mv[:, h, 1:2], EPS_LN, None, ALU.add).then_inc(var_made, 1)
                        dve.wait_ge(rstd_made, NB + q + 1)
                        if some(q - GB + 1):
                            dve.wait_ge(xr_transposed, q - GB + 1)
                        if some(q - GB + 1):
                            dve.wait_ge(rows_lo, q - GB + 1)
                        dve.wait_ge(u_summed, NB)
                        dve.tensor_scalar(xr[:, b, :], xn[:, h, :], mv[:, h, 0:1], rstd[:, h:h + 1], ALU.subtract, ALU.mult).then_inc(xr_made, 1)
                    if old and b == 1:
                        route_picks_dve(dve, 0, g - 1, (NB - GB + GB) - GB * g)
                    if old and b == 2:
                        route_slots_dve(dve, 0, g - 1)
                    if prep and b == 1:
                        w_scale(dve, *turn_gnn(g))
                    if prep and b == GB - 1:
                        w_low(dve, *turn_gnn(g))

            in_groups(dve, group_gnn, 2, NG)
            table_dve(dve, 0)
            level_params_dve(dve, 0)

            def result(l, t, h):
                n = T0[l] + t
                dve.wait_ge(y_made, n + 1)
                dve.wait_ge(tile_params, 3 * n + 3)
                if some((n - h) * 8):
                    dve.wait_ge(y_sent[h], (n - h) * 8)
                dve.tensor_scalar(xn[:, h, :], Y[:, h, :], tgam[:, at(t, 1)], None, ALU.mult).then_inc(y_scaled, 1)
                if l == 0:
                    dve.wait_ge(y_scaled, n + 1)
                    dve.tensor_reduce(ymax[:, h:h + 1], xn[:, h, :], AX.X, ALU.max, apply_absolute_value=True)
                    dve.drain()
                    dve.tensor_tensor(yrun[:, 0:1], yrun[:, 0:1], ymax[:, h:h + 1], ALU.max)
                    dve.drain()

            def tiles(l):
                def step(t, h, turn):
                    n = T0[l] + t
                    if turn and turn[1] == 3:
                        w_scale(dve, *turn_early(turn[0]))
                    if some(n - 1):
                        dve.wait_ge(y_made, n - 1)
                    for m in range(2):
                        dve.wait_ge(hid_hi_made, 2 * n + m + 1)
                        dve.tensor_tensor(hid_lo[:, h, 4 * m:4 * m + 4, :], hid[:, 4 * m:4 * m + 4, :],
                                          hid_hi[:, h, 4 * m:4 * m + 4, :], ALU.subtract).then_inc(hid_lo_made, 1)
                    if not (isinstance(t, int) and t == 0):
                        result(l, t - 1, 1 - h)
                    if turn and turn[1] == 3:
                        w_low(dve, *turn_early(turn[0]))

                if l == 0:
                    for h in range(2):
                        dve.wait_ge(x1_stored[h], 8 * NB)
                in_tiles(dve, l, step)
                result(l, TILES[l] - 1, (TILES[l] - 1) % 2)

            dve.memset(CB[:, :], 0.0)
            dve.drain()
            dve.memset(cpick[:, 0:1], 0.0).then_inc(cb_cleared, 1)
            tiles(0)
            dve.wait_ge(cb_loaded, 2 * GB * 16)
            dve.memset(tot[:, :], 0.0).then_inc(totals_made, 1)
            dve.wait_ge(totals_made, NG + 1)
            level_scales_dve(dve, 1)

            def coefficients(G, g):
                if some(G):
                    dve.wait_ge(coef_transposed, G)
                dve.tensor_copy(cgrp[:, :, :], coef[:, at(g * GB, GB), :]).then_inc(coef_grouped, 1)

            def combine(l, c, b, into):
                blk = c - NB * l if l else c
                h = b % 2
                dve.wait_ge(corr_made, c + 1)
                dve.wait_ge(yab_loaded[b], (c - b) * 4 + 16)
                dve.scalar_tensor_tensor(xb[:, h, :], yab[:, b, 1, :], p12[:, at(blk, 1), 1].rearrange("p a -> p a"), Y[:, h, :], ALU.mult, ALU.add)
                dve.drain()
                if l == 1:
                    dve.wait_ge(x_loaded[h], ring(2 * NB + blk, h))
                    dve.tensor_tensor(xb[:, h, :], xb[:, h, :], xin[:, h, :], ALU.add)
                    dve.drain()
                return dve.scalar_tensor_tensor(into, yab[:, b, 0, :], p12[:, at(blk, 1), 0].rearrange("p a -> p a"), xb[:, h, :], ALU.mult, ALU.add)

            def group_mid(g, new, old, prep):
                if new:
                    coefficients(g, g)
                for b in range(GB):
                    q = NB + g * GB + b
                    if old:
                        pack_dve(dve, 1, q - GB, b, GB * g - GB + b)
                    if new:
                        dve.wait_ge(xr_transposed, q - GB + 1)
                        dve.wait_ge(rows_lo, q - GB + 1)
                        combine(0, g * GB + b, b, xr[:, b, :]).then_inc(xr_made, 1)
                    if old and b == 1:
                        route_picks_dve(dve, 1, NG + g - 1, GB * g - GB)
                    if old and b == 2:
                        route_slots_dve(dve, 1, NG + g - 1)
                    if prep and b == 1:
                        w_scale(dve, *turn_late(g))
                    if prep and b == GB - 1:
                        w_low(dve, *turn_late(g))

            in_groups(dve, group_mid, 1, NG - 1)
            table_dve(dve, 1)
            level_params_dve(dve, 1)
            dve.wait_ge(corr_made, NB)
            dve.memset(CB[:, :], 0.0)
            dve.drain()
            dve.memset(cpick[:, 0:1], 0.0).then_inc(cb_cleared, 1)
            tiles(1)

            def last(g, first):
                coefficients(NG + g, g)
                for b in range(GB):
                    c = g * GB + b
                    if not (first and b < 2):
                        dve.wait_ge(out_stored[b % 2], (c - b % 2) * 8)
                    if first and b == 0:
                        for h in range(2):
                            dve.wait_ge(y_sent[h], 8 * sum(TILES))
                    combine(1, NB + c, b, xn[:, b % 2, :]).then_inc(out_made, 1)

            last(0, True)
            with dve.Fori(1, NG) as g:
                last(g, False)

        @block.tensor
        def _(pe):
            pe.wait_ge(gnnw_loaded, 32)
            pe.wait_ge(consts_made, NCONST)
            pe.matmul(PM[:, 0:D], onesrow[:, :], brow[:, :], start=True, stop=True).then_inc(bias_spread, 1)
            pe.wait_ge(masks_made, 2)
            for k in range(KD):
                for m in range(KD):
                    ins = pe.transpose(Zq[:, k, m * P:(m + 1) * P], wg_nat[:, m, k * P:(k + 1) * P], ident[:, :])
            ins.then_inc(gnnw_transposed, 1)
            pe.wait_ge(bias_copied, 1)
            pe.wait_ge(small_loaded, 64)
            for l in range(2):
                n = EXPERTS[l] * FC
                pe.transpose(PM[:, 256 + 64 * l:256 + 64 * l + n], b1n[l][:, :], ident[0:n, 0:n]).then_inc(b1_transposed, 1)
            pe.wait_ge(gnnw_copied, 2)

            def front(r, h):
                pe.wait_ge(xn_made, r + 1)
                if some(r):
                    pe.wait_ge(xn_copied, r)
                for k in range(KD):
                    ins = pe.transpose(PX[:, k, :], xn[:, h, k * P:(k + 1) * P], ident[:, :])
                ins.then_inc(xn_transposed, 1)
                pe.wait_ge(xn_copied, r + 1)
                if some(r - 1):
                    pe.wait_ge(u_copied, r - 1)
                for k in range(KD):
                    ins = pe.matmul(Y[:, h, :], xrT[:, 2 * h + k, :], wgT[:, k, :], start=(k == 0), stop=(k == KD - 1))
                ins.then_inc(u_summed, 1)

            def back(r, h):
                pe.wait_ge(adj_scaled, r + 1)
                for q in range(4):
                    if some(r * 4 + q - 3):
                        pe.wait_ge(adj_lo, r * 4 + q - 3)
                    for o in range(4):
                        j = 4 * q + o
                        ins = pe.transpose(Zq[:, q, o * P:(o + 1) * P], stage[:, h, j * P:(j + 1) * P], ident[:, :])
                    ins.then_inc(adj_transposed, 1)

            front(0, 0)
            for r in range(2):
                front(r + 1, 1 - r)
                back(r, r)
            with pe.Fori(1, NB // 2 - 1) as i:
                for o in range(2):
                    front(i * 2 + (o + 1), 1 - o)
                    back(i * 2 + o, o)
            front(NB - 1, 1)
            back(NB - 2, 0)
            back(NB - 1, 1)

            def product(g, b):
                q = g * GB + b
                first = isinstance(q, int) and q == 0
                if some(q - 1):
                    pe.wait_ge(x1_made, q - 1)
                if first:
                    pe.wait_ge(u_copied, NB)
                    pe.wait_ge(adj_lo, 4 * NB)
                a = (NB - GB + b - GB * g) * ATB
                pe.nop(nofuse=True)
                for j in range(NB):
                    if first:
                        pe.wait_ge(v_lo, j + 1)
                    hi, lo = (R[:, at(a + (m * NB + j) * P, P)] for m in range(2))
                    pe.matmul(Y[:, b % 2, :], hi, v[:, j, 0, :], start=(j == 0), stop=False)
                    pe.matmul(Y[:, b % 2, :], hi, v[:, j, 1, :], start=False, stop=False)
                    ins = pe.matmul(Y[:, b % 2, :], lo, v[:, j, 0, :], start=False, stop=(j == NB - 1))
                ins.then_inc(graph_summed, 1)

            def group(l):
                def body(g, new, old, prep):
                    G = g + NG * l
                    if new and l == 1:
                        pe.wait_ge(coef_grouped, g + 1)
                        if some(g):
                            pe.wait_ge(coef_copied, g)
                        if isinstance(g, int) and g == 0:
                            pe.wait_ge(cb_loaded, 2 * GB * 16)
                        pe.transpose(p_cT, cgrp[:, :, :].rearrange("p b c -> p (b c)"), ident[:, :]).then_inc(coef_transposed, 1)
                        pe.wait_ge(coef_copied, g + 1)
                    for b in range(GB):
                        q = G * GB + b
                        if new and l == 0:
                            product(g, b)
                        if new and l == 1:
                            pe.wait_ge(xr_made, q - 1)
                            pe.matmul(Y[:, b % 2, :], cT[CW * b:CW * (b + 1), :], CB[CW * b:CW * (b + 1), :], start=True, stop=True).then_inc(corr_made, 1)
                        if b == 0 and old:
                            route_t_pe(pe, q - 1, GB - 1)
                            route_logits_pe(pe, l, G - 1, q - 2, GB - 2)
                            if not new:
                                route_logits_pe(pe, l, G - 1, q - 1, GB - 1)
                        if b == 1:
                            if new:
                                route_t_pe(pe, q - 1, 0)
                            if new and old:
                                route_logits_pe(pe, l, G - 1, q - 2, GB - 1)
                        if b >= 2 and new:
                            route_t_pe(pe, q - 1, b - 1)
                            route_logits_pe(pe, l, G, q - 2, b - 2)
                        if b == 2 and old:
                            route_pos_pe(pe, l, G - 1)
                return body

            def count(l):
                pe.wait_ge(totals_made, (NG + 1) * l + NG)
                pe.matmul(p_cnt[:, 0:EXPERTS[l]], ones16[:, :], tot[:, 0:EXPERTS[l]], start=True, stop=True).then_inc(counts_made, 1)

            in_groups(pe, group(0), 2, NG)
            count(0)

            def tile_transpose(l, t, h):
                n = T0[l] + t
                pe.wait_ge(tile_loaded[h], ring(n, h))
                if some(n):
                    pe.wait_ge(tile_copied, n)
                for a in range(2 * KD):
                    ins = pe.transpose(PT[:, a, 0, :], xtile[:, h, a * P:(a + 1) * P], ident16[:, :])
                ins.then_inc(tile_transposed, 1)

            def layer1(l, t, h):
                n = T0[l] + t
                w = pe.value_load(tab[0:1, 1, at(t, 1)], min_val=0, max_val=(NSLOT - 1) * WSLOT)
                pe.wait_ge(tile_copied, n + 1)
                if some(FC * (n - 1)):
                    pe.wait_ge(hid_made, FC * (n - 1))
                for c in range(FC):
                    for k in range(KD):
                        hi, lo = (R[:, at(w + (m * UNIT + k * F + c * P), P)] for m in range(2))
                        pe.matmul(Z[:, h, c, :], hi, xT[:, h, k, :], start=(k == 0), stop=False)
                        pe.matmul(Z[:, h, c, :], hi, xT[:, h, KD + k, :], start=False, stop=False)
                        ins = pe.matmul(Z[:, h, c, :], lo, xT[:, h, k, :], start=False, stop=(k == KD - 1))
                    if c % 4 == 3:
                        ins.then_inc(z_made, 1)

            def layer2(l, t, h):
                n = T0[l] + t
                w = pe.value_load(tab[0:1, 1, at(t, 1)], min_val=0, max_val=(NSLOT - 1) * WSLOT)
                pe.wait_ge(hid_lo_made, 2 * n + 2)
                if some(n - 1):
                    pe.wait_ge(y_scaled, n - 1)
                for c in range(FC):
                    hi, lo = (R[:, at(w + (2 * UNIT + c * 2 * D + m * D), D)] for m in range(2))
                    pe.matmul(Y[:, h, :], hid_hi[:, h, c, :], hi, start=(c == 0), stop=False)
                    pe.matmul(Y[:, h, :], hid_hi[:, h, c, :], lo, start=False, stop=False)
                    ins = pe.matmul(Y[:, h, :], hid_lo[:, h, c, :], hi, start=False, stop=(c == FC - 1))
                ins.then_inc(y_made, 1)

            def tiles(l):
                pe.wait_ge(table_made, l + 1)
                pe.wait_ge(w_lo, 2 * sum(EXPERTS[:l + 1]))
                if l == 0:
                    pe.wait_ge(x1_made, NB)
                else:
                    pe.wait_ge(xr_made, 2 * NB)
                tile_transpose(l, 0, 0)

                def step(t, h, turn):
                    if not (isinstance(t, int) and t == TILES[l] - 1):
                        tile_transpose(l, t + 1, 1 - h)
                    layer1(l, t, h)
                    if not (isinstance(t, int) and t == 0):
                        layer2(l, t - 1, 1 - h)

                in_tiles(pe, l, step)
                layer2(l, TILES[l] - 1, (TILES[l] - 1) % 2)

            tiles(0)
            in_groups(pe, group(1), 1, NG - 1)
            count(1)
            tiles(1)

            def last(g, first):
                pe.wait_ge(coef_grouped, g + NG + 1)
                pe.wait_ge(coef_copied, g + NG)
                if first:
                    pe.wait_ge(cb_loaded, 4 * GB * 16)
                    pe.wait_ge(y_scaled, sum(TILES))
                pe.transpose(p_cT, cgrp[:, :, :].rearrange("p b c -> p (b c)"), ident[:, :]).then_inc(coef_transposed, 1)
                pe.wait_ge(coef_copied, g + NG + 1)
                for b in range(GB):
                    c = g * GB + b
                    if not (first and b < 2):
                        pe.wait_ge(out_made, c - 1)
                    pe.matmul(Y[:, b % 2, :], cT[CW * b:CW * (b + 1), :], CB[CW * b:CW * (b + 1), :], start=True, stop=True).then_inc(corr_made, 1)

            last(0, True)
            with pe.Fori(1, NG) as g:
                last(g, False)


_INS = ['x', 'adj', 'L0_gnn_W', 'L0_gnn_b', 'L0_ffn_Wr0', 'L0_ffn_W1_0', 'L0_ffn_b1_0', 'L0_ffn_W2_0', 'L0_ffn_b2_0',
        'L0_ffn_Wr1', 'L0_ffn_W1_1', 'L0_ffn_b1_1', 'L0_ffn_W2_1', 'L0_ffn_b2_1']
_OUTS = [((2048, 256), 'float32')]


def kernel(**inputs):
    import numpy as _np
    import concourse.bacc as _bacc
    from concourse import mybir as _mybir
    from concourse.bass_utils import run_bass_kernel_spmd as _run

    nc = _bacc.Bacc("TRN2", target_bir_lowering=False, num_devices=1, dynamic_dma_scratch_size=8192)
    arrays, args = {}, []
    for name in _INS:
        a = _np.ascontiguousarray(inputs[name])
        arrays[f"in_{name}_dram"] = a
        args.append(nc.dram_tensor(f"in_{name}_dram", a.shape, _mybir.dt.from_np(a.dtype), kind="ExternalInput").ap())
    for i, (shape, dtype) in enumerate(_OUTS):
        dt = _mybir.dt.from_np(_np.dtype(dtype))
        args.append(nc.dram_tensor(f"out_{i}_dram", shape, dt, kind="ExternalOutput").ap())
    bass_gnn_moe(nc, *args)
    r = _run(nc, [arrays], core_ids=[0])
    return r.results[0]["out_0_dram"]
```

```python
from contextlib import ExitStack

import concourse.bass as bass
from concourse import mybir

F32, F16, I32 = mybir.dt.float32, mybir.dt.float16, mybir.dt.int32
ALU = mybir.AluOpType
ACT = mybir.ActivationFunctionType
AX = mybir.AxisListType
RED = bass.bass_isa.ReduceOp

P = 128
EXPONENT = 0x7F800000


def bass_gnn_moe(nc, x, adj, gnn_W, gnn_b, Wr0, W1_0, b1_0, W2_0, b2_0, Wr1, W1_1, b1_1, W2_1, b2_1, out):
    T, D = x.shape
    NB = T // P
    GB = 4
    NG = NB // GB
    KD = D // P
    F = W1_0.shape[2]
    FC = F // P
    EXPERTS = (W1_0.shape[0], W1_1.shape[0])
    EM = max(EXPERTS)
    S = 2
    TP = S * P
    ARENA = T + TP
    TILES = [2 * T // TP + e for e in EXPERTS]
    JUNK = [e * ARENA for e in EXPERTS]
    RW = 2 * D + 2
    IDC = 2 * D
    PADROW = 2 * T
    YROWS = 2 * T + (EM + 2) * TP
    CW = 32
    WSLOT = 2 * (KD * F + FC * D)
    UNIT = KD * F
    NSLOT = 9
    ATB = 2 * NB * P
    FIRSTSLOT = (NSLOT - EXPERTS[0], 0)
    EARLY = EM - 3
    EPS_LN, EPS_DEG = 1e-5, 1e-8
    Wr, W1, b1, W2, b2 = (Wr0, Wr1), (W1_0, W1_1), (b1_0, b1_1), (W2_0, W2_1), (b2_0, b2_1)
    W1v = [w.rearrange("e (k p) f -> e p k f", p=P) for w in W1]
    W2v = [w.rearrange("e (c p) d -> e p c d", p=P) for w in W2]

    ctx = ExitStack()
    with ctx:
        def sb(name, shape, dt=F32):
            return ctx.enter_context(nc.sbuf_tensor(name, shape, dt))

        def ps(name, shape, dt=F32):
            return ctx.enter_context(nc.psum_tensor(name, shape, dt))

        def sem(name):
            return ctx.enter_context(nc.semaphore(name))

        def dram(name, shape, dt):
            return nc.dram_tensor(name, shape, dt).ap()

        arena = [dram(f"arena{l}", (EXPERTS[l] * ARENA + 2 * TP, RW), F16) for l in range(2)]
        NCONST = 16
        ys = [dram(f"ys{l}", (YROWS, D), F32) for l in range(2)]
        x1_dram = dram("x1_dram", (T, D), F32)

        R = sb("R", [P, NSLOT * WSLOT], F16)
        stage = sb("stage", [P, 2, UNIT])
        U = sb("U", [P, NB * 2 * D], F16)
        adj_in = [stage[:, i, :] for i in range(2)] + [U[:, 2 * i * UNIT:2 * (i + 1) * UNIT].bitcast(F32) for i in range(2)]
        v = U[:, :].rearrange("p (j h d) -> p j h d", j=NB, h=2)
        hid = U[:, 0:2 * FC * TP].bitcast(F32).rearrange("p (c t) -> p c t", c=FC)
        hid_hi = U[:, 2 * FC * TP:4 * FC * TP].rearrange("p (s c t) -> p s c t", s=2, c=FC)
        yab = U[:, 0:GB * 4 * D].bitcast(F32).rearrange("p (b r d) -> p b r d", b=GB, r=2)
        u_all = R[:, (NSLOT - 1) * WSLOT:NSLOT * WSLOT].bitcast(F32).rearrange("p (j d) -> p j d", j=NB)
        rows = sb("rows", [P, GB, 2, RW], F16)
        hid_lo = rows[:, :, :, :].rearrange("p b r w -> p (b r w)")[:, 0:2 * FC * TP].rearrange("p (s c t) -> p s c t", s=2, c=FC)
        xr = sb("xr", [P, GB, D])
        wg_nat = xr[:, 0:KD, :]
        wgT = xr[:, KD:2 * KD, :]
        xT = sb("xT", [P, 2, 2 * KD, TP], F16)
        xrT = xT[:, 0, :, :].rearrange("p a t -> p (a t)").bitcast(F32).rearrange("p (k t) -> p k t", k=KD * 2)
        yout = sb("yout", [P, 2, S, D])
        xin, xn = yout[:, 0, :, :], yout[:, 1, :, :]
        xtile = sb("xtile", [P, 2, S, RW], F16)
        xb = xT[:, 1, :, :].rearrange("p a t -> p (a t)").bitcast(F32).rearrange("p (b d) -> p b d", b=2)
        bB = sb("bB", [P, D])
        zeros = sb("zeros", [P, 2 * D], F16)
        ident = sb("ident", [P, P])
        ident16 = sb("ident16", [P, P], F16)
        before = sb("before", [P, P], F16)
        ones16 = sb("ones16", [P, P], F16)
        onesrow = sb("onesrow", [1, P])
        brow = sb("brow", [1, D])
        diff = xb[:, 0, 0:P]
        tileno = sb("tileno", [1, max(TILES)])
        junkrow = sb("junkrow", [1, 2, max(TILES)])
        ids = sb("ids", [P, NB, 2], I32)
        padids = sb("padids", [P, EM + 2, S], I32)
        base_e = sb("base_e", [P, EM])
        rank_e = sb("rank_e", [P, EM])
        half = sb("half", [P, 4])
        wr = [sb(f"wr{l}", [P, KD, EXPERTS[l]]) for l in range(2)]
        b1n = [sb(f"b1n{l}", [EXPERTS[l] * FC, P]) for l in range(2)]
        b1T = [sb(f"b1T{l}", [P, EXPERTS[l], FC]) for l in range(2)]
        prm = [sb(f"prm{l}", [P, EXPERTS[l], FC + 2]) for l in range(2)]
        wstat = sb("wstat", [P, 2])
        wnorm = sb("wnorm", [P, 2])
        wtot = sb("wtot", [P, 2])
        wpow = sb("wpow", [P, 2, 12])
        winv = sb("winv", [P, 2, 12])
        wscl = sb("wscl", [P, 2, 12])
        lv = [sb(f"lv{l}", [P, 16]) for l in range(2)]
        lve = [sb(f"lve{l}", [P, 4, EXPERTS[l]]) for l in range(2)]
        CB = sb("CB", [P, D])
        coef = sb("coef", [P, NB, CW])
        cgrp = sb("cgrp", [P, GB, CW])
        cT = sb("cT", [P, P])
        p12 = sb("p12", [P, NB, 2])
        stat = sb("stat", [P, 2, 6])
        mv = sb("mv", [P, 2, 2])
        rstd = sb("rstd", [P, 2])
        deg = sb("deg", [P, NB])
        dis = sb("dis", [P, NB])
        pdeg = sb("pdeg", [P, NB])
        rdeg = sb("rdeg", [P, 2])
        vscale = sb("vscale", [P, NB])
        gscale = sb("gscale", [P, NB])
        gst = sb("gst", [P, 12])
        degE = sb("degE", [P, NB])
        vare = sb("vare", [P, 2])
        rt = sb("rt", [P, 12, GB, EM])
        rs = sb("rs", [P, 8, GB])
        disp = sb("disp", [P, GB, EM], F16)
        tot = sb("tot", [P, EM], F16)
        cpick = sb("cpick", [P, EM])
        slot = sb("slot", [P, GB, 2], I32)
        cnt = sb("cnt", [1, 8, EM])
        cnti = sb("cnti", [1, 2, EM], I32)
        steps = U[0:1, 0:4 * EM * max(TILES)].bitcast(F32).rearrange("p (i e t) -> p i e t", i=2, e=EM)
        tabf = sb("tabf", [1, 2, max(TILES)])
        tab = sb("tab", [1, 3, max(TILES)], I32)
        tprm = sb("tprm", [P, 2, FC + 2])
        tgam = sb("tgam", [P, max(TILES)])
        tids = sb("tids", [P, max(TILES), S], I32)
        yid = sb("yid", [P, 2, S], I32)
        ymax = sb("ymax", [P, 2])
        yrun = sb("yrun", [P, 2])

        Zq = ps("Z", [P, 4, 4 * P])
        Z = Zq[:, :, :].rearrange("p q (o t) -> p (q o) t", o=2)
        p_log = Zq[:, 0, 0:GB * EM].rearrange("p (b e) -> p b e", b=GB)
        p_pos = Zq[:, 1, 0:GB * EM].rearrange("p (b e) -> p b e", b=GB)
        p_cnt = Zq[:, 2, 0:EM]
        p_cT = Zq[:, 3, 0:P]
        Y2 = ps("Y", [P, 2, 4 * P])
        Y = Y2[:, :, 0:D]
        PT = ps("PT", [P, 2 * KD, 2, P], F16)
        PM = PT[:, :, :, :].rearrange("p a b t -> p (a b t)").bitcast(F32)
        PX = ps("PX", [P, 2 * KD, P])

        consts_made = sem("consts_made")
        masks_made = sem("masks_made")
        gnnw_loaded = sem("gnnw_loaded")
        gnnw_squared = sem("gnnw_squared")
        gnnw_transposed = sem("gnnw_transposed")
        gnnw_copied = sem("gnnw_copied")
        bias_spread = sem("bias_spread")
        bias_copied = sem("bias_copied")
        small_loaded = sem("small_loaded")
        b1_transposed = sem("b1_transposed")
        b1_copied = sem("b1_copied")
        var_made = sem("var_made")
        rstd_made = sem("rstd_made")
        xn_made = sem("xn_made")
        xn_transposed = sem("xn_transposed")
        xn_copied = sem("xn_copied")
        u_summed = sem("u_summed")
        u_copied = sem("u_copied")
        deg_made = sem("deg_made")
        deg_rounded = sem("deg_rounded")
        dis_made = sem("dis_made")
        adj_scaled = sem("adj_scaled")
        adj_transposed = sem("adj_transposed")
        adj_hi = sem("adj_hi")
        adj_lo = sem("adj_lo")
        v_bounds = sem("v_bounds")
        v_bounds_max = sem("v_bounds_max")
        v_bound_root = sem("v_bound_root")
        v_scales = sem("v_scales")
        v_hi = sem("v_hi")
        v_lo = sem("v_lo")
        graph_summed = sem("graph_summed")
        bias_added = sem("bias_added")
        x1_made = sem("x1_made")
        xr_made = sem("xr_made")
        xr_transposed = sem("xr_transposed")
        xr_copied = sem("xr_copied")
        logits_made = sem("logits_made")
        logits_shifted = sem("logits_shifted")
        exps_made = sem("exps_made")
        picks_made = sem("picks_made")
        places_counted = sem("places_counted")
        slots_made = sem("slots_made")
        rows_hi = sem("rows_hi")
        rows_lo = sem("rows_lo")
        rows_id = sem("rows_id")
        totals_made = sem("totals_made")
        counts_made = sem("counts_made")
        table_made = sem("table_made")
        pads_stored = sem("pads_stored")
        junk_stored = sem("junk_stored")
        w_loaded = sem("w_loaded")
        w_squared = sem("w_squared")
        w_summed = sem("w_summed")
        w_normed = sem("w_normed")
        w_scaled = sem("w_scaled")
        w_hi = sem("w_hi")
        w_lo = sem("w_lo")
        level_stats = sem("level_stats")
        level_maxima = sem("level_maxima")
        level_scales = sem("level_scales")
        tile_transposed = sem("tile_transposed")
        tile_copied = sem("tile_copied")
        tile_params = sem("tile_params")
        z_made = sem("z_made")
        hid_made = sem("hid_made")
        hid_hi_made = sem("hid_hi_made")
        hid_lo_made = sem("hid_lo_made")
        y_made = sem("y_made")
        y_scaled = sem("y_scaled")
        y_ids = sem("y_ids")
        cb_cleared = sem("cb_cleared")
        cb_loaded = sem("cb_loaded")
        coef_grouped = sem("coef_grouped")
        coef_transposed = sem("coef_transposed")
        coef_copied = sem("coef_copied")
        corr_made = sem("corr_made")
        out_made = sem("out_made")
        x_loaded = [sem(f"x_loaded{h}") for h in range(2)]
        adj_loaded = [sem(f"adj_loaded{h}") for h in range(4)]
        x1_stored = [sem(f"x1_stored{h}") for h in range(2)]
        tile_loaded = [sem(f"tile_loaded{h}") for h in range(2)]
        y_sent = [sem(f"y_sent{h}") for h in range(2)]
        out_stored = [sem(f"out_stored{h}") for h in range(2)]
        rows_sent = [sem(f"rows_sent{h}") for h in range(GB)]
        yab_loaded = [sem(f"yab_loaded{h}") for h in range(GB)]


        def some(n):
            return not isinstance(n, int) or n > 0

        def ring(n, h, parts=2):
            return (n - h) * (16 // parts) + 16

        def at(start, n):
            return bass.ds(start, n) if not isinstance(start, int) else slice(start, start + n)

        def w_load(sp, n, l, e, s):
            if some(2 * n):
                sp.wait_ge(w_lo, 2 * n)
            if some(2 * n):
                sp.wait_ge(w_hi, 2 * n)
            sp.nop(nofuse=True)
            sp.dma_start(stage[:, 0, :].rearrange("p (k f) -> p k f", k=KD), W1v[l][at(e, 1)].rearrange("e p k f -> (e p) k f")).then_inc(w_loaded, 16)
            sp.dma_start(stage[:, 1, :].rearrange("p (c d) -> p c d", c=FC), W2v[l][at(e, 1)].rearrange("e p c d -> (e p) c d")).then_inc(w_loaded, 16)

        def w_square(act, n, l, e, s, place_free=0):
            act.wait_ge(w_loaded, 32 * n + 32)
            act.wait_ge(v_lo, NB)
            if some(GB * n if l == 0 else NB):
                act.wait_ge(graph_summed, GB * n if l == 0 else NB)
            if l == 1:
                if some(place_free):
                    act.wait_ge(y_made, place_free)
            for m in range(2):
                act.activation(R[:, at(s * WSLOT + m * 2 * UNIT, UNIT)], stage[:, m, :], ACT.Square,
                               accum_out=wstat[:, m:m + 1]).then_inc(w_squared, 1)

        def w_norm(pool, n, l, e, s):
            pool.wait_ge(w_squared, 2 * n + 2)
            for m in range(2):
                pool.nop(nofuse=True)
                pool.partition_all_reduce(wtot[:, m:m + 1], wstat[:, m:m + 1], P, RED.add).then_inc(w_summed, 1)
            for m in range(2):
                pool.wait_ge(w_summed, 2 * n + 1 + m)
                pool.tensor_tensor(wnorm[:, m:m + 1], wtot[:, m:m + 1], half[:, 1:2], ALU.pow).then_inc(w_normed, 1)

        def w_scale(dve, n, l, e, s):
            dve.wait_ge(w_normed, 2 * n + 2)
            dve.tensor_scalar(wpow[:, :, at(n, 1)], wnorm[:, :].unsqueeze(2), 1e-15, None, ALU.max)
            dve.drain()
            dve.tensor_scalar(wpow[:, :, at(n, 1)].bitcast(I32), wpow[:, :, at(n, 1)].bitcast(I32), EXPONENT, None, ALU.bitwise_and)
            dve.drain()
            dve.reciprocal(winv[:, :, at(n, 1)], wpow[:, :, at(n, 1)])
            dve.drain()
            dve.tensor_scalar(wscl[:, :, at(n, 1)], winv[:, :, at(n, 1)], 8192.0, None, ALU.mult).then_inc(w_scaled, 1)

        def w_parts(s):
            b = s * WSLOT
            w1 = [R[:, at(b + h * UNIT, UNIT)] for h in range(2)]
            w2 = R[:, at(b + 2 * UNIT, 2 * UNIT)].rearrange("p (c h d) -> p h c d", h=2, d=D)
            return [(w1[0], w1[1], stage[:, 0, :]),
                    (w2[:, 0], w2[:, 1], stage[:, 1, :].rearrange("p (c d) -> p c d", c=FC))]

        def w_high(act, n, l, e, s):
            act.wait_ge(w_scaled, n + 1)
            act.wait_ge(w_squared, 2 * n + 2)
            for m, (hi, lo, src) in enumerate(w_parts(s)):
                act.activation(hi, src, ACT.Copy, scale=wscl[:, m, at(n, 1)]).then_inc(w_hi, 1)

        def w_low(dve, n, l, e, s):
            for m, (hi, lo, src) in enumerate(w_parts(s)):
                dve.wait_ge(w_hi, 2 * n + 1 + m)
                dve.nop(nofuse=True)
                dve.scalar_tensor_tensor(lo, src, wscl[:, m, at(n, 1)], hi, ALU.mult, ALU.subtract).then_inc(w_lo, 1)

        def level_scales_dve(dve, l):
            E, n0 = EXPERTS[l], 0 if l == 0 else EXPERTS[0]
            dve.wait_ge(b1_copied, l + 1)
            dve.tensor_reduce(lv[l][:, 0:1], b1T[l][:, :, :].rearrange("p e c -> p (e c)"), AX.X, ALU.max, apply_absolute_value=True)
            if l == 0:
                dve.memset(lv[l][:, 1:3], 0.0).then_inc(level_stats, 1)
            else:
                dve.tensor_reduce(lv[l][:, 1:2], CB[:, :], AX.X, ALU.max, apply_absolute_value=True)
                dve.tensor_copy(lv[l][:, 2:3], yrun[:, 0:1]).then_inc(level_stats, 1)
            dve.drain()
            dve.memset(lv[l][:, 15:16], 0.0).then_inc(level_stats, 1)
            dve.wait_ge(level_maxima, 3 * l + 3)
            X, M1, PW = lv[l], lve[l], wpow
            if l == 0:
                dve.memset(X[:, 6:7], 1.0)
                dve.drain()
            else:
                dve.tensor_tensor(X[:, 6:7], X[:, 4:5], X[:, 5:6], ALU.add)
                dve.drain()
                dve.tensor_scalar(X[:, 6:7], X[:, 6:7], 1e-15, None, ALU.max)
                dve.drain()
            dve.tensor_scalar(X[:, 7:8].bitcast(I32), X[:, 6:7].bitcast(I32), EXPONENT, None, ALU.bitwise_and)
            dve.drain()
            dve.reciprocal(X[:, 8:9], X[:, 7:8])
            dve.drain()
            dve.tensor_scalar(X[:, 9:10], X[:, 8:9], 1024.0 if l == 0 else 8192.0, None, ALU.mult).then_inc(level_scales, 1)
            dve.tensor_scalar(X[:, 10:11], X[:, 7:8], 1 / 1024.0 if l == 0 else 1 / 8192.0, None, ALU.mult)
            dve.tensor_scalar(X[:, 11:12], X[:, 6:7], 32.0, None, ALU.mult)
            dve.drain()

        def level_params_dve(dve, l):
            E, n0 = EXPERTS[l], 0 if l == 0 else EXPERTS[0]
            X, M1 = lv[l], lve[l]
            order = [(e, (NG - 1 - e) if l == 0 else EXPERTS[0] + e) for e in range(E)]
            for e, n in order:
                dve.scalar_tensor_tensor(M1[:, 0, e:e + 1], wpow[:, 0, n:n + 1], X[:, 11:12], X[:, 3:4], ALU.mult, ALU.add)
            dve.drain()
            dve.tensor_scalar(M1[:, 1, :].bitcast(I32), M1[:, 0, :].bitcast(I32), EXPONENT, None, ALU.bitwise_and)
            dve.drain()
            dve.reciprocal(M1[:, 2, :], M1[:, 1, :])
            dve.drain()
            for e, n in order:
                dve.scalar_tensor_tensor(M1[:, 3, e:e + 1], wpow[:, 0, n:n + 1], 2.0, M1[:, 2, e:e + 1], ALU.mult, ALU.mult)
                dve.scalar_tensor_tensor(prm[l][:, e, 1:2], wpow[:, 1, n:n + 1], 2.0 ** -27, M1[:, 1, e:e + 1], ALU.mult, ALU.mult)
                dve.tensor_scalar(prm[l][:, e, 2:], b1T[l][:, e, :], M1[:, 2, e:e + 1], 16384.0, ALU.mult, ALU.mult)
            dve.drain()
            dve.tensor_scalar(prm[l][:, :, 0], M1[:, 3, :], X[:, 10:11], None, ALU.mult).then_inc(level_scales, 1)

        def level_scales_pool(pool, l):
            pool.wait_ge(level_stats, 2 * l + 2)
            for i in range(3):
                pool.partition_all_reduce(lv[l][:, 3 + i:4 + i], lv[l][:, i:i + 1], P, RED.max).then_inc(level_maxima, 1)


        def blk_of(l, g, b):
            return NB - GB - GB * g + b if l == 0 else GB * g - NB + b

        def route_t_pe(pe, q, b):
            pe.wait_ge(xr_made, q + 1)
            if some(q):
                pe.wait_ge(xr_copied, q)
            pe.wait_ge(xn_copied, NB)
            for k in range(KD):
                ins = pe.transpose(PX[:, k, :], xr[:, b, k * P:(k + 1) * P], ident[:, :])
            ins.then_inc(xr_transposed, 1)

        def route_copy_act(act, q, b):
            act.wait_ge(xr_transposed, q + 1)
            if some(q - 1):
                act.wait_ge(logits_made, q - 1)
            act.wait_ge(u_summed, NB)
            act.activation(xrT[:, 2 * (b % 2):2 * (b % 2) + 2, :], PX[:, 0:KD, :], ACT.Copy).then_inc(xr_copied, 1)

        def route_logits_pe(pe, l, g, q, b):
            pe.wait_ge(xr_copied, q + 1)
            if some(g):
                pe.wait_ge(logits_shifted, g)
            for k in range(KD):
                ins = pe.matmul(p_log[:, b, 0:EXPERTS[l]], xrT[:, 2 * (b % 2) + k, :], wr[l][:, k, :],
                                start=(k == 0), stop=(k == KD - 1))
            ins.then_inc(logits_made, 1)

        def route_pos_pe(pe, l, g):
            E = EXPERTS[l]
            pe.wait_ge(picks_made, g + 1)
            if some(g + l):
                pe.wait_ge(totals_made, g + l)
            if some(2 * g):
                pe.wait_ge(slots_made, 2 * g)
            for b in range(GB):
                pe.matmul(p_pos[:, b, 0:E], ones16[:, :], tot[:, 0:E], start=True, stop=False)
                for b2 in range(b):
                    pe.matmul(p_pos[:, b, 0:E], ones16[:, :], disp[:, b2, 0:E], start=False, stop=False)
                ins = pe.matmul(p_pos[:, b, 0:E], before[:, :], disp[:, b, 0:E], start=False, stop=True)
            ins.then_inc(places_counted, 1)

        def route_exp_act(act, l, g):
            act.wait_ge(logits_shifted, g + 1)
            act.activation(rt[:, 1, :, 0:EXPERTS[l]], rt[:, 0, :, 0:EXPERTS[l]], ACT.Exp).then_inc(exps_made, 1)

        def route_picks_dve(dve, l, g, blk):
            E = EXPERTS[l]
            r = [rt[:, i, :, 0:E] for i in range(12)]
            s = [rs[:, i, :] for i in range(8)]

            def wide(x):
                return x.unsqueeze(2).broadcast_to([P, GB, E])

            rank = rank_e[:, 0:E].unsqueeze(1).broadcast_to([P, GB, E])
            dve.wait_ge(logits_made, GB * g + GB)
            dve.tensor_reduce(s[0], p_log[:, :, 0:E], AX.X, ALU.max)
            dve.drain()
            dve.tensor_tensor(r[0], p_log[:, :, 0:E], wide(s[0]), ALU.subtract).then_inc(logits_shifted, 1)
            dve.wait_ge(exps_made, g + 1)
            dve.tensor_reduce(s[1], r[1], AX.X, ALU.add)
            dve.drain()
            dve.reciprocal(s[2], s[1])
            dve.drain()
            dve.tensor_tensor(r[2], r[1], wide(s[2]), ALU.mult)
            dve.drain()
            left, masks = r[2], []
            for i, (eq, best, pick) in enumerate(((3, 4, 5), (6, 7, 8))):
                dve.tensor_reduce(s[3 + i], left, AX.X, ALU.max)
                dve.drain()
                dve.tensor_tensor(r[eq], left, wide(s[3 + i]), ALU.is_equal)
                dve.drain()
                dve.tensor_tensor(r[best], r[eq], rank, ALU.mult)
                dve.drain()
                dve.tensor_reduce(s[5 + i], r[best], AX.X, ALU.max)
                dve.drain()
                dve.tensor_tensor(r[pick], r[best], wide(s[5 + i]), ALU.is_equal)
                dve.drain()
                masks.append(r[pick])
                if i == 0:
                    dve.scalar_tensor_tensor(r[9], r[pick], -2.0, r[2], ALU.mult, ALU.add)
                    dve.drain()
                    left = r[9]
            if some(g):
                dve.wait_ge(places_counted, g)
            dve.tensor_tensor(disp[:, :, 0:E], masks[0], masks[1], ALU.add).then_inc(picks_made, 1)
            dve.tensor_tensor(r[10], masks[0], masks[1], ALU.add)
            for i in range(2):
                dve.tensor_copy(p12[:, at(blk, GB), i], s[3 + i])
            dve.tensor_copy(coef[:, at(blk, GB), E:2 * E], r[2])
            dve.drain()
            dve.tensor_tensor(r[11], r[10], r[2], ALU.mult)
            dve.drain()
            dve.tensor_tensor(coef[:, at(blk, GB), 0:E], r[2], r[11], ALU.subtract)

        def route_slots_dve(dve, l, g):
            E = EXPERTS[l]
            base = base_e[:, 0:E].unsqueeze(1).broadcast_to([P, GB, E])
            dve.wait_ge(places_counted, g + 1)
            dve.tensor_tensor(rt[:, 0, :, 0:E], p_pos[:, :, 0:E], base, ALU.add)
            dve.tensor_reduce(cpick[:, 0:E], disp[:, :, 0:E].rearrange("p b e -> p e b"), AX.X, ALU.add)
            dve.drain()
            dve.tensor_tensor(rt[:, 3, :, 0:E], rt[:, 0, :, 0:E], rt[:, 5, :, 0:E], ALU.mult)
            dve.tensor_tensor(rt[:, 4, :, 0:E], rt[:, 0, :, 0:E], rt[:, 8, :, 0:E], ALU.mult)
            dve.tensor_tensor(tot[:, 0:E], tot[:, 0:E], cpick[:, 0:E], ALU.add).then_inc(totals_made, 1)
            dve.drain()
            for b in range(GB):
                if some(2 * 16 * g):
                    dve.wait_ge(rows_sent[b], 2 * 16 * g)
            with nc.allow_low_precision(reason="row numbers, whole and below 2^24"):
                for i in range(2):
                    dve.tensor_reduce(slot[:, :, i], rt[:, 3 + i, :, 0:E], AX.X, ALU.add).then_inc(slots_made, 1)

        def pack_act(act, l, q, b):
            act.wait_ge(xr_made, q + 1)
            if some((q - b) * 8):
                act.wait_ge(rows_sent[b], (q - b) * 8)
            act.wait_ge(level_scales, 2 * l + 1)
            act.activation(rows[:, b, :, 0:D], xr[:, b, :].unsqueeze(1).broadcast_to([P, 2, D]), ACT.Copy,
                           scale=lv[l][:, 9:10]).then_inc(rows_hi, 1)

        def pack_dve(dve, l, q, b, blk):
            dve.wait_ge(rows_hi, q + 1)
            dve.scalar_tensor_tensor(rows[:, b, :, D:2 * D], xr[:, b, :].unsqueeze(1).broadcast_to([P, 2, D]),
                                     lv[l][:, 9:10], rows[:, b, :, 0:D], ALU.mult, ALU.subtract).then_inc(rows_lo, 1)
            dve.tensor_copy(rows[:, b, :, IDC:IDC + 2].bitcast(I32).rearrange("p r a -> p (r a)"),
                            ids[:, at(blk, 1), :].rearrange("p a r -> p (a r)")).then_inc(rows_id, 1)

        def scatter_pool(pool, l, g, q, b):
            pool.wait_ge(slots_made, 2 * g + 2)
            pool.wait_ge(rows_lo, q + 1)
            pool.wait_ge(rows_id, q + 1)
            for i in range(2):
                pool.nop(nofuse=True)
                pool.indirect_dma_start(arena[l], bass.IndirectOffsetOnAxis(ap=slot[:, b, i:i + 1], axis=0),
                                        rows[:, b, i, :], None).then_inc(rows_sent[b], 16)

        def table_dve(dve, l):
            E, NT = EXPERTS[l], TILES[l]
            c = [cnt[:, i, 0:E] for i in range(8)]
            tn = tileno[:, 0:NT]
            dve.wait_ge(counts_made, l + 1)
            dve.tensor_copy(c[0], p_cnt[0:1, 0:E])
            dve.memset(c[4], 1.0)
            dve.drain()
            dve.tensor_copy(cnti[:, 0, 0:E], c[0])
            dve.tensor_tensor(cnti[:, 1, 0:E], c[0], base_e[0:1, 0:E], ALU.add)
            dve.drain()
            dve.tensor_scalar(cnti[:, 0, 0:E], cnti[:, 0, 0:E], TP.bit_length() - 1, None, ALU.logical_shift_right)
            dve.drain()
            dve.tensor_copy(c[1], cnti[:, 0, 0:E])
            dve.drain()
            dve.tensor_scalar(c[1], c[1], 1.0, None, ALU.add)
            dve.drain()
            dve.tensor_tensor_scan(c[2], c[4], c[1], 0.0, ALU.mult, ALU.add)
            dve.tensor_scalar(c[3], c[1], -float(TP), float(ARENA), ALU.mult, ALU.add)
            dve.drain()
            dve.memset(c[3][:, E - 1:E], float(1 << 17))
            dve.memset(steps[:, 1, E - 1:E, 0:NT], 0.0)
            dve.drain()
            for e in range(E):
                dve.tensor_scalar(steps[:, 0, e, 0:NT], tn, c[2][:, e:e + 1], c[3][:, e:e + 1], ALU.is_ge, ALU.mult)
                if e < E - 1:
                    dve.tensor_scalar(steps[:, 1, e, 0:NT], tn, c[2][:, e:e + 1], None, ALU.is_ge)
            dve.drain()
            for i in range(2):
                dve.tensor_reduce(tabf[:, i, 0:NT], steps[:, i, 0:E, 0:NT].rearrange("p e t -> p t e"), AX.X, ALU.add)
            dve.drain()
            dve.scalar_tensor_tensor(tabf[:, 0, 0:NT], tn, float(TP), tabf[:, 0, 0:NT], ALU.mult, ALU.add)
            dve.drain()
            dve.tensor_tensor(tab[:, 0, 0:NT], tabf[:, 0, 0:NT], junkrow[:, l, 0:NT], ALU.min)
            dve.tensor_scalar(tab[:, 1, 0:NT], tabf[:, 1, 0:NT], float(WSLOT), float(FIRSTSLOT[l] * WSLOT), ALU.mult, ALU.add)
            dve.tensor_copy(tab[:, 2, 0:NT], tabf[:, 1, 0:NT])
            dve.drain()
            dve.memset(cnt[:, 5, 0:1], 0.0).then_inc(table_made, 1)

        def pads_sp(sp, l):
            sp.wait_ge(table_made, l + 1)
            sp.wait_ge(consts_made, NCONST)
            for e in range(EXPERTS[l]):
                row = sp.value_load(cnti[0:1, 1, e:e + 1], min_val=e * ARENA, max_val=e * ARENA + T)
                pads = arena[l][at(row, TP), :].rearrange("(p s) w -> p s w", s=S)
                sp.dma_start(pads[:, :, 0:2 * D], zeros[:, :].unsqueeze(1).broadcast_to([P, S, 2 * D])).then_inc(pads_stored, 16)
                sp.dma_start(pads[:, :, IDC:IDC + 2], padids[:, e, :].bitcast(F16).rearrange("p (s a) -> p s a", s=S)).then_inc(pads_stored, 16)

        T0 = (0, TILES[0])

        def tile_load(sp, l, t, h):
            n = T0[l] + t
            if isinstance(t, int) and t == 0:
                for b in range(GB):
                    sp.wait_ge(rows_sent[b], 2 * 16 * NG * (l + 1))
                sp.wait_ge(pads_stored, 32 * sum(EXPERTS[:l + 1]))
                sp.wait_ge(junk_stored, 128)
            src = sp.value_load(tab[0:1, 0, at(t, 1)], min_val=0, max_val=JUNK[l] + TP)
            if some(n - 1):
                sp.wait_ge(tile_transposed, n - 1)
            if some(3 * (n - 1)):
                sp.nop(nofuse=True)
                sp.wait_ge(tile_params, 3 * (n - 1))
            sp.dma_start(xtile[:, h, :, :], arena[l][at(src, TP), :].rearrange("(p s) w -> p s w", s=S)).then_inc(tile_loaded[h], 16)


        def turn_gnn(g):
            return g, 0, EXPERTS[0] - 1 - g, NSLOT - 1 - g

        def turn_early(j):
            return EXPERTS[0] + j, 1, j, j

        def turn_late(g):
            return EXPERTS[0] + EARLY + g, 1, EARLY + g, EARLY + g

        def in_groups(eng, body, peeled, count):
            for g in range(peeled):
                body(g, True, g > 0, True)
            with eng.Fori(peeled, count) as g:
                body(g, True, True, True)
            for g in range(count, NG):
                body(g, True, True, False)
            body(NG, False, True, False)

        def inside(r):
            return not isinstance(r, int) or 0 <= r < NB

        def in_blocks(eng, step):
            for r in range(-2, 4):
                step(r, r % 4)
            with eng.Fori(1, NB // 4 - 1) as i:
                for o in range(4):
                    step(i * 4 + o, o)
            for r in range(NB - 4, NB):
                step(r, r % 4)

        def in_tiles(eng, l, step):
            NT = TILES[l]
            first = 2
            for t in range(first):
                step(t, t % 2, None)
            mid = first + 2 * EARLY if l == 0 else first
            if l == 0:
                with eng.Fori(0, EARLY) as j:
                    for o in range(2):
                        step(j * 2 + (first + o), o, (j, o))
            with eng.Fori(mid // 2, NT // 2 - 1) as i:
                for o in range(2):
                    step(i * 2 + o, o, None)
            for t in range(NT - 2, NT):
                step(t, t % 2, None)

        block = ctx.enter_context(nc.Block())

        @block.sync
        def _(sp):
            sp.dma_start(wg_nat, gnn_W.rearrange("(k p) d -> p k d", p=P)).then_inc(gnnw_loaded, 16)
            sp.dma_start(brow[:, :], gnn_b.rearrange("(a d) -> a d", a=1)).then_inc(gnnw_loaded, 16)

            def front(r, o):
                if some(r - 1):
                    sp.wait_ge(xn_made, r - 1)
                sp.dma_start(xin[:, o % 2, :], x[at(r * P, P), :]).then_inc(x_loaded[o % 2], 16)
                if some(4 * (r - 3)):
                    sp.wait_ge(adj_transposed, 4 * (r - 3))
                sp.dma_start(adj_in[o], adj[at(r * P, P), :]).then_inc(adj_loaded[o], 16)

            for r in range(2):
                front(r, r)
            for l in range(2):
                sp.dma_start(wr[l][:, :, :], Wr[l].rearrange("(k p) e -> p k e", p=P)).then_inc(small_loaded, 16)
                sp.dma_start(b1n[l][:, :], b1[l].rearrange("e (c p) -> (e c) p", p=P)).then_inc(small_loaded, 16)
            for r in range(2, 4):
                front(r, r)
            sp.wait_ge(consts_made, NCONST)
            for l in range(2):
                for o in range(2):
                    junk = arena[l][JUNK[l] + o * TP:JUNK[l] + (o + 1) * TP, :].rearrange("(p s) w -> p s w", s=S)
                    sp.dma_start(junk[:, :, 0:2 * D], zeros[:, :].unsqueeze(1).broadcast_to([P, S, 2 * D])).then_inc(junk_stored, 16)
                    sp.dma_start(junk[:, :, IDC:IDC + 2], padids[:, EM + o, :].bitcast(F16).rearrange("p (s a) -> p s a", s=S)).then_inc(junk_stored, 16)
            with sp.Fori(1, NB // 4) as i:
                for o in range(4):
                    front(i * 4 + o, o)

            def group_gnn(g, new, old, prep):
                if not new:
                    return
                if prep:
                    if isinstance(g, int):
                        sp.wait_ge(adj_transposed, 4 * NB)
                    w_load(sp, *turn_gnn(g))
                for b in range(GB):
                    q = g * GB + b
                    sp.wait_ge(xn_made, NB)
                    if some(q - 1):
                        sp.wait_ge(bias_added, q - 1)
                    sp.nop(nofuse=True)
                    sp.dma_start(xin[:, b % 2, :], x[at((NB - GB - GB * g + b) * P, P), :]).then_inc(x_loaded[b % 2], 16)
                    if b:
                        store_x1(g * GB + b - 1, g, b - 1)
                store_x1(g * GB + GB - 1, g, GB - 1)

            def store_x1(q, g, b):
                sp.wait_ge(x1_made, q + 1)
                sp.dma_start(x1_dram[at((NB - GB - GB * g + b) * P, P), :], xn[:, b % 2, :]).then_inc(x1_stored[b % 2], 16)

            in_groups(sp, group_gnn, 2, NG)

            def tiles(l):
                pads_sp(sp, l)
                tile_load(sp, l, 0, 0)

                def step(t, h, turn):
                    if not (isinstance(t, int) and t == TILES[l] - 1):
                        tile_load(sp, l, t + 1, 1 - h)
                    if turn and turn[1] == 0:
                        w_load(sp, *turn_early(turn[0]))

                in_tiles(sp, l, step)

            def load_corrections(l):
                E = EXPERTS[l]
                for h in range(2):
                    sp.wait_ge(y_sent[h], 16 * (T0[l] + TILES[l]))
                sp.wait_ge(cb_cleared, l + 1)
                for b in range(GB):
                    sp.dma_start(CB[CW * b:CW * b + E, :],
                                 ys[l][PADROW:PADROW + E * TP, :].rearrange("(e p) d -> e p d", p=TP)[:, 0, :]).then_inc(cb_loaded, 16)
                    sp.dma_start(CB[CW * b + E:CW * b + 2 * E, :], b2[l]).then_inc(cb_loaded, 16)

            tiles(0)
            load_corrections(0)

            def group_mid(g, new, old, prep):
                if not new:
                    return
                if prep:
                    w_load(sp, *turn_late(g))
                for b in range(GB):
                    sp.wait_ge(xr_made, NB + GB * g + b - GB + 1)
                    sp.dma_start(yab[:, b, :, :], ys[0][0:2 * T, :].rearrange("(t r) d -> t r d", r=2)[at((g * GB + b) * P, P), :, :]).then_inc(yab_loaded[b], 16)

            in_groups(sp, group_mid, 1, NG - 1)
            tiles(1)
            load_corrections(1)

            def last(g, first):
                for b in range(GB):
                    c = g * GB + b
                    if not (first and b < 2):
                        sp.wait_ge(out_made, c - 1)
                    if not first:
                        sp.nop(nofuse=True)
                        sp.wait_ge(out_made, c - GB + 1)
                    sp.dma_start(xin[:, b % 2, :], x1_dram[at(c * P, P), :]).then_inc(x_loaded[b % 2], 16)
                    sp.dma_start(yab[:, b, :, :], ys[1][0:2 * T, :].rearrange("(t r) d -> t r d", r=2)[at(c * P, P), :, :]).then_inc(yab_loaded[b], 16)
                    if not (first and b == 0):
                        store(c - 1, (b - 1) % 2)

            def store(c, h):
                sp.wait_ge(out_made, c + 1)
                sp.dma_start(out[at(c * P, P), :], xn[:, h, :]).then_inc(out_stored[h], 16)

            for h in range(2):
                sp.wait_ge(x1_stored[h], 8 * NB)
            last(0, True)
            with sp.Fori(1, NG) as g:
                last(g, False)
            store(NB - 1, 1)
            for h in range(2):
                sp.wait_ge(out_stored[h], 8 * NB)

        @block.gpsimd
        def _(pool):
            pool.iota(diff, [[1, P]], base=0, channel_multiplier=-1, allow_small_or_imprecise_dtypes=True).then_inc(consts_made, 1)
            pool.memset(onesrow[:, :], 1.0).then_inc(consts_made, 1)
            pool.memset(half[:, 0:1], -0.5).then_inc(consts_made, 1)
            pool.memset(half[:, 1:2], 0.5).then_inc(consts_made, 1)
            pool.memset(zeros[:, :], 0.0).then_inc(consts_made, 1)
            pool.memset(ones16[:, :], 1.0).then_inc(consts_made, 1)
            pool.iota(tileno[:, :], [[1, max(TILES)]], base=0, channel_multiplier=0, allow_small_or_imprecise_dtypes=True).then_inc(consts_made, 1)
            for l in range(2):
                pool.iota(junkrow[:, l, :].rearrange("a (i o) -> a i o", o=2), [[0, max(TILES) // 2], [TP, 2]], base=JUNK[l],
                          channel_multiplier=0, allow_small_or_imprecise_dtypes=True).then_inc(consts_made, 1)
            pool.iota(ids[:, :, :], [[2 * P, NB], [1, 2]], base=0, channel_multiplier=2).then_inc(consts_made, 1)
            pool.iota(padids[:, :, :], [[TP, EM + 2], [1, S]], base=PADROW, channel_multiplier=S).then_inc(consts_made, 1)
            pool.iota(base_e[:, :], [[ARENA, EM]], base=0, channel_multiplier=0, allow_small_or_imprecise_dtypes=True).then_inc(consts_made, 1)
            pool.iota(rank_e[:, :], [[-1, EM]], base=EM, channel_multiplier=0, allow_small_or_imprecise_dtypes=True).then_inc(consts_made, 1)
            pool.memset(coef[:, :, :], 0.0).then_inc(consts_made, 1)
            pool.memset(tot[:, :], 0.0).then_inc(consts_made, 1)
            pool.memset(yrun[:, :], 0.0).then_inc(consts_made, 1)

            def block_step(r, o):
                if inside(r + 2):
                    pool.wait_ge(var_made, r + 3)
                    pool.tensor_tensor(rstd[:, o % 2:o % 2 + 1], vare[:, o % 2:o % 2 + 1], half[:, 0:1], ALU.pow).then_inc(rstd_made, 1)
                if inside(r + 1):
                    h, rows_in = (o + 1) % 2, adj_in[(o + 1) % 4]
                    pool.wait_ge(deg_rounded, r + 2)
                    pool.nop(nofuse=True)
                    pool.tensor_scalar(rows_in, rows_in, rdeg[:, h:h + 1], 4096.0, ALU.mult, ALU.mult).then_inc(adj_scaled, 1)
                    pool.tensor_tensor(dis[:, at(r + 1, 1)], degE[:, at(r + 1, 1)], half[:, 0:1], ALU.pow).then_inc(dis_made, 1)

            in_blocks(pool, block_step)
            pool.wait_ge(v_bounds, 2)
            for i in range(2):
                pool.partition_all_reduce(gst[:, 2 + i:3 + i], gst[:, i:i + 1], P, RED.max).then_inc(v_bounds_max, 1)
            pool.wait_ge(v_bounds_max, 2)
            pool.tensor_tensor(gst[:, 4:5], gst[:, 2:3], half[:, 1:2], ALU.pow).then_inc(v_bound_root, 1)

            level_scales_pool(pool, 0)

            def group_gnn(g, new, old, prep):
                for b in range(GB):
                    q = g * GB + b
                    if new:
                        pool.wait_ge(x_loaded[b % 2], ring(NB + q, b % 2))
                        pool.wait_ge(bias_copied, 1)
                        if some(q - 1):
                            pool.wait_ge(x1_made, q - 1)
                        pool.tensor_tensor(xb[:, b % 2, :], xin[:, b % 2, :], bB[:, :], ALU.add).then_inc(bias_added, 1)
                    if old and b == GB - 1:
                        for b2 in range(2):
                            scatter_pool(pool, 0, g - 1, q - b - GB + b2, b2)
                    if new:
                        pool.wait_ge(var_made, NB + q + 1)
                        pool.tensor_tensor(rstd[:, b % 2:b % 2 + 1], vare[:, b % 2:b % 2 + 1], half[:, 0:1], ALU.pow).then_inc(rstd_made, 1)
                    if prep and b == 1:
                        w_norm(pool, *turn_gnn(g))
                if old:
                    for b2 in range(2, GB):
                        scatter_pool(pool, 0, g - 1, g * GB - GB + b2, b2)

            in_groups(pool, group_gnn, 2, NG)

            def keep(l, t, h):
                n = T0[l] + t
                e = pool.value_load(tab[0:1, 2, at(t, 1)], min_val=0, max_val=EXPERTS[l] - 1)
                pool.wait_ge(tile_loaded[h], ring(n, h))
                if some(FC * (n - 1)):
                    pool.wait_ge(hid_made, FC * (n - 1))
                pool.tensor_copy(tprm[:, h, :], prm[l][:, at(e, 1), :].rearrange("p a c -> p (a c)")).then_inc(tile_params, 1)
                pool.tensor_copy(tgam[:, at(t, 1)], prm[l][:, at(e, 1), 1:2].rearrange("p a c -> p (a c)")).then_inc(tile_params, 1)
                pool.tensor_copy(tids[:, at(t, 1), :].rearrange("p a s -> p (a s)").unsqueeze(2), xtile[:, h, :, IDC:IDC + 2].bitcast(I32)).then_inc(tile_params, 1)

            def scatter_results(l, t, h):
                n = T0[l] + t
                if some((n - h) * 16):
                    pool.wait_ge(y_sent[h], (n - h) * 16)
                pool.wait_ge(tile_params, 3 * n + 3)
                pool.nop(nofuse=True)
                pool.tensor_copy(yid[:, h, :], tids[:, at(t, 1), :].rearrange("p a s -> p (a s)")).then_inc(y_ids, 1)
                pool.wait_ge(y_ids, n + 1)
                for i in range(S):
                    pool.wait_ge(y_scaled, S * n + i + 1)
                    pool.nop(nofuse=True)
                    pool.indirect_dma_start(ys[l], bass.IndirectOffsetOnAxis(ap=yid[:, h, i:i + 1], axis=0), yout[:, h, i, :], None).then_inc(y_sent[h], 16)

            def tiles(l):
                pool.wait_ge(table_made, l + 1)
                pool.wait_ge(level_scales, 2 * l + 2)
                if l == 1:
                    for h in range(2):
                        pool.wait_ge(y_sent[h], 16 * TILES[0])
                keep(l, 0, 0)

                def step(t, h, turn):
                    if not (isinstance(t, int) and t == TILES[l] - 1):
                        keep(l, t + 1, 1 - h)
                    if not (isinstance(t, int) and t == 0):
                        scatter_results(l, t - 1, 1 - h)
                    if turn and turn[1] == 1:
                        w_norm(pool, *turn_early(turn[0]))

                in_tiles(pool, l, step)
                scatter_results(l, TILES[l] - 1, (TILES[l] - 1) % 2)

            tiles(0)
            level_scales_pool(pool, 1)

            def group_mid(g, new, old, prep):
                if prep:
                    w_norm(pool, *turn_late(g))
                if old:
                    for b in range(GB):
                        scatter_pool(pool, 1, NG + g - 1, NB + g * GB - GB + b, b)

            in_groups(pool, group_mid, 1, NG - 1)
            tiles(1)

        @block.scalar
        def _(act):
            act.wait_ge(gnnw_loaded, 32)
            for k in range(KD):
                act.activation(rows[:, k, 0, 0:2 * D].bitcast(F32), wg_nat[:, k, :], ACT.Square,
                               accum_out=gst[:, 10 + k:11 + k]).then_inc(gnnw_squared, 1)
            act.wait_ge(bias_spread, 1)
            act.activation(bB[:, :], PM[:, 0:D], ACT.Copy).then_inc(bias_copied, 1)
            act.wait_ge(gnnw_transposed, 1)
            for k in range(KD):
                act.activation(wgT[:, k, :], Zq[:, k, 0:D], ACT.Copy).then_inc(gnnw_copied, 1)

            def block_step(r, o):
                h = (o + 1) % 2
                if inside(r + 1):
                    act.wait_ge(xn_transposed, r + 2)
                    if some(r):
                        act.wait_ge(u_summed, r)
                    act.activation(xrT[:, 2 * h:2 * h + 2, :], PX[:, 0:KD, :], ACT.Copy).then_inc(xn_copied, 1)
                for q in range(4):
                    if q == 2 and inside(r + 1):
                        act.wait_ge(u_summed, r + 2)
                        act.activation(u_all[:, at(r + 1, 1), :].rearrange("p a d -> p (a d)"), Y[:, h, :], ACT.Copy).then_inc(u_copied, 1)
                    if inside(r):
                        act.wait_ge(adj_transposed, r * 4 + q + 1)
                        act.activation(R[:, at(r * ATB + q * 4 * P, 4 * P)], Zq[:, q, :], ACT.Copy).then_inc(adj_hi, 1)
                if inside(r + 2):
                    rows_in = adj_in[(o + 2) % 4]
                    act.wait_ge(adj_loaded[(o + 2) % 4], ring(r + 2, (o + 2) % 4, 4))
                    act.activation(rows_in, rows_in, ACT.Copy, accum_out=deg[:, at(r + 2, 1)]).then_inc(deg_made, 1)

            in_blocks(act, block_step)
            for l in range(2):
                act.wait_ge(b1_transposed, 2)
                act.activation(b1T[l][:, :, :].rearrange("p e c -> p (e c)"), PM[:, 256 + 64 * l:256 + 64 * l + EXPERTS[l] * FC], ACT.Copy).then_inc(b1_copied, 1)
            act.wait_ge(v_scales, 1)
            with act.Fori(0, NB) as j:
                act.activation(v[:, at(j, 1), 0, :].rearrange("p a d -> p (a d)"), u_all[:, at(j, 1), :].rearrange("p a d -> p (a d)"),
                               ACT.Copy, scale=vscale[:, at(j, 1)]).then_inc(v_hi, 1)

            def group(l):
                def body(g, new, old, prep):
                    G = g + NG * l
                    turn = (turn_gnn if l == 0 else turn_late)
                    if new and l == 1:
                        act.wait_ge(coef_transposed, g + 1)
                        if some(GB * g):
                            act.wait_ge(corr_made, GB * g)
                        act.activation(cT[:, :], p_cT, ACT.Copy).then_inc(coef_copied, 1)
                    for b in range(GB):
                        q = G * GB + b
                        if old:
                            pack_act(act, l, q - GB, b)
                            if b == 0:
                                route_copy_act(act, q - 1, GB - 1)
                            elif b == 1:
                                route_exp_act(act, l, G - 1)
                        if new and b:
                            route_copy_act(act, q - 1, b - 1)
                        if prep and b == 0:
                            w_square(act, *turn(g), place_free=TILES[0])
                        if prep and b == 2:
                            w_high(act, *turn(g))
                return body

            in_groups(act, group(0), 2, NG)

            def tile_copy(l, t, h):
                n = T0[l] + t
                act.wait_ge(tile_transposed, n + 1)
                if some(2 * (n - 1)):
                    act.wait_ge(z_made, 4 * (n - 1))
                act.activation(xT[:, h, :, :], PT[:, :, :, :].rearrange("p a s t -> p a (s t)"), ACT.Copy).then_inc(tile_copied, 1)

            def tiles(l):
                if l == 0:
                    act.wait_ge(logits_made, NB)
                    act.wait_ge(graph_summed, NB)
                else:
                    act.wait_ge(logits_made, 2 * NB)
                tile_copy(l, 0, 0)

                def step(t, h, turn):
                    n = T0[l] + t
                    if not (isinstance(t, int) and t == TILES[l] - 1):
                        tile_copy(l, t + 1, 1 - h)
                    act.wait_ge(tile_params, 3 * n + 3)
                    for q in range(4):
                        act.wait_ge(z_made, 4 * n + q + 1)
                        if some(4 * n + q - 3):
                            act.wait_ge(hid_lo_made, 4 * n + q - 3)
                        for c in range(2 * q, 2 * q + 2):
                            act.activation(hid[:, c, :], Z[:, c, :], ACT.Relu, bias=tprm[:, h, 2 + c:3 + c],
                                           scale=tprm[:, h, 0:1]).then_inc(hid_made, 1)
                        if some(n - 1):
                            act.wait_ge(y_made, n - 1)
                        act.wait_ge(hid_made, n * FC + 2 * q + 2)
                        act.activation(hid_hi[:, h, 2 * q:2 * q + 2, :], hid[:, 2 * q:2 * q + 2, :], ACT.Copy).then_inc(hid_hi_made, 1)
                    if turn and turn[1] == 0:
                        w_square(act, *turn_early(turn[0]))
                    if turn and turn[1] == 1:
                        w_high(act, *turn_early(turn[0]))

                in_tiles(act, l, step)

            tiles(0)
            in_groups(act, group(1), 1, NG - 1)
            tiles(1)

            def last(g):
                act.wait_ge(coef_transposed, g + NG + 1)
                act.wait_ge(corr_made, g * GB + NB)
                act.activation(cT[:, :], p_cT, ACT.Copy).then_inc(coef_copied, 1)
            with act.Fori(0, NG) as g:
                last(g)

        @block.vector
        def _(dve):
            dve.wait_ge(consts_made, NCONST)
            dve.tensor_scalar(ident[:, :], diff, 0.0, None, ALU.is_equal)
            dve.tensor_scalar(ident16[:, :], diff, 0.0, None, ALU.is_equal)
            dve.tensor_scalar(before[:, :], diff, 0.0, None, ALU.is_gt).then_inc(masks_made, 1)
            dve.drain()
            dve.memset(cpick[:, 0:1], 0.0).then_inc(masks_made, 1)

            def block_step(r, o):
                h = o % 2
                if inside(r + 2):
                    dve.wait_ge(x_loaded[h], ring(r + 2, h))
                    dve.bn_stats(stat[:, h, :], xin[:, h, :])
                    dve.drain()
                    dve.bn_aggr(mv[:, h, :], stat[:, h, :])
                    dve.drain()
                    dve.tensor_scalar(vare[:, h:h + 1], mv[:, h, 1:2], EPS_LN, None, ALU.add).then_inc(var_made, 1)
                if inside(r + 1):
                    dve.wait_ge(deg_made, r + 2)
                    dve.tensor_scalar(degE[:, at(r + 1, 1)], deg[:, at(r + 1, 1)], EPS_DEG, None, ALU.add)
                    dve.drain()
                    dve.tensor_scalar(pdeg[:, at(r + 1, 1)].bitcast(I32), degE[:, at(r + 1, 1)].bitcast(I32), EXPONENT, None, ALU.bitwise_and)
                    dve.drain()
                    dve.reciprocal(rdeg[:, 1 - h:2 - h], pdeg[:, at(r + 1, 1)]).then_inc(deg_rounded, 1)
                for q in range(4):
                    if q == 1 and inside(r + 2):
                        dve.wait_ge(rstd_made, r + 3)
                        if some(r + 1):
                            dve.wait_ge(xn_transposed, r + 1)
                        dve.tensor_scalar(xn[:, h, :], xin[:, h, :], mv[:, h, 0:1], rstd[:, h:h + 1], ALU.subtract, ALU.mult).then_inc(xn_made, 1)
                    if inside(r):
                        dve.wait_ge(adj_hi, r * 4 + q + 1)
                        dve.tensor_tensor(R[:, at(r * ATB + (NB * P + q * 4 * P), 4 * P)], Zq[:, q, :],
                                          R[:, at(r * ATB + q * 4 * P, 4 * P)], ALU.subtract).then_inc(adj_lo, 1)

            in_blocks(dve, block_step)

            dve.wait_ge(gnnw_squared, 2)
            dve.wait_ge(dis_made, NB)
            dve.tensor_tensor(gst[:, 0:1], gst[:, 10:11], gst[:, 11:12], ALU.max).then_inc(v_bounds, 1)
            dve.tensor_reduce(gst[:, 1:2], dis[:, :], AX.X, ALU.max).then_inc(v_bounds, 1)
            dve.wait_ge(v_bound_root, 1)
            dve.tensor_scalar(gst[:, 5:6], gst[:, 4:5], 16.0, gst[:, 3:4], ALU.mult, ALU.mult)
            dve.drain()
            dve.tensor_scalar(gst[:, 5:6], gst[:, 5:6], 1e-15, None, ALU.max)
            dve.drain()
            dve.tensor_scalar(gst[:, 6:7].bitcast(I32), gst[:, 5:6].bitcast(I32), EXPONENT, None, ALU.bitwise_and)
            dve.drain()
            dve.reciprocal(gst[:, 7:8], gst[:, 6:7])
            dve.drain()
            dve.tensor_scalar(gscale[:, :], dis[:, :], gst[:, 6:7], 2.0 ** -26, ALU.mult, ALU.mult)
            dve.drain()
            dve.tensor_tensor(gscale[:, :], gscale[:, :], pdeg[:, :], ALU.mult)
            dve.tensor_scalar(vscale[:, :], dis[:, :], gst[:, 7:8], 16384.0, ALU.mult, ALU.mult).then_inc(v_scales, 1)
            dve.drain()
            with dve.Fori(0, NB) as j:
                dve.wait_ge(v_hi, j + 1)
                dve.scalar_tensor_tensor(v[:, at(j, 1), 1, :].rearrange("p a d -> p (a d)"),
                                         u_all[:, at(j, 1), :].rearrange("p a d -> p (a d)"), vscale[:, at(j, 1)],
                                         v[:, at(j, 1), 0, :].rearrange("p a d -> p (a d)"), ALU.mult, ALU.subtract).then_inc(v_lo, 1)
            level_scales_dve(dve, 0)

            def group_gnn(g, new, old, prep):
                for b in range(GB):
                    q, h = g * GB + b, b % 2
                    if old:
                        pack_dve(dve, 0, q - GB, b, (NB - GB + GB + b) - GB * g)
                    if new:
                        dve.wait_ge(graph_summed, q + 1)
                        dve.wait_ge(bias_added, q + 1)
                        if some((q - h) * 8):
                            dve.wait_ge(x1_stored[h], (q - h) * 8)
                        dve.wait_ge(xn_transposed, NB)
                        dve.nop(nofuse=True)
                        dve.scalar_tensor_tensor(xn[:, h, :], Y[:, h, :], gscale[:, at(NB - GB + b - GB * g, 1)], xb[:, h, :],
                                                 ALU.mult, ALU.add).then_inc(x1_made, 1)
                        dve.wait_ge(x1_made, q + 1)
                        dve.bn_stats(stat[:, h, :], xn[:, h, :])
                        dve.drain()
                        dve.bn_aggr(mv[:, h, :], stat[:, h, :])
                        dve.drain()
                        dve.tensor_scalar(vare[:, h:h + 1], mv[:, h, 1:2], EPS_LN, None, ALU.add).then_inc(var_made, 1)
                        dve.wait_ge(rstd_made, NB + q + 1)
                        if some(q - GB + 1):
                            dve.wait_ge(xr_transposed, q - GB + 1)
                        if some(q - GB + 1):
                            dve.wait_ge(rows_lo, q - GB + 1)
                        dve.wait_ge(u_summed, NB)
                        dve.tensor_scalar(xr[:, b, :], xn[:, h, :], mv[:, h, 0:1], rstd[:, h:h + 1], ALU.subtract, ALU.mult).then_inc(xr_made, 1)
                    if old and b == 1:
                        route_picks_dve(dve, 0, g - 1, (NB - GB + GB) - GB * g)
                    if old and b == 2:
                        route_slots_dve(dve, 0, g - 1)
                    if prep and b == 1:
                        w_scale(dve, *turn_gnn(g))
                    if prep and b == GB - 1:
                        w_low(dve, *turn_gnn(g))

            in_groups(dve, group_gnn, 2, NG)
            table_dve(dve, 0)
            level_params_dve(dve, 0)

            def result(l, t, h):
                n = T0[l] + t
                dve.wait_ge(y_made, n + 1)
                dve.wait_ge(tile_params, 3 * n + 3)
                if some((n - h) * 16):
                    dve.wait_ge(y_sent[h], (n - h) * 16)
                for i in range(S):
                    dve.tensor_scalar(yout[:, h, i, :], Y[:, i, :], tgam[:, at(t, 1)], None, ALU.mult).then_inc(y_scaled, 1)
                if l == 0:
                    dve.wait_ge(y_scaled, S * n + S)
                    dve.tensor_reduce(ymax[:, h:h + 1], yout[:, h, :, :].rearrange("p s d -> p (s d)"), AX.X, ALU.max, apply_absolute_value=True)
                    dve.drain()
                    dve.tensor_tensor(yrun[:, 0:1], yrun[:, 0:1], ymax[:, h:h + 1], ALU.max)
                    dve.drain()

            def tiles(l):
                def step(t, h, turn):
                    n = T0[l] + t
                    if some(n - 1):
                        dve.wait_ge(y_made, n - 1)
                    for q in range(4):
                        dve.wait_ge(hid_hi_made, 4 * n + q + 1)
                        dve.tensor_tensor(hid_lo[:, h, 2 * q:2 * q + 2, :], hid[:, 2 * q:2 * q + 2, :],
                                          hid_hi[:, h, 2 * q:2 * q + 2, :], ALU.subtract).then_inc(hid_lo_made, 1)
                    if not (isinstance(t, int) and t == 0):
                        result(l, t - 1, 1 - h)
                    if turn and turn[1] == 1:
                        w_scale(dve, *turn_early(turn[0]))
                        w_low(dve, *turn_early(turn[0]))

                for b in range(GB):
                    dve.wait_ge(rows_sent[b], 2 * 16 * NG * (l + 1))
                if l == 0:
                    for h in range(2):
                        dve.wait_ge(x1_stored[h], 8 * NB)
                in_tiles(dve, l, step)
                result(l, TILES[l] - 1, (TILES[l] - 1) % 2)

            dve.memset(CB[:, :], 0.0)
            dve.drain()
            dve.memset(cpick[:, 0:1], 0.0).then_inc(cb_cleared, 1)
            tiles(0)
            dve.wait_ge(cb_loaded, 2 * GB * 16)
            dve.memset(tot[:, :], 0.0).then_inc(totals_made, 1)
            dve.wait_ge(totals_made, NG + 1)
            level_scales_dve(dve, 1)

            def coefficients(G, g):
                if some(G):
                    dve.wait_ge(coef_transposed, G)
                dve.tensor_copy(cgrp[:, :, :], coef[:, at(g * GB, GB), :]).then_inc(coef_grouped, 1)

            def combine(l, c, b, into):
                blk = c - NB * l if l else c
                h = b % 2
                dve.wait_ge(corr_made, c + 1)
                dve.wait_ge(yab_loaded[b], (c - b) * 4 + 16)
                dve.scalar_tensor_tensor(xb[:, h, :], yab[:, b, 1, :], p12[:, at(blk, 1), 1].rearrange("p a -> p a"), Y[:, h, :], ALU.mult, ALU.add)
                dve.drain()
                if l == 1:
                    dve.wait_ge(x_loaded[h], ring(2 * NB + blk, h))
                    dve.tensor_tensor(xb[:, h, :], xb[:, h, :], xin[:, h, :], ALU.add)
                    dve.drain()
                return dve.scalar_tensor_tensor(into, yab[:, b, 0, :], p12[:, at(blk, 1), 0].rearrange("p a -> p a"), xb[:, h, :], ALU.mult, ALU.add)

            def group_mid(g, new, old, prep):
                if new:
                    coefficients(g, g)
                for b in range(GB):
                    q = NB + g * GB + b
                    if old:
                        pack_dve(dve, 1, q - GB, b, GB * g - GB + b)
                    if new:
                        dve.wait_ge(xr_transposed, q - GB + 1)
                        dve.wait_ge(rows_lo, q - GB + 1)
                        combine(0, g * GB + b, b, xr[:, b, :]).then_inc(xr_made, 1)
                    if old and b == 1:
                        route_picks_dve(dve, 1, NG + g - 1, GB * g - GB)
                    if old and b == 2:
                        route_slots_dve(dve, 1, NG + g - 1)
                    if prep and b == 1:
                        w_scale(dve, *turn_late(g))
                    if prep and b == GB - 1:
                        w_low(dve, *turn_late(g))

            in_groups(dve, group_mid, 1, NG - 1)
            table_dve(dve, 1)
            level_params_dve(dve, 1)
            dve.wait_ge(corr_made, NB)
            dve.memset(CB[:, :], 0.0)
            dve.drain()
            dve.memset(cpick[:, 0:1], 0.0).then_inc(cb_cleared, 1)
            tiles(1)

            def last(g, first):
                coefficients(NG + g, g)
                for b in range(GB):
                    c = g * GB + b
                    if not (first and b < 2):
                        dve.wait_ge(out_stored[b % 2], (c - b % 2) * 8)
                    if first and b == 0:
                        for h in range(2):
                            dve.wait_ge(y_sent[h], 16 * sum(TILES))
                    combine(1, NB + c, b, xn[:, b % 2, :]).then_inc(out_made, 1)

            last(0, True)
            with dve.Fori(1, NG) as g:
                last(g, False)

        @block.tensor
        def _(pe):
            pe.wait_ge(gnnw_loaded, 32)
            pe.wait_ge(consts_made, NCONST)
            pe.matmul(PM[:, 0:D], onesrow[:, :], brow[:, :], start=True, stop=True).then_inc(bias_spread, 1)
            pe.wait_ge(masks_made, 2)
            for k in range(KD):
                for m in range(KD):
                    ins = pe.transpose(Zq[:, k, m * P:(m + 1) * P], wg_nat[:, m, k * P:(k + 1) * P], ident[:, :])
            ins.then_inc(gnnw_transposed, 1)
            pe.wait_ge(bias_copied, 1)
            pe.wait_ge(gnnw_copied, 2)

            def block_step(r, o):
                h = (o + 1) % 2
                if inside(r + 1):
                    pe.wait_ge(xn_made, r + 2)
                    if some(r + 1):
                        pe.wait_ge(xn_copied, r + 1)
                    for k in range(KD):
                        ins = pe.transpose(PX[:, k, :], xn[:, h, k * P:(k + 1) * P], ident[:, :])
                    ins.then_inc(xn_transposed, 1)
                if inside(r):
                    pe.wait_ge(adj_scaled, r + 1)
                for q in range(4):
                    if q == 2 and inside(r + 1):
                        pe.wait_ge(xn_copied, r + 2)
                        if some(r):
                            pe.wait_ge(u_copied, r)
                        for k in range(KD):
                            ins = pe.matmul(Y[:, h, :], xrT[:, 2 * h + k, :], wgT[:, k, :], start=(k == 0), stop=(k == KD - 1))
                        ins.then_inc(u_summed, 1)
                    if inside(r):
                        if some(r * 4 + q - 3):
                            pe.wait_ge(adj_lo, r * 4 + q - 3)
                        for j in range(4 * q, 4 * q + 4):
                            ins = pe.transpose(Zq[:, q, (j % 4) * P:(j % 4 + 1) * P], adj_in[o][:, j * P:(j + 1) * P], ident[:, :])
                        ins.then_inc(adj_transposed, 1)

            in_blocks(pe, block_step)
            pe.wait_ge(small_loaded, 64)
            for l in range(2):
                n = EXPERTS[l] * FC
                pe.transpose(PM[:, 256 + 64 * l:256 + 64 * l + n], b1n[l][:, :], ident[0:n, 0:n]).then_inc(b1_transposed, 1)

            def product(g, b):
                q = g * GB + b
                first = isinstance(q, int) and q == 0
                if some(q - 1):
                    pe.wait_ge(x1_made, q - 1)
                if first:
                    pe.wait_ge(u_copied, NB)
                    pe.wait_ge(adj_lo, 4 * NB)
                a = (NB - GB + b - GB * g) * ATB
                pe.nop(nofuse=True)
                for j in range(NB):
                    if first:
                        pe.wait_ge(v_lo, j + 1)
                    hi, lo = (R[:, at(a + (m * NB + j) * P, P)] for m in range(2))
                    pe.matmul(Y[:, b % 2, :], hi, v[:, j, 0, :], start=(j == 0), stop=False)
                    pe.matmul(Y[:, b % 2, :], hi, v[:, j, 1, :], start=False, stop=False)
                    ins = pe.matmul(Y[:, b % 2, :], lo, v[:, j, 0, :], start=False, stop=(j == NB - 1))
                ins.then_inc(graph_summed, 1)

            def group(l):
                def body(g, new, old, prep):
                    G = g + NG * l
                    if new and l == 1:
                        pe.wait_ge(coef_grouped, g + 1)
                        if some(g):
                            pe.wait_ge(coef_copied, g)
                        if isinstance(g, int) and g == 0:
                            pe.wait_ge(cb_loaded, 2 * GB * 16)
                        pe.transpose(p_cT, cgrp[:, :, :].rearrange("p b c -> p (b c)"), ident[:, :]).then_inc(coef_transposed, 1)
                        pe.wait_ge(coef_copied, g + 1)
                    for b in range(GB):
                        q = G * GB + b
                        if new and l == 0:
                            product(g, b)
                        if new and l == 1:
                            pe.wait_ge(xr_made, q - 1)
                            pe.matmul(Y[:, b % 2, :], cT[CW * b:CW * (b + 1), :], CB[CW * b:CW * (b + 1), :], start=True, stop=True).then_inc(corr_made, 1)
                        if b == 0 and old:
                            route_t_pe(pe, q - 1, GB - 1)
                            route_logits_pe(pe, l, G - 1, q - 2, GB - 2)
                            if not new:
                                route_logits_pe(pe, l, G - 1, q - 1, GB - 1)
                        if b == 1:
                            if new:
                                route_t_pe(pe, q - 1, 0)
                            if new and old:
                                route_logits_pe(pe, l, G - 1, q - 2, GB - 1)
                        if b >= 2 and new:
                            route_t_pe(pe, q - 1, b - 1)
                            route_logits_pe(pe, l, G, q - 2, b - 2)
                        if b == 2 and old:
                            route_pos_pe(pe, l, G - 1)
                return body

            def count(l):
                pe.wait_ge(totals_made, (NG + 1) * l + NG)
                pe.matmul(p_cnt[:, 0:EXPERTS[l]], ones16[:, :], tot[:, 0:EXPERTS[l]], start=True, stop=True).then_inc(counts_made, 1)

            in_groups(pe, group(0), 2, NG)
            count(0)

            def tile_transpose(l, t, h):
                n = T0[l] + t
                pe.wait_ge(tile_loaded[h], ring(n, h))
                if some(n):
                    pe.wait_ge(tile_copied, n)
                for a in range(2 * KD):
                    for i in range(S):
                        ins = pe.transpose(PT[:, a, i, :], xtile[:, h, i, a * P:(a + 1) * P], ident16[:, :])
                ins.then_inc(tile_transposed, 1)

            def weights(t):
                w = pe.value_load(tab[0:1, 1, at(t, 1)], min_val=0, max_val=(NSLOT - 1) * WSLOT)
                return lambda start, n: R[:, at(w + start, n)]

            def layer1(n, h, q, w):
                if some(FC * n + 2 * q + 2 - FC):
                    pe.wait_ge(hid_made, FC * n + 2 * q + 2 - FC)
                for c in range(2 * q, 2 * q + 2):
                    for k in range(KD):
                        hi, lo = (w(m * UNIT + k * F + c * P, P) for m in range(2))
                        pe.matmul(Z[:, c, :], hi, xT[:, h, k, :], start=(k == 0), stop=False)
                        pe.matmul(Z[:, c, :], hi, xT[:, h, KD + k, :], start=False, stop=False)
                        ins = pe.matmul(Z[:, c, :], lo, xT[:, h, k, :], start=False, stop=(k == KD - 1))
                ins.then_inc(z_made, 1)

            def layer2(n, h, q, w):
                pe.wait_ge(hid_lo_made, 4 * n + q + 1)
                if q == 0 and some(S * n):
                    pe.wait_ge(y_scaled, S * n)
                for c in range(2 * q, 2 * q + 2):
                    hi, lo = (w(2 * UNIT + (2 * c + m) * D, D) for m in range(2))
                    for i in range(S):
                        block = slice(i * P, (i + 1) * P)
                        pe.matmul(Y[:, i, :], hid_hi[:, h, c, block], hi, start=(c == 0), stop=False)
                        pe.matmul(Y[:, i, :], hid_hi[:, h, c, block], lo, start=False, stop=False)
                        ins = pe.matmul(Y[:, i, :], hid_lo[:, h, c, block], hi, start=False, stop=(c == FC - 1))
                if q == 3:
                    ins.then_inc(y_made, 1)

            def tiles(l):
                pe.wait_ge(table_made, l + 1)
                pe.wait_ge(w_lo, 2 * sum(EXPERTS[:l + 1]))
                if l == 0:
                    pe.wait_ge(x1_made, NB)
                else:
                    pe.wait_ge(xr_made, 2 * NB)
                tile_transpose(l, 0, 0)

                def step(t, h, turn):
                    n = T0[l] + t
                    w = weights(t)
                    before_it = not (isinstance(t, int) and t == 0)
                    if before_it:
                        w_before = weights(t - 1)
                    pe.wait_ge(tile_copied, n + 1)
                    for q in range(4):
                        layer1(n, h, q, w)
                        if q == 0 and not (isinstance(t, int) and t == TILES[l] - 1):
                            tile_transpose(l, t + 1, 1 - h)
                        if before_it:
                            layer2(n - 1, 1 - h, q, w_before)

                in_tiles(pe, l, step)
                w = weights(TILES[l] - 1)
                for q in range(4):
                    layer2(T0[l] + TILES[l] - 1, (TILES[l] - 1) % 2, q, w)

            tiles(0)
            in_groups(pe, group(1), 1, NG - 1)
            count(1)
            tiles(1)

            def last(g, first):
                pe.wait_ge(coef_grouped, g + NG + 1)
                pe.wait_ge(coef_copied, g + NG)
                if first:
                    pe.wait_ge(cb_loaded, 4 * GB * 16)
                    pe.wait_ge(y_scaled, S * sum(TILES))
                pe.transpose(p_cT, cgrp[:, :, :].rearrange("p b c -> p (b c)"), ident[:, :]).then_inc(coef_transposed, 1)
                pe.wait_ge(coef_copied, g + NG + 1)
                for b in range(GB):
                    c = g * GB + b
                    if not (first and b < 2):
                        pe.wait_ge(out_made, c - 1)
                    pe.matmul(Y[:, b % 2, :], cT[CW * b:CW * (b + 1), :], CB[CW * b:CW * (b + 1), :], start=True, stop=True).then_inc(corr_made, 1)

            last(0, True)
            with pe.Fori(1, NG) as g:
                last(g, False)


_INS = ['x', 'adj', 'L0_gnn_W', 'L0_gnn_b', 'L0_ffn_Wr0', 'L0_ffn_W1_0', 'L0_ffn_b1_0', 'L0_ffn_W2_0', 'L0_ffn_b2_0',
        'L0_ffn_Wr1', 'L0_ffn_W1_1', 'L0_ffn_b1_1', 'L0_ffn_W2_1', 'L0_ffn_b2_1']
_OUTS = [((2048, 256), 'float32')]


def kernel(**inputs):
    import numpy as _np
    import concourse.bacc as _bacc
    from concourse import mybir as _mybir
    from concourse.bass_utils import run_bass_kernel_spmd as _run

    nc = _bacc.Bacc("TRN2", target_bir_lowering=False, num_devices=1, dynamic_dma_scratch_size=8192)
    arrays, args = {}, []
    for name in _INS:
        a = _np.ascontiguousarray(inputs[name])
        arrays[f"in_{name}_dram"] = a
        args.append(nc.dram_tensor(f"in_{name}_dram", a.shape, _mybir.dt.from_np(a.dtype), kind="ExternalInput").ap())
    for i, (shape, dtype) in enumerate(_OUTS):
        dt = _mybir.dt.from_np(_np.dtype(dtype))
        args.append(nc.dram_tensor(f"out_{i}_dram", shape, dt, kind="ExternalOutput").ap())
    bass_gnn_moe(nc, *args)
    r = _run(nc, [arrays], core_ids=[0])
    return r.results[0]["out_0_dram"]
```

```python
from contextlib import ExitStack

import concourse.bass as bass
from concourse import mybir

F32, F16, I32 = mybir.dt.float32, mybir.dt.float16, mybir.dt.int32
ALU = mybir.AluOpType
ACT = mybir.ActivationFunctionType
AX = mybir.AxisListType
RED = bass.bass_isa.ReduceOp

P = 128
EXPONENT = 0x7F800000


def bass_gnn_moe(nc, x, adj, gnn_W, gnn_b, Wr0, W1_0, b1_0, W2_0, b2_0, Wr1, W1_1, b1_1, W2_1, b2_1, out):
    T, D = x.shape
    NB = T // P
    GB = 4
    NG = NB // GB
    KD = D // P
    F = W1_0.shape[2]
    FC = F // P
    EXPERTS = (W1_0.shape[0], W1_1.shape[0])
    EM = max(EXPERTS)
    S = 2
    TP = S * P
    ARENA = T + TP
    TILES = [2 * T // TP + e for e in EXPERTS]
    JUNK = [e * ARENA for e in EXPERTS]
    RW = 2 * D + 2
    IDC = 2 * D
    PADROW = 2 * T
    YROWS = 2 * T + (EM + 2) * TP
    CW = 32
    WSLOT = 2 * (KD * F + FC * D)
    UNIT = KD * F
    NSLOT = 9
    ATB = 2 * NB * P
    EARLY = EM - 3
    EPS_LN, EPS_DEG = 1e-5, 1e-8
    Wr, W1, b1, W2, b2 = (Wr0, Wr1), (W1_0, W1_1), (b1_0, b1_1), (W2_0, W2_1), (b2_0, b2_1)
    W1v = [w.rearrange("e (k p) f -> e p k f", p=P) for w in W1]
    W2v = [w.rearrange("e (c p) d -> e p c d", p=P) for w in W2]

    ctx = ExitStack()
    with ctx:
        def sb(name, shape, dt=F32):
            return ctx.enter_context(nc.sbuf_tensor(name, shape, dt))

        def ps(name, shape, dt=F32):
            return ctx.enter_context(nc.psum_tensor(name, shape, dt))

        def sem(name):
            return ctx.enter_context(nc.semaphore(name))

        def dram(name, shape, dt):
            return nc.dram_tensor(name, shape, dt).ap()

        arena = [dram(f"arena{l}", (EXPERTS[l] * ARENA + 2 * TP, RW), F16) for l in range(2)]
        NCONST = 16
        ys = [dram(f"ys{l}", (YROWS, D), F32) for l in range(2)]
        x1_dram = dram("x1_dram", (T, D), F32)
        pad_rows = dram("pad_rows", (EM * TP, RW), F16)

        R = sb("R", [P, NSLOT * WSLOT], F16)
        stage = sb("stage", [P, 2, UNIT])
        U = sb("U", [P, NB * 2 * D], F16)
        adj_in = [stage[:, i, :] for i in range(2)] + [U[:, 2 * i * UNIT:2 * (i + 1) * UNIT].bitcast(F32) for i in range(2)]
        v = U[:, :].rearrange("p (j h d) -> p j h d", j=NB, h=2)
        hid = U[:, 0:2 * FC * TP].bitcast(F32).rearrange("p (c t) -> p c t", c=FC)
        hid_hi = U[:, 2 * FC * TP:4 * FC * TP].rearrange("p (s c t) -> p s c t", s=2, c=FC)
        yab = R[:, EARLY * WSLOT:(EARLY + 2) * WSLOT].bitcast(F32).rearrange("p (j r d) -> p j r d", j=NB, r=2)
        rows_1 = R[:, (EARLY + 2) * WSLOT:(EARLY + 4) * WSLOT][:, 0:(NG - 1) * GB * 2 * RW].rearrange("p (g b r w) -> p g b r w", g=NG - 1, b=GB, r=2)
        out_all = R[:, 0:WSLOT].bitcast(F32).rearrange("p (j d) -> p j d", j=NB)
        u_all = R[:, (NSLOT - 1) * WSLOT:NSLOT * WSLOT].bitcast(F32).rearrange("p (j d) -> p j d", j=NB)
        rows = sb("rows", [P, GB, 2, RW], F16)
        hid_lo = rows[:, :, :, :].rearrange("p b r w -> p (b r w)")[:, 0:2 * FC * TP].rearrange("p (s c t) -> p s c t", s=2, c=FC)
        xr = sb("xr", [P, GB, D])
        wg_nat = xr[:, 0:KD, :]
        wgT = xr[:, KD:2 * KD, :]
        xT = sb("xT", [P, 2, 2 * KD, TP], F16)
        xrT = xT[:, 0, :, :].rearrange("p a t -> p (a t)").bitcast(F32).rearrange("p (k t) -> p k t", k=KD * 2)
        yout = sb("yout", [P, 2, S, D])
        xin, xn = yout[:, 0, :, :], yout[:, 1, :, :]
        xtile = sb("xtile", [P, 2, S, RW], F16)
        xb = xT[:, 1, :, :].rearrange("p a t -> p (a t)").bitcast(F32).rearrange("p (b d) -> p b d", b=2)
        bB = sb("bB", [P, D])
        zeros = sb("zeros", [P, 2 * D], F16)
        ident = sb("ident", [P, P])
        ident16 = sb("ident16", [P, P], F16)
        before = sb("before", [P, P], F16)
        ones16 = sb("ones16", [P, P], F16)
        onesrow = sb("onesrow", [1, P])
        brow = sb("brow", [1, D])
        diff = xb[:, 0, 0:P]
        tileno = sb("tileno", [1, max(TILES)])
        junkrow = sb("junkrow", [1, 2, max(TILES)])
        ids = sb("ids", [P, NB, 2], I32)
        padids = sb("padids", [P, EM + 2, S], I32)
        base_e = sb("base_e", [P, EM])
        rank_e = sb("rank_e", [P, EM])
        half = sb("half", [P, 4])
        wr = [sb(f"wr{l}", [P, KD, EXPERTS[l]]) for l in range(2)]
        b1n = [sb(f"b1n{l}", [EXPERTS[l] * FC, P]) for l in range(2)]
        b1T = [sb(f"b1T{l}", [P, EXPERTS[l], FC]) for l in range(2)]
        prm = [sb(f"prm{l}", [P, EXPERTS[l], FC + 2]) for l in range(2)]
        wstat = sb("wstat", [P, 2])
        wnorm = sb("wnorm", [P, 2])
        wtot = sb("wtot", [P, 2])
        wpow = sb("wpow", [P, 2, 12])
        winv = sb("winv", [P, 2, 12])
        wscl = sb("wscl", [P, 2, 12])
        lv = [sb(f"lv{l}", [P, 16]) for l in range(2)]
        lve = [sb(f"lve{l}", [P, 4, EXPERTS[l]]) for l in range(2)]
        CB = sb("CB", [P, D])
        coef = sb("coef", [P, NB, CW])
        cT_all = stage[:, 0, 0:NG * P]
        x1_all = R[:, EM * WSLOT:NSLOT * WSLOT].bitcast(F32).rearrange("p (j d) -> p j d", j=NB)
        p12 = sb("p12", [P, NB, 2])
        stat = sb("stat", [P, 2, 6])
        mv = sb("mv", [P, 2, 2])
        rstd = sb("rstd", [P, 2])
        deg = sb("deg", [P, NB])
        dis = sb("dis", [P, NB])
        pdeg = sb("pdeg", [P, NB])
        rdeg = sb("rdeg", [P, 2])
        vscale = sb("vscale", [P, NB])
        gscale = sb("gscale", [P, NB])
        gst = sb("gst", [P, 12])
        degE = sb("degE", [P, NB])
        vare = sb("vare", [P, 2])
        rt = sb("rt", [P, 12, GB, EM])
        rs = sb("rs", [P, 8, GB])
        disp = sb("disp", [P, GB, EM], F16)
        tot = sb("tot", [P, EM], F16)
        cpick = sb("cpick", [P, EM])
        slot = [sb("slot0", [P, 1, GB, 2], I32), sb("slot1", [P, NG, GB, 2], I32)]
        cnt = sb("cnt", [1, 8, EM])
        cnti = sb("cnti", [1, 2, EM], I32)
        steps = U[0:1, 0:4 * EM * max(TILES)].bitcast(F32).rearrange("p (i e t) -> p i e t", i=2, e=EM)
        tabf = sb("tabf", [1, 2, max(TILES)])
        tab = sb("tab", [1, 3, max(TILES)], I32)
        tprm = sb("tprm", [P, 2, FC + 2])
        tgam = sb("tgam", [P, max(TILES)])
        tids = sb("tids", [P, max(TILES), S], I32)
        yid = sb("yid", [P, 2, S], I32)
        ymax = sb("ymax", [P, 2])
        yrun = sb("yrun", [P, 2])

        Zq = ps("Z", [P, 4, 4 * P])
        Z = Zq[:, :, :].rearrange("p q (o t) -> p (q o) t", o=2)
        p_log = Zq[:, 0, 0:GB * EM].rearrange("p (b e) -> p b e", b=GB)
        p_pos = Zq[:, 1, 0:GB * EM].rearrange("p (b e) -> p b e", b=GB)
        p_cnt = Zq[:, 2, 0:EM]
        p_cT = Zq[:, 3, 0:NG * P]
        Y2 = ps("Y", [P, 2, 4 * P])
        Y = Y2[:, :, 0:D]
        PT = ps("PT", [P, 2 * KD, 2, P], F16)
        PM = PT[:, :, :, :].rearrange("p a b t -> p (a b t)").bitcast(F32)
        PX = ps("PX", [P, 2 * KD, P])

        consts_made = sem("consts_made")
        masks_made = sem("masks_made")
        gnnw_loaded = sem("gnnw_loaded")
        gnnw_squared = sem("gnnw_squared")
        gnnw_transposed = sem("gnnw_transposed")
        gnnw_copied = sem("gnnw_copied")
        bias_spread = sem("bias_spread")
        bias_copied = sem("bias_copied")
        small_loaded = sem("small_loaded")
        b1_transposed = sem("b1_transposed")
        b1_copied = sem("b1_copied")
        var_made = sem("var_made")
        rstd_made = sem("rstd_made")
        xn_made = sem("xn_made")
        xn_transposed = sem("xn_transposed")
        xn_copied = sem("xn_copied")
        u_summed = sem("u_summed")
        u_copied = sem("u_copied")
        deg_made = sem("deg_made")
        deg_rounded = sem("deg_rounded")
        dis_made = sem("dis_made")
        adj_scaled = sem("adj_scaled")
        adj_transposed = sem("adj_transposed")
        adj_hi = sem("adj_hi")
        adj_lo = sem("adj_lo")
        v_bounds = sem("v_bounds")
        v_bounds_max = sem("v_bounds_max")
        v_bound_root = sem("v_bound_root")
        v_scales = sem("v_scales")
        v_hi = sem("v_hi")
        v_lo = sem("v_lo")
        graph_summed = sem("graph_summed")
        bias_added = sem("bias_added")
        x1_made = sem("x1_made")
        xr_made = sem("xr_made")
        xr_transposed = sem("xr_transposed")
        xr_copied = sem("xr_copied")
        logits_made = sem("logits_made")
        logits_shifted = sem("logits_shifted")
        exps_made = sem("exps_made")
        picks_made = sem("picks_made")
        places_counted = sem("places_counted")
        slots_made = sem("slots_made")
        rows_hi = sem("rows_hi")
        rows_lo = sem("rows_lo")
        rows_id = sem("rows_id")
        totals_made = sem("totals_made")
        counts_made = sem("counts_made")
        ends_made = sem("ends_made")
        table_made = sem("table_made")
        pad_rows_stored = sem("pad_rows_stored")
        pads_stored = sem("pads_stored")
        junk_stored = sem("junk_stored")
        w_squared = sem("w_squared")
        w_summed = sem("w_summed")
        w_normed = sem("w_normed")
        w_scaled = sem("w_scaled")
        w_hi = sem("w_hi")
        w_lo = sem("w_lo")
        level_stats = sem("level_stats")
        level_maxima = sem("level_maxima")
        level_scales = sem("level_scales")
        params_made = sem("params_made")
        tile_transposed = sem("tile_transposed")
        tile_copied = sem("tile_copied")
        tile_params = sem("tile_params")
        z_made = sem("z_made")
        hid_made = sem("hid_made")
        hid_hi_made = sem("hid_hi_made")
        hid_lo_made = sem("hid_lo_made")
        y_made = sem("y_made")
        y_scaled = sem("y_scaled")
        y_ids = sem("y_ids")
        cb_cleared = sem("cb_cleared")
        cb_loaded = sem("cb_loaded")
        coef_transposed = sem("coef_transposed")
        coef_kept = sem("coef_kept")
        x1_back = sem("x1_back")
        corr_made = sem("corr_made")
        out_made = sem("out_made")
        x_loaded = [sem(f"x_loaded{h}") for h in range(2)]
        adj_loaded = [sem(f"adj_loaded{h}") for h in range(4)]
        x1_stored = [sem(f"x1_stored{h}") for h in range(2)]
        w_loaded = [sem(f"w_loaded{m}") for m in range(2)]
        tile_loaded = [sem(f"tile_loaded{h}") for h in range(2)]
        y_sent = [sem(f"y_sent{h}") for h in range(2)]
        out_stored = sem("out_stored")
        rows_sent = [sem(f"rows_sent{h}") for h in range(GB)]
        yab_loaded = [sem(f"yab_loaded{g}") for g in range(NG)]


        def some(n):
            return not isinstance(n, int) or n > 0

        def ring(n, h, parts=2):
            return (n - h) * (16 // parts) + 16

        def at(start, n):
            return bass.ds(start, n) if not isinstance(start, int) else slice(start, start + n)

        BOTH = (0, 1)

        def w_load(sp, n, l, e, s, ms=BOTH):
            for m in ms:
                if some(2 * n - 1 + m):
                    sp.wait_ge(w_hi, 2 * n - 1 + m)
                    sp.wait_ge(w_lo, 2 * n - 1 + m)
                sp.nop(nofuse=True)
                if m == 0:
                    sp.dma_start(stage[:, 0, :].rearrange("p (k f) -> p k f", k=KD), W1v[l][at(e, 1)].rearrange("e p k f -> (e p) k f")).then_inc(w_loaded[0], 16)
                else:
                    sp.dma_start(stage[:, 1, :].rearrange("p (c d) -> p c d", c=FC), W2v[l][at(e, 1)].rearrange("e p c d -> (e p) c d")).then_inc(w_loaded[1], 16)

        def w_square(act, n, l, e, s, ms=BOTH):
            if l == 1:
                act.wait_ge(graph_summed, NB)
            else:
                act.wait_ge(v_lo, NB)
                if some(GB * n):
                    act.wait_ge(graph_summed, GB * n)
            for m in ms:
                act.wait_ge(w_loaded[m], 16 * n + 16)
                if some(2 * n - 1 + m):
                    act.wait_ge(w_summed, 2 * n - 1 + m)
                act.activation(R[:, at(s * WSLOT + m * 2 * UNIT, UNIT)], stage[:, m, :], ACT.Square,
                               accum_out=wstat[:, m:m + 1]).then_inc(w_squared, 1)

        def w_norm(pool, n, l, e, s, ms=BOTH):
            for m in ms:
                pool.wait_ge(w_squared, 2 * n + 1 + m)
                if some(2 * n - 1 + m):
                    pool.wait_ge(w_scaled, 2 * n - 1 + m)
                pool.nop(nofuse=True)
                pool.partition_all_reduce(wtot[:, m:m + 1], wstat[:, m:m + 1], P, RED.add).then_inc(w_summed, 1)
            for m in ms:
                pool.wait_ge(w_summed, 2 * n + 1 + m)
                pool.tensor_tensor(wnorm[:, m:m + 1], wtot[:, m:m + 1], half[:, 1:2], ALU.pow).then_inc(w_normed, 1)

        def w_scale(dve, n, l, e, s, ms=BOTH):
            its = slice(ms[0], ms[-1] + 1)
            dve.wait_ge(w_normed, 2 * n + 1 + ms[-1])
            dve.tensor_scalar(wpow[:, its, at(n, 1)], wnorm[:, its].unsqueeze(2), 1e-15, None, ALU.max)
            dve.drain()
            dve.tensor_scalar(wpow[:, its, at(n, 1)].bitcast(I32), wpow[:, its, at(n, 1)].bitcast(I32), EXPONENT, None, ALU.bitwise_and)
            dve.drain()
            dve.reciprocal(winv[:, its, at(n, 1)], wpow[:, its, at(n, 1)])
            dve.drain()
            dve.tensor_scalar(wscl[:, its, at(n, 1)], winv[:, its, at(n, 1)], 8192.0, None, ALU.mult).then_inc(w_scaled, len(ms))

        def w_parts(s, m):
            if m == 0:
                return R[:, at(s * WSLOT, UNIT)], R[:, at(s * WSLOT + UNIT, UNIT)], stage[:, 0, :]
            w2 = R[:, at(s * WSLOT + 2 * UNIT, 2 * UNIT)].rearrange("p (c h d) -> p h c d", h=2, d=D)
            return w2[:, 0], w2[:, 1], stage[:, 1, :].rearrange("p (c d) -> p c d", c=FC)

        def w_high(act, n, l, e, s, ms=BOTH):
            for m in ms:
                hi, lo, src = w_parts(s, m)
                act.wait_ge(w_scaled, 2 * n + 1 + m)
                act.wait_ge(w_squared, 2 * n + 1 + m)
                act.activation(hi, src, ACT.Copy, scale=wscl[:, m, at(n, 1)]).then_inc(w_hi, 1)

        def w_low(dve, n, l, e, s, ms=BOTH):
            for m in ms:
                hi, lo, src = w_parts(s, m)
                dve.wait_ge(w_hi, 2 * n + 1 + m)
                dve.nop(nofuse=True)
                dve.scalar_tensor_tensor(lo, src, wscl[:, m, at(n, 1)], hi, ALU.mult, ALU.subtract).then_inc(w_lo, 1)

        def level_scales_dve(dve, l):
            E, n0 = EXPERTS[l], 0 if l == 0 else EXPERTS[0]
            dve.wait_ge(b1_copied, l + 1)
            dve.tensor_reduce(lv[l][:, 0:1], b1T[l][:, :, :].rearrange("p e c -> p (e c)"), AX.X, ALU.max, apply_absolute_value=True)
            if l == 0:
                dve.memset(lv[l][:, 1:3], 0.0).then_inc(level_stats, 1)
            else:
                dve.tensor_reduce(lv[l][:, 1:2], CB[:, :], AX.X, ALU.max, apply_absolute_value=True)
                dve.tensor_copy(lv[l][:, 2:3], yrun[:, 0:1]).then_inc(level_stats, 1)
            dve.drain()
            dve.memset(lv[l][:, 15:16], 0.0).then_inc(level_stats, 1)
            dve.wait_ge(level_maxima, 3 * l + 3)
            X, M1, PW = lv[l], lve[l], wpow
            if l == 0:
                dve.memset(X[:, 6:7], 1.0)
                dve.drain()
            else:
                dve.tensor_tensor(X[:, 6:7], X[:, 4:5], X[:, 5:6], ALU.add)
                dve.drain()
                dve.tensor_scalar(X[:, 6:7], X[:, 6:7], 1e-15, None, ALU.max)
                dve.drain()
            dve.tensor_scalar(X[:, 7:8].bitcast(I32), X[:, 6:7].bitcast(I32), EXPONENT, None, ALU.bitwise_and)
            dve.drain()
            dve.reciprocal(X[:, 8:9], X[:, 7:8])
            dve.drain()
            dve.tensor_scalar(X[:, 9:10], X[:, 8:9], 1024.0 if l == 0 else 8192.0, None, ALU.mult).then_inc(level_scales, 1)
            dve.tensor_scalar(X[:, 10:11], X[:, 7:8], 1 / 1024.0 if l == 0 else 1 / 8192.0, None, ALU.mult)
            dve.tensor_scalar(X[:, 11:12], X[:, 6:7], 32.0, None, ALU.mult)
            dve.drain()

        def level_params_dve(dve, l, e, k):
            X, M1 = lv[l], lve[l]
            its = at(e, k)
            p1, p2 = (wpow[:, m, at(e + (EXPERTS[0] if l else 0), k)] for m in range(2))
            dve.scalar_tensor_tensor(M1[:, 0, its], p1, X[:, 11:12], X[:, 3:4].broadcast_to([P, k]), ALU.mult, ALU.add)
            dve.drain()
            dve.tensor_scalar(M1[:, 1, its].bitcast(I32), M1[:, 0, its].bitcast(I32), EXPONENT, None, ALU.bitwise_and)
            dve.drain()
            dve.reciprocal(M1[:, 2, its], M1[:, 1, its])
            dve.drain()
            dve.scalar_tensor_tensor(M1[:, 3, its], p1, 2.0, M1[:, 2, its], ALU.mult, ALU.mult)
            dve.scalar_tensor_tensor(prm[l][:, its, 1], p2, 2.0 ** -27, M1[:, 1, its], ALU.mult, ALU.mult)
            dve.scalar_tensor_tensor(prm[l][:, its, 2:], b1T[l][:, its, :], 16384.0,
                                     M1[:, 2, its].unsqueeze(2).broadcast_to([P, k, FC]), ALU.mult, ALU.mult)
            dve.drain()
            dve.tensor_scalar(prm[l][:, its, 0], M1[:, 3, its], X[:, 10:11], None, ALU.mult).then_inc(params_made, 1)

        def level_scales_pool(pool, l):
            pool.wait_ge(level_stats, 2 * l + 2)
            for i in range(3):
                pool.partition_all_reduce(lv[l][:, 3 + i:4 + i], lv[l][:, i:i + 1], P, RED.max).then_inc(level_maxima, 1)


        def blk_of(l, g, b):
            return NB - GB - GB * g + b if l == 0 else GB * g - NB + b

        def route_t_pe(pe, q, b):
            pe.wait_ge(xr_made, q + 1)
            if some(q):
                pe.wait_ge(xr_copied, q)
            pe.wait_ge(xn_copied, NB)
            for k in range(KD):
                ins = pe.transpose(PX[:, k, :], xr[:, b, k * P:(k + 1) * P], ident[:, :])
            ins.then_inc(xr_transposed, 1)

        def route_copy_act(act, q, b):
            act.wait_ge(xr_transposed, q + 1)
            if some(q - 1):
                act.wait_ge(logits_made, q - 1)
            act.wait_ge(u_summed, NB)
            act.activation(xrT[:, 2 * (b % 2):2 * (b % 2) + 2, :], PX[:, 0:KD, :], ACT.Copy).then_inc(xr_copied, 1)

        def route_logits_pe(pe, l, g, q, b):
            pe.wait_ge(xr_copied, q + 1)
            if some(g):
                pe.wait_ge(logits_shifted, g)
            for k in range(KD):
                ins = pe.matmul(p_log[:, b, 0:EXPERTS[l]], xrT[:, 2 * (b % 2) + k, :], wr[l][:, k, :],
                                start=(k == 0), stop=(k == KD - 1))
            ins.then_inc(logits_made, 1)

        def route_pos_pe(pe, l, g):
            E = EXPERTS[l]
            pe.wait_ge(picks_made, g + 1)
            if some(g + l):
                pe.wait_ge(totals_made, g + l)
            if some(2 * g):
                pe.wait_ge(slots_made, 2 * g)
            for b in range(GB):
                pe.matmul(p_pos[:, b, 0:E], ones16[:, :], tot[:, 0:E], start=True, stop=False)
                for b2 in range(b):
                    pe.matmul(p_pos[:, b, 0:E], ones16[:, :], disp[:, b2, 0:E], start=False, stop=False)
                ins = pe.matmul(p_pos[:, b, 0:E], before[:, :], disp[:, b, 0:E], start=False, stop=True)
            ins.then_inc(places_counted, 1)

        def route_exp_act(act, l, g):
            act.wait_ge(logits_shifted, g + 1)
            act.activation(rt[:, 1, :, 0:EXPERTS[l]], rt[:, 0, :, 0:EXPERTS[l]], ACT.Exp).then_inc(exps_made, 1)

        def route_picks_dve(dve, l, g, blk):
            E = EXPERTS[l]
            r = [rt[:, i, :, 0:E] for i in range(12)]
            s = [rs[:, i, :] for i in range(8)]

            def wide(x):
                return x.unsqueeze(2).broadcast_to([P, GB, E])

            rank = rank_e[:, 0:E].unsqueeze(1).broadcast_to([P, GB, E])
            probs = coef[:, at(blk, GB), E:2 * E]
            tops = [p12[:, at(blk, GB), i] for i in range(2)]
            dve.wait_ge(logits_made, GB * g + GB)
            dve.tensor_reduce(s[0], p_log[:, :, 0:E], AX.X, ALU.max)
            dve.drain()
            dve.tensor_tensor(r[0], p_log[:, :, 0:E], wide(s[0]), ALU.subtract).then_inc(logits_shifted, 1)
            dve.wait_ge(exps_made, g + 1)
            dve.tensor_reduce(s[1], r[1], AX.X, ALU.add)
            dve.drain()
            dve.reciprocal(s[2], s[1])
            dve.drain()
            dve.tensor_tensor(probs, r[1], wide(s[2]), ALU.mult)
            dve.drain()
            left, masks = probs, []
            for i, (eq, best, pick) in enumerate(((3, 4, 5), (6, 7, 8))):
                dve.tensor_reduce(tops[i], left, AX.X, ALU.max)
                dve.drain()
                dve.tensor_tensor(r[eq], left, wide(tops[i]), ALU.is_equal)
                dve.drain()
                dve.tensor_tensor(r[best], r[eq], rank, ALU.mult)
                dve.drain()
                dve.tensor_reduce(s[5 + i], r[best], AX.X, ALU.max)
                dve.drain()
                dve.tensor_tensor(r[pick], r[best], wide(s[5 + i]), ALU.is_equal)
                dve.drain()
                masks.append(r[pick])
                if i == 0:
                    dve.scalar_tensor_tensor(r[9], r[pick], -2.0, probs, ALU.mult, ALU.add)
                    dve.drain()
                    left = r[9]
            if some(g):
                dve.wait_ge(places_counted, g)
            dve.tensor_tensor(disp[:, :, 0:E], masks[0], masks[1], ALU.add).then_inc(picks_made, 1)
            dve.drain()
            dve.scalar_tensor_tensor(coef[:, at(blk, GB), 0:E], disp[:, :, 0:E], 0.0, probs, ALU.is_equal, ALU.mult)

        def route_slots_dve(dve, l, g):
            E = EXPERTS[l]
            base = base_e[:, 0:E].unsqueeze(1).broadcast_to([P, GB, E])
            dve.wait_ge(places_counted, g + 1)
            dve.tensor_tensor(rt[:, 0, :, 0:E], p_pos[:, :, 0:E], base, ALU.add)
            dve.tensor_reduce(cpick[:, 0:E], disp[:, :, 0:E].rearrange("p b e -> p e b"), AX.X, ALU.add)
            dve.drain()
            dve.tensor_tensor(rt[:, 3, :, 0:E], rt[:, 0, :, 0:E], rt[:, 5, :, 0:E], ALU.mult)
            dve.tensor_tensor(rt[:, 4, :, 0:E], rt[:, 0, :, 0:E], rt[:, 8, :, 0:E], ALU.mult)
            dve.tensor_tensor(tot[:, 0:E], tot[:, 0:E], cpick[:, 0:E], ALU.add).then_inc(totals_made, 1)
            dve.drain()
            for b in range(GB):
                if l == 0 and some(2 * 16 * g):
                    dve.wait_ge(rows_sent[b], 2 * 16 * g)
            with nc.allow_low_precision(reason="row numbers, whole and below 2^24"):
                for i in range(2):
                    dve.tensor_reduce(slots_of(l, g)[:, :, i], rt[:, 3 + i, :, 0:E], AX.X, ALU.add).then_inc(slots_made, 1)

        def rows_of(l, q, b):
            return rows[:, b] if l == 0 or q < NB + GB else rows_1[:, (q - NB) // GB - 1, b]

        def slots_of(l, g):
            return slot[l][:, g - NG if l else 0]

        def pack_act(act, l, q, b):
            act.wait_ge(xr_made, q + 1)
            if l == 1:
                if q < NB + GB:
                    act.wait_ge(rows_sent[b], NB * 8)
            elif some((q - b) * 8):
                act.wait_ge(rows_sent[b], (q - b) * 8)
            act.wait_ge(level_scales, l + 1)
            act.activation(rows_of(l, q, b)[:, :, 0:D], xr[:, b, :].unsqueeze(1).broadcast_to([P, 2, D]), ACT.Copy,
                           scale=lv[l][:, 9:10]).then_inc(rows_hi, 1)

        def pack_dve(dve, l, q, b, blk):
            dve.wait_ge(rows_hi, q + 1)
            into = rows_of(l, q, b)
            dve.scalar_tensor_tensor(into[:, :, D:2 * D], xr[:, b, :].unsqueeze(1).broadcast_to([P, 2, D]),
                                     lv[l][:, 9:10], into[:, :, 0:D], ALU.mult, ALU.subtract).then_inc(rows_lo, 1)
            dve.tensor_copy(into[:, :, IDC:IDC + 2].bitcast(I32).rearrange("p r a -> p (r a)"),
                            ids[:, at(blk, 1), :].rearrange("p a r -> p (a r)")).then_inc(rows_id, 1)

        def scatter_pool(pool, l, g, q, b):
            pool.wait_ge(slots_made, 2 * g + 2)
            pool.wait_ge(rows_lo, q + 1)
            pool.wait_ge(rows_id, q + 1)
            for i in range(2):
                pool.nop(nofuse=True)
                pool.indirect_dma_start(arena[l], bass.IndirectOffsetOnAxis(ap=slots_of(l, g)[:, b, i:i + 1], axis=0),
                                        rows_of(l, q, b)[:, i, :], None).then_inc(rows_sent[b], 16)

        def table_dve(dve, l):
            E, NT = EXPERTS[l], TILES[l]
            c = [cnt[:, i, 0:E] for i in range(8)]
            tn = tileno[:, 0:NT]
            dve.wait_ge(counts_made, l + 1)
            dve.tensor_copy(c[0], p_cnt[0:1, 0:E])
            dve.memset(c[4], 1.0)
            dve.drain()
            dve.tensor_tensor(cnti[:, 1, 0:E], c[0], base_e[0:1, 0:E], ALU.add).then_inc(ends_made, 1)
            dve.tensor_copy(cnti[:, 0, 0:E], c[0])
            dve.drain()
            dve.tensor_scalar(cnti[:, 0, 0:E], cnti[:, 0, 0:E], TP.bit_length() - 1, None, ALU.logical_shift_right)
            dve.drain()
            dve.tensor_copy(c[1], cnti[:, 0, 0:E])
            dve.drain()
            dve.tensor_scalar(c[1], c[1], 1.0, None, ALU.add)
            dve.drain()
            dve.tensor_tensor_scan(c[2], c[4], c[1], 0.0, ALU.mult, ALU.add)
            dve.tensor_scalar(c[3], c[1], -float(TP), float(ARENA), ALU.mult, ALU.add)
            dve.drain()
            dve.memset(c[3][:, E - 1:E], float(1 << 17))
            over = [steps[:, i, 0:E, 0:NT] for i in range(2)]
            dve.tensor_tensor(over[1], tn.unsqueeze(1).broadcast_to([1, E, NT]), c[2].unsqueeze(2).broadcast_to([1, E, NT]), ALU.is_ge)
            dve.drain()
            dve.tensor_tensor(over[0], over[1], c[3].unsqueeze(2).broadcast_to([1, E, NT]), ALU.mult)
            dve.drain()
            dve.memset(over[1][:, E - 1:E], 0.0)
            dve.drain()
            for i in range(2):
                dve.tensor_reduce(tabf[:, i, 0:NT], steps[:, i, 0:E, 0:NT].rearrange("p e t -> p t e"), AX.X, ALU.add)
            dve.drain()
            dve.scalar_tensor_tensor(tabf[:, 0, 0:NT], tn, float(TP), tabf[:, 0, 0:NT], ALU.mult, ALU.add)
            dve.drain()
            dve.tensor_tensor(tab[:, 0, 0:NT], tabf[:, 0, 0:NT], junkrow[:, l, 0:NT], ALU.min)
            slots_up = float(WSLOT) if l else -float(WSLOT)
            dve.tensor_scalar(tab[:, 1, 0:NT], tabf[:, 1, 0:NT], slots_up, 0.0 if l else float((NSLOT - 1) * WSLOT), ALU.mult, ALU.add)
            dve.tensor_copy(tab[:, 2, 0:NT], tabf[:, 1, 0:NT])
            dve.drain()
            dve.memset(cnt[:, 5, 0:1], 0.0).then_inc(table_made, 1)

        def pads(eng, l, experts):
            eng.wait_ge(ends_made, l + 1)
            eng.wait_ge(pad_rows_stored, 2 * 16 * EM)
            for e in experts:
                row = eng.value_load(cnti[0:1, 1, e:e + 1], min_val=e * ARENA, max_val=e * ARENA + T)
                eng.dma_start(arena[l][at(row, TP), 0:IDC + 2], pad_rows[e * TP:(e + 1) * TP, 0:IDC + 2]).then_inc(pads_stored, 16)

        T0 = (0, TILES[0])

        def tile_load(sp, l, t, h):
            n = T0[l] + t
            first = isinstance(t, int) and t == 0
            if first:
                sp.wait_ge(table_made, l + 1)
            src = sp.value_load(tab[0:1, 0, at(t, 1)], min_val=0, max_val=JUNK[l] + TP)
            if first:
                for b in range(GB):
                    sp.wait_ge(rows_sent[b], 2 * 16 * NG * (l + 1))
                sp.wait_ge(pads_stored, 16 * sum(EXPERTS[:l + 1]))
                sp.wait_ge(junk_stored, 128)
            if some(n - 1):
                sp.wait_ge(tile_transposed, n - 1)
            if some(3 * (n - 1)):
                sp.nop(nofuse=True)
                sp.wait_ge(tile_params, 3 * (n - 1))
            sp.dma_start(xtile[:, h, :, :], arena[l][at(src, TP), :].rearrange("(p s) w -> p s w", s=S)).then_inc(tile_loaded[h], 16)


        def load_zero_results(eng, l, quarters):
            for b in quarters:
                eng.dma_start(CB[CW * b:CW * b + EXPERTS[l], :],
                              ys[l][PADROW:PADROW + EXPERTS[l] * TP, :].rearrange("(e p) d -> e p d", p=TP)[:, 0, :]).then_inc(cb_loaded, 16)

        def turn_gnn(g):
            return g, 0, g, NSLOT - 1 - g

        def turn_tiles(j):
            return EXPERTS[0] + j, 1, j, j

        def in_groups(eng, body, peeled):
            for g in range(peeled):
                body(g, True, g > 0)
            if peeled < NG:
                with eng.Fori(peeled, NG) as g:
                    body(g, True, True)
            body(NG, False, True)

        def corr_at(c):
            i = c % (2 * GB)
            if i < GB:
                return Zq[:, i, 0:D]
            if i < GB + 2:
                return Y[:, i - GB, :]
            return PM[:, 0:D] if i == GB + 2 else PX[:, 0:KD, :].rearrange("p k t -> p (k t)")

        def inside(r):
            return not isinstance(r, int) or 0 <= r < NB

        def in_blocks(eng, step):
            for r in range(-2, 4):
                step(r, r % 4)
            with eng.Fori(1, NB // 4 - 1) as i:
                for o in range(4):
                    step(i * 4 + o, o)
            for r in range(NB - 4, NB):
                step(r, r % 4)

        def in_tiles(eng, l, step):
            NT = TILES[l]
            first = EARLY if l else 0
            for t in range(2):
                step(t, t % 2, (first, t % 2) if l else None)
            turns = (first + 1, EM) if l else (0, EARLY)
            with eng.Fori(*turns) as j:
                for o in range(2):
                    step(j * 2 + (o + 2 - 2 * turns[0]), o, (j, o))
            with eng.Fori(1 + turns[1] - turns[0], NT // 2 - 1) as i:
                for o in range(2):
                    step(i * 2 + o, o, None)
            for t in range(NT - 2, NT):
                step(t, t % 2, None)

        block = ctx.enter_context(nc.Block())

        @block.sync
        def _(sp):
            sp.dma_start(wg_nat, gnn_W.rearrange("(k p) d -> p k d", p=P)).then_inc(gnnw_loaded, 16)
            sp.dma_start(brow[:, :], gnn_b.rearrange("(a d) -> a d", a=1)).then_inc(gnnw_loaded, 16)

            def front(r, o):
                if some(r - 1):
                    sp.wait_ge(xn_made, r - 1)
                sp.dma_start(xin[:, o % 2, :], x[at(r * P, P), :]).then_inc(x_loaded[o % 2], 16)
                if some(4 * (r - 3)):
                    sp.wait_ge(adj_transposed, 4 * (r - 3))
                sp.dma_start(adj_in[o], adj[at(r * P, P), :]).then_inc(adj_loaded[o], 16)

            for r in range(2):
                front(r, r)
            for l in range(2):
                sp.dma_start(wr[l][:, :, :], Wr[l].rearrange("(k p) e -> p k e", p=P)).then_inc(small_loaded, 16)
                sp.dma_start(b1n[l][:, :], b1[l].rearrange("e (c p) -> (e c) p", p=P)).then_inc(small_loaded, 16)
            for r in range(2, 4):
                front(r, r)
            sp.wait_ge(consts_made, NCONST)
            for l in range(2):
                for o in range(2):
                    junk = arena[l][JUNK[l] + o * TP:JUNK[l] + (o + 1) * TP, :].rearrange("(p s) w -> p s w", s=S)
                    sp.dma_start(junk[:, :, 0:2 * D], zeros[:, :].unsqueeze(1).broadcast_to([P, S, 2 * D])).then_inc(junk_stored, 16)
                    sp.dma_start(junk[:, :, IDC:IDC + 2], padids[:, EM + o, :].bitcast(F16).rearrange("p (s a) -> p s a", s=S)).then_inc(junk_stored, 16)
            with sp.Fori(1, NB // 4) as i:
                for o in range(4):
                    front(i * 4 + o, o)

            def store_pad_rows(e):
                place = pad_rows[e * TP:(e + 1) * TP, :].rearrange("(p s) w -> p s w", s=S)
                sp.dma_start(place[:, :, 0:2 * D], zeros[:, :].unsqueeze(1).broadcast_to([P, S, 2 * D])).then_inc(pad_rows_stored, 16)
                sp.dma_start(place[:, :, IDC:IDC + 2], padids[:, e, :].bitcast(F16).rearrange("p (s a) -> p s a", s=S)).then_inc(pad_rows_stored, 16)

            def group_gnn(g, new, old):
                if not new:
                    return
                if isinstance(g, int):
                    sp.wait_ge(adj_transposed, 4 * NB)
                for b in range(GB):
                    q = g * GB + b
                    sp.wait_ge(xn_made, NB)
                    if some(q - 1):
                        sp.wait_ge(bias_added, q - 1)
                    sp.nop(nofuse=True)
                    sp.dma_start(xin[:, b % 2, :], x[at((NB - GB - GB * g + b) * P, P), :]).then_inc(x_loaded[b % 2], 16)
                    if b:
                        store_x1(g * GB + b - 1, g, b - 1)
                    if b == 1:
                        w_load(sp, *turn_gnn(g))
                    if isinstance(g, int):
                        store_pad_rows(EM // 2 * g + b)
                store_x1(g * GB + GB - 1, g, GB - 1)

            def store_x1(q, g, b):
                sp.wait_ge(x1_made, q + 1)
                sp.dma_start(x1_dram[at((NB - GB - GB * g + b) * P, P), :], xn[:, b % 2, :]).then_inc(x1_stored[b % 2], 16)

            in_groups(sp, group_gnn, 2)

            def tiles(l):
                E = EXPERTS[l]
                pads(sp, l, range(0, E, 2))
                tile_load(sp, l, 0, 0)
                tile_load(sp, l, 1, 1)
                sp.wait_ge(cb_cleared, l + 1)
                for b in range(GB):
                    sp.dma_start(CB[CW * b + E:CW * b + 2 * E, :], b2[l]).then_inc(cb_loaded, 16)

                def step(t, h, turn):
                    if not (isinstance(t, int) and t in (0, TILES[l] - 1)):
                        tile_load(sp, l, t + 1, 1 - h)
                    if turn:
                        w_load(sp, *turn_tiles(turn[0]), ms=(turn[1],))

                in_tiles(sp, l, step)

            def load_results(l):
                for h in range(2):
                    sp.wait_ge(y_sent[h], 16 * (T0[l] + TILES[l]))
                load_zero_results(sp, l, range(0, GB, 2))
                for c in range(0, NB, 2):
                    sp.dma_start(yab[:, c:c + 2, :, :].rearrange("p j r d -> p j (r d)"),
                                 ys[l][2 * c * P:2 * (c + 2) * P, :].rearrange("(j p r) d -> p j (r d)", p=P, r=2)).then_inc(yab_loaded[c // GB], 16)

            tiles(0)
            load_results(0)
            sp.wait_ge(corr_made, NB)
            tiles(1)
            for h in range(2):
                sp.wait_ge(x1_stored[h], 8 * NB)
            sp.dma_start(x1_all, x1_dram.rearrange("(j p) d -> p j d", p=P)).then_inc(x1_back, 16)
            load_results(1)
            sp.wait_ge(out_stored, 16 * NB // 2)

        @block.gpsimd
        def _(pool):
            pool.iota(diff, [[1, P]], base=0, channel_multiplier=-1, allow_small_or_imprecise_dtypes=True).then_inc(consts_made, 1)
            pool.memset(onesrow[:, :], 1.0).then_inc(consts_made, 1)
            pool.memset(half[:, 0:1], -0.5).then_inc(consts_made, 1)
            pool.memset(half[:, 1:2], 0.5).then_inc(consts_made, 1)
            pool.memset(zeros[:, :], 0.0).then_inc(consts_made, 1)
            pool.memset(ones16[:, :], 1.0).then_inc(consts_made, 1)
            pool.iota(tileno[:, :], [[1, max(TILES)]], base=0, channel_multiplier=0, allow_small_or_imprecise_dtypes=True).then_inc(consts_made, 1)
            for l in range(2):
                pool.iota(junkrow[:, l, :].rearrange("a (i o) -> a i o", o=2), [[0, max(TILES) // 2], [TP, 2]], base=JUNK[l],
                          channel_multiplier=0, allow_small_or_imprecise_dtypes=True).then_inc(consts_made, 1)
            pool.iota(ids[:, :, :], [[2 * P, NB], [1, 2]], base=0, channel_multiplier=2).then_inc(consts_made, 1)
            pool.iota(padids[:, :, :], [[TP, EM + 2], [1, S]], base=PADROW, channel_multiplier=S).then_inc(consts_made, 1)
            pool.iota(base_e[:, :], [[ARENA, EM]], base=0, channel_multiplier=0, allow_small_or_imprecise_dtypes=True).then_inc(consts_made, 1)
            pool.iota(rank_e[:, :], [[-1, EM]], base=EM, channel_multiplier=0, allow_small_or_imprecise_dtypes=True).then_inc(consts_made, 1)
            pool.memset(coef[:, :, :], 0.0).then_inc(consts_made, 1)
            pool.memset(tot[:, :], 0.0).then_inc(consts_made, 1)
            pool.memset(yrun[:, :], 0.0).then_inc(consts_made, 1)

            def block_step(r, o):
                if inside(r + 2):
                    pool.wait_ge(var_made, r + 3)
                    pool.tensor_tensor(rstd[:, o % 2:o % 2 + 1], vare[:, o % 2:o % 2 + 1], half[:, 0:1], ALU.pow).then_inc(rstd_made, 1)
                if inside(r + 1):
                    h, rows_in = (o + 1) % 2, adj_in[(o + 1) % 4]
                    pool.wait_ge(deg_rounded, r + 2)
                    pool.nop(nofuse=True)
                    pool.tensor_scalar(rows_in, rows_in, rdeg[:, h:h + 1], 4096.0, ALU.mult, ALU.mult).then_inc(adj_scaled, 1)
                    pool.tensor_tensor(dis[:, at(r + 1, 1)], degE[:, at(r + 1, 1)], half[:, 0:1], ALU.pow).then_inc(dis_made, 1)

            in_blocks(pool, block_step)
            pool.wait_ge(v_bounds, 2)
            for i in range(2):
                pool.partition_all_reduce(gst[:, 2 + i:3 + i], gst[:, i:i + 1], P, RED.max).then_inc(v_bounds_max, 1)
            pool.wait_ge(v_bounds_max, 2)
            pool.tensor_tensor(gst[:, 4:5], gst[:, 2:3], half[:, 1:2], ALU.pow).then_inc(v_bound_root, 1)

            level_scales_pool(pool, 0)

            def group_gnn(g, new, old):
                for b in range(GB):
                    q = g * GB + b
                    if new:
                        pool.wait_ge(x_loaded[b % 2], ring(NB + q, b % 2))
                        pool.wait_ge(bias_copied, 1)
                        if some(q - 1):
                            pool.wait_ge(x1_made, q - 1)
                        pool.tensor_tensor(xb[:, b % 2, :], xin[:, b % 2, :], bB[:, :], ALU.add).then_inc(bias_added, 1)
                    if old and b == GB - 1:
                        for b2 in range(2):
                            scatter_pool(pool, 0, g - 1, q - b - GB + b2, b2)
                    if new:
                        pool.wait_ge(var_made, NB + q + 1)
                        pool.tensor_tensor(rstd[:, b % 2:b % 2 + 1], vare[:, b % 2:b % 2 + 1], half[:, 0:1], ALU.pow).then_inc(rstd_made, 1)
                    if new and b == GB - 1:
                        w_norm(pool, *turn_gnn(g))
                    if b == 0 and (not isinstance(g, int) or g >= 2):
                        for b2 in range(2, GB):
                            scatter_pool(pool, 0, g - 2, g * GB - 2 * GB + b2, b2)
                if not new:
                    for b2 in range(2, GB):
                        scatter_pool(pool, 0, g - 1, g * GB - GB + b2, b2)

            in_groups(pool, group_gnn, 2)

            def keep(l, t, h):
                n = T0[l] + t
                e = pool.value_load(tab[0:1, 2, at(t, 1)], min_val=0, max_val=EXPERTS[l] - 1)
                pool.wait_ge(tile_loaded[h], ring(n, h))
                if some(FC * (n - 1)):
                    pool.wait_ge(hid_made, FC * (n - 1))
                pool.tensor_copy(tprm[:, h, :], prm[l][:, at(e, 1), :].rearrange("p a c -> p (a c)")).then_inc(tile_params, 1)
                pool.tensor_copy(tgam[:, at(t, 1)], prm[l][:, at(e, 1), 1:2].rearrange("p a c -> p (a c)")).then_inc(tile_params, 1)
                pool.tensor_copy(tids[:, at(t, 1), :].rearrange("p a s -> p (a s)").unsqueeze(2), xtile[:, h, :, IDC:IDC + 2].bitcast(I32)).then_inc(tile_params, 1)

            def scatter_results(l, t, h):
                n = T0[l] + t
                if some((n - h) * 16):
                    pool.wait_ge(y_sent[h], (n - h) * 16)
                pool.wait_ge(tile_params, 3 * n + 3)
                pool.nop(nofuse=True)
                pool.tensor_copy(yid[:, h, :], tids[:, at(t, 1), :].rearrange("p a s -> p (a s)")).then_inc(y_ids, 1)
                pool.wait_ge(y_ids, n + 1)
                for i in range(S):
                    pool.wait_ge(y_scaled, S * n + i + 1)
                    pool.nop(nofuse=True)
                    pool.indirect_dma_start(ys[l], bass.IndirectOffsetOnAxis(ap=yid[:, h, i:i + 1], axis=0), yout[:, h, i, :], None).then_inc(y_sent[h], 16)

            def tiles(l):
                pool.wait_ge(table_made, l + 1)
                pool.wait_ge(params_made, l + 1)
                if l == 1:
                    for h in range(2):
                        pool.wait_ge(y_sent[h], 16 * TILES[0])
                keep(l, 0, 0)

                def step(t, h, turn):
                    if l == 1 and not isinstance(t, int):
                        pool.wait_ge(params_made, 2 + turn[0] - EARLY if turn else 2 + EM - EARLY) if h or not turn else None
                    if not (isinstance(t, int) and t == TILES[l] - 1):
                        keep(l, t + 1, 1 - h)
                    if turn:
                        w_norm(pool, *turn_tiles(turn[0]), ms=(turn[1],))
                    if not (isinstance(t, int) and t == 0):
                        scatter_results(l, t - 1, 1 - h)

                in_tiles(pool, l, step)
                scatter_results(l, TILES[l] - 1, (TILES[l] - 1) % 2)

            tiles(0)
            level_scales_pool(pool, 1)

            def group_mid(g, new, old):
                if old:
                    for b in range(GB):
                        scatter_pool(pool, 1, NG + g - 1, NB + g * GB - GB + b, b)

            in_groups(pool, group_mid, NG)
            tiles(1)

        @block.scalar
        def _(act):
            act.wait_ge(gnnw_loaded, 32)
            for k in range(KD):
                act.activation(rows[:, k, 0, 0:2 * D].bitcast(F32), wg_nat[:, k, :], ACT.Square,
                               accum_out=gst[:, 10 + k:11 + k]).then_inc(gnnw_squared, 1)
            act.wait_ge(bias_spread, 1)
            act.activation(bB[:, :], PM[:, 0:D], ACT.Copy).then_inc(bias_copied, 1)
            act.wait_ge(gnnw_transposed, 1)
            for k in range(KD):
                act.activation(wgT[:, k, :], Zq[:, k, 0:D], ACT.Copy).then_inc(gnnw_copied, 1)

            def block_step(r, o):
                h = (o + 1) % 2
                if inside(r + 1):
                    act.wait_ge(xn_transposed, r + 2)
                    if some(r):
                        act.wait_ge(u_summed, r)
                    act.activation(xrT[:, 2 * h:2 * h + 2, :], PX[:, 0:KD, :], ACT.Copy).then_inc(xn_copied, 1)
                for q in range(4):
                    if q == 2 and inside(r + 1):
                        act.wait_ge(u_summed, r + 2)
                        act.activation(u_all[:, at(r + 1, 1), :].rearrange("p a d -> p (a d)"), Y[:, h, :], ACT.Copy).then_inc(u_copied, 1)
                    if inside(r):
                        act.wait_ge(adj_transposed, r * 4 + q + 1)
                        act.activation(R[:, at(r * ATB + q * 4 * P, 4 * P)], Zq[:, q, :], ACT.Copy).then_inc(adj_hi, 1)
                if inside(r + 2):
                    rows_in = adj_in[(o + 2) % 4]
                    act.wait_ge(adj_loaded[(o + 2) % 4], ring(r + 2, (o + 2) % 4, 4))
                    act.activation(rows_in, rows_in, ACT.Copy, accum_out=deg[:, at(r + 2, 1)]).then_inc(deg_made, 1)

            in_blocks(act, block_step)
            for l in range(2):
                act.wait_ge(b1_transposed, 2)
                act.activation(b1T[l][:, :, :].rearrange("p e c -> p (e c)"), PM[:, 256 + 64 * l:256 + 64 * l + EXPERTS[l] * FC], ACT.Copy).then_inc(b1_copied, 1)
            act.wait_ge(v_scales, 1)
            for j in range(NB):
                act.activation(v[:, j, 0, :], u_all[:, j, :], ACT.Copy, scale=vscale[:, j:j + 1]).then_inc(v_hi, 1)

            def group(l):
                def body(g, new, old):
                    G = g + NG * l
                    for b in range(GB):
                        q = G * GB + b
                        if old and not new and b == 0:
                            route_copy_act(act, q - 1, GB - 1)
                            route_exp_act(act, l, G - 1)
                        if old:
                            pack_act(act, l, q - GB, b)
                        if old and new and b == 0:
                            route_copy_act(act, q - 1, GB - 1)
                        if old and new and b == 1:
                            route_exp_act(act, l, G - 1)
                        if new and b:
                            route_copy_act(act, q - 1, b - 1)
                        if l == 0 and new and old and b == 0:
                            w_high(act, *turn_gnn(g - 1))
                        if l == 0 and new and b == GB - 1:
                            w_square(act, *turn_gnn(g))
                return body

            in_groups(act, group(0), 2)
            pads(act, 0, range(1, EXPERTS[0], 2))
            w_high(act, *turn_gnn(NG - 1))

            def tile_copy(l, t, h):
                n = T0[l] + t
                act.wait_ge(tile_transposed, n + 1)
                if some(2 * (n - 1)):
                    act.wait_ge(z_made, 4 * (n - 1))
                act.activation(xT[:, h, :, :], PT[:, :, :, :].rearrange("p a s t -> p a (s t)"), ACT.Copy).then_inc(tile_copied, 1)

            def tiles(l):
                if l == 0:
                    act.wait_ge(logits_made, NB)
                    act.wait_ge(graph_summed, NB)
                else:
                    act.wait_ge(logits_made, 2 * NB)
                tile_copy(l, 0, 0)

                def step(t, h, turn):
                    n = T0[l] + t
                    if not (isinstance(t, int) and t == TILES[l] - 1):
                        tile_copy(l, t + 1, 1 - h)
                    act.wait_ge(tile_params, 3 * n + 3)
                    for q in range(4):
                        act.wait_ge(z_made, 4 * n + q + 1)
                        if some(4 * n + q - 3):
                            act.wait_ge(hid_lo_made, 4 * n + q - 3)
                        for c in range(2 * q, 2 * q + 2):
                            act.activation(hid[:, c, :], Z[:, c, :], ACT.Relu, bias=tprm[:, h, 2 + c:3 + c],
                                           scale=tprm[:, h, 0:1]).then_inc(hid_made, 1)
                        if some(n - 1):
                            act.wait_ge(y_made, n - 1)
                        act.wait_ge(hid_made, n * FC + 2 * q + 2)
                        act.activation(hid_hi[:, h, 2 * q:2 * q + 2, :], hid[:, 2 * q:2 * q + 2, :], ACT.Copy).then_inc(hid_hi_made, 1)
                        if turn and q == 0:
                            w_square(act, *turn_tiles(turn[0]), ms=(turn[1],))
                        if turn and q == 2:
                            w_high(act, *turn_tiles(turn[0]), ms=(turn[1],))

                in_tiles(act, l, step)

            def results_done(l):
                E = EXPERTS[l]
                act.wait_ge(coef_transposed, l + 1)
                act.wait_ge(w_lo, 2 * (sum(EXPERTS) if l else EXPERTS[0] + EARLY))
                act.activation(cT_all, p_cT, ACT.Copy).then_inc(coef_kept, 1)
                for h in range(2):
                    act.wait_ge(y_sent[h], 16 * (T0[l] + TILES[l]))
                load_zero_results(act, l, range(1, GB, 2))

            tiles(0)
            results_done(0)
            in_groups(act, group(1), NG)
            pads(act, 1, range(1, EXPERTS[1], 2))
            tiles(1)
            results_done(1)
            for c in range(0, NB, 2):
                act.wait_ge(out_made, c + 2)
                act.dma_start(out[c * P:(c + 2) * P, :].rearrange("(j p) d -> p j d", p=P), out_all[:, c:c + 2, :]).then_inc(out_stored, 16)

        @block.vector
        def _(dve):
            dve.wait_ge(consts_made, NCONST)
            dve.tensor_scalar(ident[:, :], diff, 0.0, None, ALU.is_equal)
            dve.tensor_scalar(ident16[:, :], diff, 0.0, None, ALU.is_equal)
            dve.tensor_scalar(before[:, :], diff, 0.0, None, ALU.is_gt).then_inc(masks_made, 1)
            dve.drain()
            dve.memset(cpick[:, 0:1], 0.0).then_inc(masks_made, 1)

            def block_step(r, o):
                h = o % 2
                if inside(r + 2):
                    dve.wait_ge(x_loaded[h], ring(r + 2, h))
                    dve.bn_stats(stat[:, h, :], xin[:, h, :])
                    dve.drain()
                    dve.bn_aggr(mv[:, h, :], stat[:, h, :])
                    dve.drain()
                    dve.tensor_scalar(vare[:, h:h + 1], mv[:, h, 1:2], EPS_LN, None, ALU.add).then_inc(var_made, 1)
                if inside(r + 1):
                    dve.wait_ge(deg_made, r + 2)
                    dve.tensor_scalar(degE[:, at(r + 1, 1)], deg[:, at(r + 1, 1)], EPS_DEG, None, ALU.add)
                    dve.drain()
                    dve.tensor_scalar(pdeg[:, at(r + 1, 1)].bitcast(I32), degE[:, at(r + 1, 1)].bitcast(I32), EXPONENT, None, ALU.bitwise_and)
                    dve.drain()
                    dve.reciprocal(rdeg[:, 1 - h:2 - h], pdeg[:, at(r + 1, 1)]).then_inc(deg_rounded, 1)
                for q in range(4):
                    if q == 1 and inside(r + 2):
                        dve.wait_ge(rstd_made, r + 3)
                        if some(r + 1):
                            dve.wait_ge(xn_transposed, r + 1)
                        dve.tensor_scalar(xn[:, h, :], xin[:, h, :], mv[:, h, 0:1], rstd[:, h:h + 1], ALU.subtract, ALU.mult).then_inc(xn_made, 1)
                    if inside(r):
                        dve.wait_ge(adj_hi, r * 4 + q + 1)
                        dve.tensor_tensor(R[:, at(r * ATB + (NB * P + q * 4 * P), 4 * P)], Zq[:, q, :],
                                          R[:, at(r * ATB + q * 4 * P, 4 * P)], ALU.subtract).then_inc(adj_lo, 1)

            in_blocks(dve, block_step)

            dve.wait_ge(gnnw_squared, 2)
            dve.wait_ge(dis_made, NB)
            dve.tensor_tensor(gst[:, 0:1], gst[:, 10:11], gst[:, 11:12], ALU.max).then_inc(v_bounds, 1)
            dve.tensor_reduce(gst[:, 1:2], dis[:, :], AX.X, ALU.max).then_inc(v_bounds, 1)
            dve.wait_ge(v_bound_root, 1)
            dve.tensor_scalar(gst[:, 5:6], gst[:, 4:5], 16.0, gst[:, 3:4], ALU.mult, ALU.mult)
            dve.drain()
            dve.tensor_scalar(gst[:, 5:6], gst[:, 5:6], 1e-15, None, ALU.max)
            dve.drain()
            dve.tensor_scalar(gst[:, 6:7].bitcast(I32), gst[:, 5:6].bitcast(I32), EXPONENT, None, ALU.bitwise_and)
            dve.drain()
            dve.reciprocal(gst[:, 7:8], gst[:, 6:7])
            dve.drain()
            dve.tensor_scalar(gscale[:, :], dis[:, :], gst[:, 6:7], 2.0 ** -26, ALU.mult, ALU.mult)
            dve.drain()
            dve.tensor_tensor(gscale[:, :], gscale[:, :], pdeg[:, :], ALU.mult)
            dve.tensor_scalar(vscale[:, :], dis[:, :], gst[:, 7:8], 16384.0, ALU.mult, ALU.mult).then_inc(v_scales, 1)
            dve.drain()
            for j in range(NB):
                dve.wait_ge(v_hi, j + 1)
                dve.scalar_tensor_tensor(v[:, j, 1, :], u_all[:, j, :], vscale[:, j:j + 1], v[:, j, 0, :],
                                         ALU.mult, ALU.subtract).then_inc(v_lo, 1)
            level_scales_dve(dve, 0)

            def group_gnn(g, new, old):
                for b in range(GB):
                    q, h = g * GB + b, b % 2
                    if old and not new and b == GB - 1:
                        w_scale(dve, *turn_gnn(g - 1))
                    if old and not new and b == 0:
                        route_picks_dve(dve, 0, g - 1, NB - GB * g)
                    if old:
                        pack_dve(dve, 0, q - GB, b, (NB - GB + GB + b) - GB * g)
                    if old and new and b == 0:
                        w_scale(dve, *turn_gnn(g - 1))
                    if new:
                        dve.wait_ge(graph_summed, q + 1)
                        dve.wait_ge(bias_added, q + 1)
                        if some((q - h) * 8):
                            dve.wait_ge(x1_stored[h], (q - h) * 8)
                        dve.wait_ge(xn_transposed, NB)
                        dve.nop(nofuse=True)
                        dve.scalar_tensor_tensor(xn[:, h, :], Y[:, h, :], gscale[:, at(NB - GB + b - GB * g, 1)], xb[:, h, :],
                                                 ALU.mult, ALU.add).then_inc(x1_made, 1)
                        dve.wait_ge(x1_made, q + 1)
                        dve.bn_stats(stat[:, h, :], xn[:, h, :])
                        dve.drain()
                        dve.bn_aggr(mv[:, h, :], stat[:, h, :])
                        dve.drain()
                        dve.tensor_scalar(vare[:, h:h + 1], mv[:, h, 1:2], EPS_LN, None, ALU.add).then_inc(var_made, 1)
                        dve.wait_ge(rstd_made, NB + q + 1)
                        if some(q - GB + 1):
                            dve.wait_ge(xr_transposed, q - GB + 1)
                        if some(q - GB + 1):
                            dve.wait_ge(rows_lo, q - GB + 1)
                        dve.wait_ge(u_summed, NB)
                        dve.tensor_scalar(xr[:, b, :], xn[:, h, :], mv[:, h, 0:1], rstd[:, h:h + 1], ALU.subtract, ALU.mult).then_inc(xr_made, 1)
                    if old and new and b == 1:
                        route_picks_dve(dve, 0, g - 1, NB - GB * g)
                    if old and b == (2 if new else 0):
                        route_slots_dve(dve, 0, g - 1)
                    if old and new and b == 0:
                        w_low(dve, *turn_gnn(g - 1))

            in_groups(dve, group_gnn, 2)
            table_dve(dve, 0)
            level_params_dve(dve, 0, 0, EXPERTS[0])
            w_low(dve, *turn_gnn(NG - 1))

            def result(l, t, h):
                n = T0[l] + t
                dve.wait_ge(y_made, n + 1)
                dve.wait_ge(tile_params, 3 * n + 3)
                if some((n - h) * 16):
                    dve.wait_ge(y_sent[h], (n - h) * 16)
                for i in range(S):
                    dve.tensor_scalar(yout[:, h, i, :], Y[:, i, :], tgam[:, at(t, 1)], None, ALU.mult).then_inc(y_scaled, 1)
                if l == 0:
                    dve.wait_ge(y_scaled, S * n + S)
                    dve.tensor_reduce(ymax[:, h:h + 1], yout[:, h, :, :].rearrange("p s d -> p (s d)"), AX.X, ALU.max, apply_absolute_value=True)
                    dve.drain()
                    dve.tensor_tensor(yrun[:, 0:1], yrun[:, 0:1], ymax[:, h:h + 1], ALU.max)
                    dve.drain()

            def tiles(l):
                def step(t, h, turn):
                    n = T0[l] + t
                    if some(n - 1):
                        dve.wait_ge(y_made, n - 1)
                    for q in range(4):
                        dve.wait_ge(hid_hi_made, 4 * n + q + 1)
                        dve.tensor_tensor(hid_lo[:, h, 2 * q:2 * q + 2, :], hid[:, 2 * q:2 * q + 2, :],
                                          hid_hi[:, h, 2 * q:2 * q + 2, :], ALU.subtract).then_inc(hid_lo_made, 1)
                        if turn and q == 1:
                            w_scale(dve, *turn_tiles(turn[0]), ms=(turn[1],))
                    if not (isinstance(t, int) and t == 0):
                        result(l, t - 1, 1 - h)
                    if turn:
                        if l == 1 and turn[1] == 1:
                            level_params_dve(dve, 1, turn[0], 1)
                        w_low(dve, *turn_tiles(turn[0]), ms=(turn[1],))

                for b in range(GB):
                    dve.wait_ge(rows_sent[b], 2 * 16 * NG * (l + 1))
                if l == 0:
                    for h in range(2):
                        dve.wait_ge(x1_stored[h], 8 * NB)
                in_tiles(dve, l, step)
                result(l, TILES[l] - 1, (TILES[l] - 1) % 2)

            dve.memset(CB[:, :], 0.0)
            dve.drain()
            dve.memset(cpick[:, 0:1], 0.0).then_inc(cb_cleared, 1)
            tiles(0)
            dve.wait_ge(cb_loaded, 2 * GB * 16)
            dve.memset(tot[:, :], 0.0).then_inc(totals_made, 1)
            dve.wait_ge(totals_made, NG + 1)
            level_scales_dve(dve, 1)

            def group_mid(g, new, old):
                if new:
                    dve.wait_ge(yab_loaded[g], 32)
                for b in range(GB):
                    q = NB + g * GB + b
                    if old and not new and b == 0:
                        route_picks_dve(dve, 1, NG + g - 1, GB * g - GB)
                    if old:
                        pack_dve(dve, 1, q - GB, b, GB * g - GB + b)
                    if new:
                        dve.wait_ge(xr_transposed, q - GB + 1)
                        dve.wait_ge(rows_lo, q - GB + 1)
                        c = g * GB + b
                        dve.wait_ge(corr_made, c + 1)
                        dve.scalar_tensor_tensor(xb[:, b % 2, :], yab[:, at(c, 1), 1, :], p12[:, at(c, 1), 1], Y[:, b % 2, :], ALU.mult, ALU.add)
                        dve.drain()
                        dve.scalar_tensor_tensor(xr[:, b, :], yab[:, at(c, 1), 0, :], p12[:, at(c, 1), 0], xb[:, b % 2, :],
                                                 ALU.mult, ALU.add).then_inc(xr_made, 1)
                    if old and new and b == 1:
                        route_picks_dve(dve, 1, NG + g - 1, GB * g - GB)
                    if old and b == (2 if new else 0):
                        route_slots_dve(dve, 1, NG + g - 1)

            in_groups(dve, group_mid, NG)
            table_dve(dve, 1)
            level_params_dve(dve, 1, 0, EARLY)
            dve.wait_ge(corr_made, NB)
            dve.memset(CB[:, :], 0.0)
            dve.drain()
            dve.memset(cpick[:, 0:1], 0.0).then_inc(cb_cleared, 1)
            tiles(1)

            dve.wait_ge(x1_back, 16)
            for g in range(NG):
                blocks = range(g * GB, (g + 1) * GB)
                dve.wait_ge(yab_loaded[g], 64)
                for c in blocks:
                    dve.wait_ge(corr_made, NB + c + 1)
                    dve.scalar_tensor_tensor(out_all[:, c, :], yab[:, c, 1, :], p12[:, c, 1:2], corr_at(c), ALU.mult, ALU.add)
                dve.drain()
                dve.tensor_tensor(out_all[:, blocks[0]:blocks[0] + GB, :], out_all[:, blocks[0]:blocks[0] + GB, :],
                                  x1_all[:, blocks[0]:blocks[0] + GB, :], ALU.add)
                dve.drain()
                for c in blocks:
                    dve.scalar_tensor_tensor(out_all[:, c, :], yab[:, c, 0, :], p12[:, c, 0:1], out_all[:, c, :], ALU.mult, ALU.add).then_inc(out_made, 1)

        @block.tensor
        def _(pe):
            pe.wait_ge(gnnw_loaded, 32)
            pe.wait_ge(consts_made, NCONST)
            pe.matmul(PM[:, 0:D], onesrow[:, :], brow[:, :], start=True, stop=True).then_inc(bias_spread, 1)
            pe.wait_ge(masks_made, 2)
            for k in range(KD):
                for m in range(KD):
                    ins = pe.transpose(Zq[:, k, m * P:(m + 1) * P], wg_nat[:, m, k * P:(k + 1) * P], ident[:, :])
            ins.then_inc(gnnw_transposed, 1)
            pe.wait_ge(bias_copied, 1)
            pe.wait_ge(gnnw_copied, 2)

            def block_step(r, o):
                h = (o + 1) % 2
                if inside(r + 1):
                    pe.wait_ge(xn_made, r + 2)
                    if some(r + 1):
                        pe.wait_ge(xn_copied, r + 1)
                    for k in range(KD):
                        ins = pe.transpose(PX[:, k, :], xn[:, h, k * P:(k + 1) * P], ident[:, :])
                    ins.then_inc(xn_transposed, 1)
                if inside(r):
                    pe.wait_ge(adj_scaled, r + 1)
                for q in range(4):
                    if q == 2 and inside(r + 1):
                        pe.wait_ge(xn_copied, r + 2)
                        if some(r):
                            pe.wait_ge(u_copied, r)
                        for k in range(KD):
                            ins = pe.matmul(Y[:, h, :], xrT[:, 2 * h + k, :], wgT[:, k, :], start=(k == 0), stop=(k == KD - 1))
                        ins.then_inc(u_summed, 1)
                    if inside(r):
                        if some(r * 4 + q - 3):
                            pe.wait_ge(adj_lo, r * 4 + q - 3)
                        for j in range(4 * q, 4 * q + 4):
                            ins = pe.transpose(Zq[:, q, (j % 4) * P:(j % 4 + 1) * P], adj_in[o][:, j * P:(j + 1) * P], ident[:, :])
                        ins.then_inc(adj_transposed, 1)

            in_blocks(pe, block_step)
            pe.wait_ge(small_loaded, 64)
            for l in range(2):
                n = EXPERTS[l] * FC
                pe.transpose(PM[:, 256 + 64 * l:256 + 64 * l + n], b1n[l][:, :], ident[0:n, 0:n]).then_inc(b1_transposed, 1)

            def product(g, b):
                q = g * GB + b
                first = isinstance(q, int) and q == 0
                if some(q - 1):
                    pe.wait_ge(x1_made, q - 1)
                if first:
                    pe.wait_ge(u_copied, NB)
                    pe.wait_ge(adj_lo, 4 * NB)
                a = (NB - GB + b - GB * g) * ATB
                pe.nop(nofuse=True)
                for j in range(NB):
                    if first:
                        pe.wait_ge(v_lo, j + 1)
                    hi, lo = (R[:, at(a + (m * NB + j) * P, P)] for m in range(2))
                    pe.matmul(Y[:, b % 2, :], hi, v[:, j, 0, :], start=(j == 0), stop=False)
                    pe.matmul(Y[:, b % 2, :], hi, v[:, j, 1, :], start=False, stop=False)
                    ins = pe.matmul(Y[:, b % 2, :], lo, v[:, j, 0, :], start=False, stop=(j == NB - 1))
                ins.then_inc(graph_summed, 1)

            def group(l):
                def body(g, new, old):
                    G = g + NG * l
                    if new and l == 1:
                        if isinstance(g, int) and g == 0:
                            pe.wait_ge(cb_loaded, 2 * GB * 16)
                        pe.wait_ge(coef_kept, 1)
                    for b in range(GB):
                        q = G * GB + b
                        if new and l == 0:
                            product(g, b)
                        if new and l == 1:
                            pe.wait_ge(xr_made, q - 1)
                            pe.matmul(Y[:, b % 2, :], cT_all[CW * b:CW * (b + 1), g * P:(g + 1) * P], CB[CW * b:CW * (b + 1), :], start=True, stop=True).then_inc(corr_made, 1)
                        if b == 0 and old:
                            route_t_pe(pe, q - 1, GB - 1)
                            route_logits_pe(pe, l, G - 1, q - 2, GB - 2)
                            if not new:
                                route_logits_pe(pe, l, G - 1, q - 1, GB - 1)
                        if b == 1:
                            if new:
                                route_t_pe(pe, q - 1, 0)
                            if new and old:
                                route_logits_pe(pe, l, G - 1, q - 2, GB - 1)
                        if b >= 2 and new:
                            route_t_pe(pe, q - 1, b - 1)
                            route_logits_pe(pe, l, G, q - 2, b - 2)
                        if b == 2 and old:
                            route_pos_pe(pe, l, G - 1)
                return body

            def count(l):
                pe.wait_ge(totals_made, (NG + 1) * l + NG)
                pe.matmul(p_cnt[:, 0:EXPERTS[l]], ones16[:, :], tot[:, 0:EXPERTS[l]], start=True, stop=True).then_inc(counts_made, 1)

            in_groups(pe, group(0), 2)
            count(0)

            def tile_transpose(l, t, h):
                n = T0[l] + t
                pe.wait_ge(tile_loaded[h], ring(n, h))
                if some(n):
                    pe.wait_ge(tile_copied, n)
                for a in range(2 * KD):
                    for i in range(S):
                        ins = pe.transpose(PT[:, a, i, :], xtile[:, h, i, a * P:(a + 1) * P], ident16[:, :])
                ins.then_inc(tile_transposed, 1)

            def weights(t):
                w = pe.value_load(tab[0:1, 1, at(t, 1)], min_val=0, max_val=(NSLOT - 1) * WSLOT)
                return lambda start, n: R[:, at(w + start, n)]

            def layer1(n, h, q, w):
                if some(FC * n + 2 * q + 2 - FC):
                    pe.wait_ge(hid_made, FC * n + 2 * q + 2 - FC)
                for c in range(2 * q, 2 * q + 2):
                    for k in range(KD):
                        hi, lo = (w(m * UNIT + k * F + c * P, P) for m in range(2))
                        pe.matmul(Z[:, c, :], hi, xT[:, h, k, :], start=(k == 0), stop=False)
                        pe.matmul(Z[:, c, :], hi, xT[:, h, KD + k, :], start=False, stop=False)
                        ins = pe.matmul(Z[:, c, :], lo, xT[:, h, k, :], start=False, stop=(k == KD - 1))
                ins.then_inc(z_made, 1)

            def layer2(n, h, q, w):
                pe.wait_ge(hid_lo_made, 4 * n + q + 1)
                if q == 0 and some(S * n):
                    pe.wait_ge(y_scaled, S * n)
                for c in range(2 * q, 2 * q + 2):
                    hi, lo = (w(2 * UNIT + (2 * c + m) * D, D) for m in range(2))
                    for i in range(S):
                        block = slice(i * P, (i + 1) * P)
                        pe.matmul(Y[:, i, :], hid_hi[:, h, c, block], hi, start=(c == 0), stop=False)
                        pe.matmul(Y[:, i, :], hid_hi[:, h, c, block], lo, start=False, stop=False)
                        ins = pe.matmul(Y[:, i, :], hid_lo[:, h, c, block], hi, start=False, stop=(c == FC - 1))
                if q == 3:
                    ins.then_inc(y_made, 1)

            def tiles(l):
                pe.wait_ge(table_made, l + 1)
                pe.wait_ge(w_lo, 2 * (EXPERTS[0] + EARLY if l else EXPERTS[0] - 1))
                if l == 0:
                    pe.wait_ge(x1_made, NB)
                else:
                    pe.wait_ge(xr_made, 2 * NB)
                tile_transpose(l, 0, 0)

                def step(t, h, turn):
                    n = T0[l] + t
                    if l == 0 and isinstance(t, int) and t == 1:
                        pe.wait_ge(w_lo, 2 * EXPERTS[0])
                    if l == 1 and h and not isinstance(t, int):
                        pe.wait_ge(w_lo, 2 * (EXPERTS[0] + (turn[0] if turn else EM)))
                    w = weights(t)
                    before_it = not (isinstance(t, int) and t == 0)
                    if before_it:
                        w_before = weights(t - 1)
                    pe.wait_ge(tile_copied, n + 1)
                    for q in range(4):
                        layer1(n, h, q, w)
                        if q == 0 and not (isinstance(t, int) and t == TILES[l] - 1):
                            tile_transpose(l, t + 1, 1 - h)
                        if before_it:
                            layer2(n - 1, 1 - h, q, w_before)

                in_tiles(pe, l, step)
                w = weights(TILES[l] - 1)
                for q in range(4):
                    layer2(T0[l] + TILES[l] - 1, (TILES[l] - 1) % 2, q, w)

            def transpose_coefficients(l):
                pe.wait_ge(hid_made, FC * (T0[l] + TILES[l]))
                for g in range(NG):
                    ins = pe.transpose(p_cT[:, g * P:(g + 1) * P], coef[:, g * GB:(g + 1) * GB, :].rearrange("p b c -> p (b c)"), ident[:, :])
                ins.then_inc(coef_transposed, 1)

            tiles(0)
            transpose_coefficients(0)
            in_groups(pe, group(1), NG)
            count(1)
            tiles(1)
            transpose_coefficients(1)

            pe.wait_ge(cb_loaded, 4 * GB * 16)
            pe.wait_ge(coef_kept, 2)
            for c in range(NB):
                g, b = c // GB, c % GB
                if g >= 2:
                    pe.wait_ge(out_made, (g - 1) * GB)
                pe.matmul(corr_at(c), cT_all[CW * b:CW * (b + 1), g * P:(g + 1) * P], CB[CW * b:CW * (b + 1), :],
                          start=True, stop=True).then_inc(corr_made, 1)


_INS = ['x', 'adj', 'L0_gnn_W', 'L0_gnn_b', 'L0_ffn_Wr0', 'L0_ffn_W1_0', 'L0_ffn_b1_0', 'L0_ffn_W2_0', 'L0_ffn_b2_0',
        'L0_ffn_Wr1', 'L0_ffn_W1_1', 'L0_ffn_b1_1', 'L0_ffn_W2_1', 'L0_ffn_b2_1']
_OUTS = [((2048, 256), 'float32')]


def kernel(**inputs):
    import numpy as _np
    import concourse.bacc as _bacc
    from concourse import mybir as _mybir
    from concourse.bass_utils import run_bass_kernel_spmd as _run

    nc = _bacc.Bacc("TRN2", target_bir_lowering=False, num_devices=1, dynamic_dma_scratch_size=8192)
    arrays, args = {}, []
    for name in _INS:
        a = _np.ascontiguousarray(inputs[name])
        arrays[f"in_{name}_dram"] = a
        args.append(nc.dram_tensor(f"in_{name}_dram", a.shape, _mybir.dt.from_np(a.dtype), kind="ExternalInput").ap())
    for i, (shape, dtype) in enumerate(_OUTS):
        dt = _mybir.dt.from_np(_np.dtype(dtype))
        args.append(nc.dram_tensor(f"out_{i}_dram", shape, dt, kind="ExternalOutput").ap())
    bass_gnn_moe(nc, *args)
    r = _run(nc, [arrays], core_ids=[0])
    return r.results[0]["out_0_dram"]
```
